# Optimizing a Trainium2 kernel written in Bass

```python
import numpy as np
import jax
import jax.numpy as jnp

def _softmax(x, axis=-1):
    return jax.nn.softmax(x, axis=axis)

def _gelu(x):
    return jax.nn.gelu(x, approximate=True)

def _silu(x):
    return jax.nn.silu(x)

def _sigmoid(x):
    return jax.nn.sigmoid(x)

def _layernorm(x, axis=-1, eps=1e-05):
    m = jnp.mean(x, axis=axis, keepdims=True)
    v = jnp.var(x, axis=axis, keepdims=True)
    return (x - m) / jnp.sqrt(v + eps)

def _scatter_add(tgt, idx, src, axis=0):
    return tgt.at[idx].add(src)

def _segment_sum(src, seg, n):
    return jax.ops.segment_sum(src, seg, n)
kernel_name = 'mk_seq_preln_d1_jaxref_r4_5c32e5'

def setup_inputs(seed: int=0):
    np.random.seed(seed)
    _w = jnp.asarray

    def _L0_attn_setup():
        import jax, jax.numpy as jnp
        import numpy as np
        B, T, D, C = (4, 2048, 256, 64)
        key = jax.random.key(seed)
        k1, k2, k3 = jax.random.split(key, 3)
        out = jax.random.normal(k1, (B, T, D), jnp.float32)
        W_write = jax.random.normal(k2, (D, D), jnp.float32) / np.float32(np.sqrt(D))
        W_read = jax.random.normal(k3, (D, D), jnp.float32) / np.float32(np.sqrt(D))
        decay = jnp.float32(4.6)
        log_alpha = jnp.log(jnp.float32(0.03))
        return {'out': out, 'W_write': W_write, 'W_read': W_read, 'decay': decay, 'log_alpha': log_alpha}
    _L0_attn_in = _L0_attn_setup()

    def _L0_ffn_setup():
        import jax, jax.numpy as jnp
        import numpy as np
        HID = 256
        INTER = 1024
        RDIM = 128
        HEADS = 4
        NUM_EXPERTS = 4096
        NUM_KEYS = 128
        TOPK = 8
        B, T = (2, 512)
        key = jax.random.key(seed)
        ks = jax.random.split(key, 8)
        s = lambda fan_in: 1.0 / np.sqrt(fan_in)
        return {'hidden_states': jax.random.normal(ks[0], (B, T, HID), jnp.float32), 'Wq': jax.random.normal(ks[1], (HEADS * RDIM, HID), jnp.float32) * s(HID), 'keys': jax.random.normal(ks[2], (HEADS, NUM_KEYS, 2, RDIM // 2), jnp.float32) * s(RDIM // 2), 'down_embed': jax.random.normal(ks[3], (NUM_EXPERTS, HID), jnp.float32) * 0.02, 'up_embed': jax.random.normal(ks[4], (NUM_EXPERTS, HID), jnp.float32) * 0.02, 'Wg': jax.random.normal(ks[5], (INTER, HID), jnp.float32) * s(HID), 'Wu': jax.random.normal(ks[6], (INTER, HID), jnp.float32) * s(HID), 'Wd': jax.random.normal(ks[7], (HID, INTER), jnp.float32) * s(INTER)}
    _L0_ffn_in = _L0_ffn_setup()
    _d = {'L0_attn_out': _L0_attn_in['out'], 'L0_attn_W_write': _L0_attn_in['W_write'], 'L0_attn_W_read': _L0_attn_in['W_read'], 'L0_attn_decay': _L0_attn_in['decay'], 'L0_attn_log_alpha': _L0_attn_in['log_alpha'], 'L0_ffn_Wq': _L0_ffn_in['Wq'], 'L0_ffn_keys': _L0_ffn_in['keys'], 'L0_ffn_down_embed': _L0_ffn_in['down_embed'], 'L0_ffn_up_embed': _L0_ffn_in['up_embed'], 'L0_ffn_Wg': _L0_ffn_in['Wg'], 'L0_ffn_Wu': _L0_ffn_in['Wu'], 'L0_ffn_Wd': _L0_ffn_in['Wd']}
    _x0 = _d['L0_attn_out']
    _d['L0_attn_out'] = jax.random.normal(jax.random.fold_in(jax.random.key(seed), 1), (8, 512, 256), dtype=_x0.dtype)
    del _x0
    return _d

def reference(L0_attn_out, L0_attn_W_write, L0_attn_W_read, L0_attn_decay, L0_attn_log_alpha, L0_ffn_Wq, L0_ffn_keys, L0_ffn_down_embed, L0_ffn_up_embed, L0_ffn_Wg, L0_ffn_Wu, L0_ffn_Wd):

    def _L0_attn_ref(out, W_write, W_read, decay, log_alpha):
        import jax, jax.numpy as jnp
        import numpy as np
        B, T, D, C = (4, 2048, 256, 64)
        Bd, Td, Dd = out.shape
        nC = Td // C
        out32 = out.astype(jnp.float32)
        gamma = jax.nn.sigmoid(decay)
        log_gamma = jnp.log(gamma)
        v = out32 @ W_write.T
        wk = jnp.pad(out32[:, :-1], ((0, 0), (1, 0), (0, 0)))
        rk = out32
        p = jnp.arange(C)
        diffs = jnp.maximum(p[:, None] - 1 - p[None, :], 0)
        causal = (p[:, None] > p[None, :]).astype(jnp.float32)
        M = jnp.exp(diffs * log_gamma) * causal
        dec_inter = gamma ** p
        gw = gamma ** (C - 1 - p)
        gC = gamma ** C

        def chunk(x):
            return x.reshape(Bd, nC, C, Dd).transpose(1, 0, 2, 3)
        rk_c, wk_c, v_c = (chunk(rk), chunk(wk), chunk(v))

        def body(W, xs):
            r, w, vv = xs
            inter = jnp.einsum('bde,bce->bcd', W, r) * dec_inter[None, :, None]
            S = jnp.einsum('bcd,bed->bce', r, w)
            intra = jnp.einsum('bce,bed->bcd', S * M, vv)
            W_new = gC * W + jnp.einsum('bcd,bce->bde', vv * gw[None, :, None], w)
            return (W_new, inter + intra)
        W0 = jnp.zeros((Bd, Dd, Dd), jnp.float32)
        _, reads = jax.lax.scan(body, W0, (rk_c, wk_c, v_c))
        reads = reads.transpose(1, 0, 2, 3).reshape(Bd, Td, Dd)
        alpha = jnp.exp(log_alpha)
        return out + alpha * (reads @ W_read.T).astype(out.dtype)

    def _L0_ffn_ref(hidden_states, Wq, keys, down_embed, up_embed, Wg, Wu, Wd):
        import jax, jax.numpy as jnp
        import numpy as np
        HID = 256
        INTER = 1024
        RDIM = 128
        HEADS = 4
        NUM_EXPERTS = 4096
        NUM_KEYS = 128
        TOPK = 8
        B, T = (2, 512)
        b, t, _ = hidden_states.shape
        q = hidden_states @ Wq.T
        q = q.reshape(b, t, 2, HEADS, RDIM // 2)
        q = jnp.transpose(q, (2, 0, 1, 3, 4))
        sim = jnp.einsum('pbthn,hkpn->pbthk', q, keys)
        sx, ix = jax.lax.top_k(sim[0], TOPK)
        sy, iy = jax.lax.top_k(sim[1], TOPK)
        all_scores = (sx[..., :, None] + sy[..., None, :]).reshape(b, t, HEADS, TOPK * TOPK)
        all_indices = (ix[..., :, None] * NUM_KEYS + iy[..., None, :]).reshape(b, t, HEADS, TOPK * TOPK)
        scores, pk = jax.lax.top_k(all_scores, TOPK)
        indices = jnp.take_along_axis(all_indices, pk, axis=-1)
        down = down_embed[indices]
        up = up_embed[indices]
        w = jnp.einsum('btd,bthkd->bthk', hidden_states, down)
        w = jax.nn.silu(w) * jax.nn.softmax(scores, axis=-1)
        experts_states = jnp.einsum('bthk,bthkd->btd', w, up)
        mlp = jax.nn.silu(hidden_states @ Wg.T) * (hidden_states @ Wu.T) @ Wd.T
        return mlp + experts_states
    x = L0_attn_out
    x = x + _L0_attn_ref(_layernorm(x, axis=-1), L0_attn_W_write, L0_attn_W_read, L0_attn_decay, L0_attn_log_alpha)
    x = x + _L0_ffn_ref(_layernorm(x, axis=-1), L0_ffn_Wq, L0_ffn_keys, L0_ffn_down_embed, L0_ffn_up_embed, L0_ffn_Wg, L0_ffn_Wu, L0_ffn_Wd)
    return x

_drawn_inputs = setup_inputs


def setup_inputs(seed=0):
    import zlib

    import numpy as np

    out = dict(_drawn_inputs(seed))
    spreads = {}
    factors = {'L0_ffn_Wq': 8.0, 'L0_ffn_keys': 8.0, 'L0_ffn_down_embed': 8.0, 'L0_ffn_up_embed': 8.0}
    for name, (base, spread) in spreads.items():
        noise = np.random.default_rng([zlib.crc32(name.encode()), seed]).standard_normal(out[name].shape)
        drawn = base * np.exp(spread * noise) if base else spread * noise
        out[name] = jnp.asarray(drawn.astype(out[name].dtype))
    for name, factor in factors.items():
        out[name] = (out[name] * factor).astype(out[name].dtype)
    return out
```

```python
from contextlib import ExitStack

import concourse.bass as bass
from concourse import mybir

ALU = mybir.AluOpType
ACT = mybir.ActivationFunctionType
F32, F16, I32, U32 = mybir.dt.float32, mybir.dt.float16, mybir.dt.int32, mybir.dt.uint32
AX_X = mybir.AxisListType.X

P = 128
NB, T, D = 8, 512, 256
NQ = T // P
KC = D // P
INTER, NIC = 1024, 1024 // P
HEADS, NK, TOPK, HALF = 4, 128, 8, 64
PAIRS = HEADS * TOPK
NE = 4096
NI = NE // P
TH = T // 2
TQ = TH // NQ
EPS = 1e-5

X_SCALE = 2.0 ** 10
W_SCALE = 2.0 ** 14
P_SCALE = 2.0 ** 12
RSQRT_SEED = 0x5F3759DF
EXPONENT = 0x7F800000
PIECE = 2048
NPIECE = 2 * KC * NE // PIECE
HALVES = ((0, 0), (0, 1), (1, 0))


def dense_kernel(nc, x, wwrite, wreadT, decay, log_alpha, wq, keys, emb, wg, wu, wd,
                 ident_d, diffs_d, causal_d, iota_d, rank_d, qmask_d, x2_d, tab_d, x1_d, out):
    ctx = ExitStack()
    with ctx:
        ARENA = 36400
        arena = ctx.enter_context(nc.sbuf_tensor("arena", [P, ARENA], F32))
        embs = ctx.enter_context(nc.sbuf_tensor("embs", [P, 2 * KC * NE], F32))
        ident = ctx.enter_context(nc.sbuf_tensor("ident", [P, P], F32))
        iota = ctx.enter_context(nc.sbuf_tensor("iota", [P, P], F16))
        rank = ctx.enter_context(nc.sbuf_tensor("rank", [P, TOPK], F32))
        qmask = ctx.enter_context(nc.sbuf_tensor("qmask", [P, NQ], F32))
        scal = ctx.enter_context(nc.sbuf_tensor("scal", [P, 64], F32))
        bank = [ctx.enter_context(nc.psum_tensor(f"bank{i}", [P, 512], F32)) for i in range(8)]

        sems = {}

        def sem(name):
            if name not in sems:
                sems[name] = ctx.enter_context(nc.semaphore(name))
            return sems[name]

        class Region:

            def __init__(self, whole, start=0):
                self.whole, self.at = whole, start

            def take(self, n, dt=F32):
                words = n if dt in (F32, I32, U32) else n // 2
                v = self.whole[:, self.at:self.at + words]
                self.at += words
                assert self.at <= self.whole.shape[1], self.at
                return v if dt == F32 else v.bitcast(dt)

        e = Region(embs)
        down_s = e.take(2 * KC * NE, F16).rearrange("p (s k e) -> p s k e", s=2, k=KC)
        up_s = e.take(2 * NI * D, F16).rearrange("p (s i d) -> p s i d", s=2, i=NI)
        assert e.at == 2 * KC * NE
        e = Region(embs)
        raw_gu = e.take(2 * KC * INTER)
        raw_wd = e.take(NIC * D)
        kf32 = e.take(KC * 2 * HEADS * NK)
        wq_sb = e.take(8 * D)[0:HALF].rearrange("p (g d) -> p g d", g=8)
        keys_sb = e.take(8 * NK)[0:HALF].rearrange("p (g k) -> p g k", g=8)
        ww_sb = e.take(KC * D).rearrange("p (k d) -> p k d", k=KC)
        wr_sb = e.take(KC * D).rearrange("p (k d) -> p k d", k=KC)
        diffs = e.take(T)
        causal = e.take(T)
        max_piece = e.take(PIECE)

        a = Region(arena)
        xin = a.take(NQ * D).rearrange("p (q d) -> p q d", q=NQ)
        xhat = a.take(NQ * D).rearrange("p (q d) -> p q d", q=NQ)
        xT = a.take(KC * (T + 2)).rearrange("p (k t) -> p k t", k=KC)
        v_sb = a.take(NQ * D).rearrange("p (q d) -> p q d", q=NQ)
        split_piece = arena[:, 0:2 * PIECE].rearrange("p (n c) -> p n c", n=2)
        assert a.at >= 2 * PIECE
        att = [a.take(T - P * s) for s in range(NQ)]
        decay_tab = a.take(T)
        wc = a.take(KC * D).rearrange("p (k d) -> p k d", k=KC)
        x1 = a.take(NQ * D).rearrange("p (q d) -> p q d", q=NQ)
        x1k = a.take(NQ * D).rearrange("p (q d) -> p q d", q=NQ)
        x1m = a.take(NQ * D).rearrange("p (q d) -> p q d", q=NQ)
        x2n = a.take(NQ * D).rearrange("p (q d) -> p q d", q=NQ)
        x2s = a.take(2 * KC * T, F16).rearrange("p (s k t) -> p s k t", s=2, k=KC)
        wgu_s = a.take(4 * KC * INTER, F16).rearrange("p (s g k n) -> p s g k n", s=2, g=2, k=KC)
        wd_s = a.take(2 * NIC * D, F16).rearrange("p (s c d) -> p s c d", s=2, c=NIC)
        kf_s = a.take(2 * KC * 2 * HEADS * NK, F16).rearrange("p (s k n) -> p s k n", s=2, k=KC)
        sim = a.take(NQ * 8 * NK).rearrange("p (q g k) -> p q g k", q=NQ, g=8)
        h_s = a.take(2 * NIC * T, F16).rearrange("p (s c t) -> p s c t", s=2, c=NIC)
        gate = a.take(2 * T).rearrange("p (n t) -> p n t", n=2)
        h32 = a.take(2 * T).rearrange("p (n t) -> p n t", n=2)
        top = a.take(2 * NQ * HEADS * TOPK).rearrange("p (g q h k) -> p g q h k", g=2, q=NQ, h=HEADS)
        topi = a.take(2 * NQ * HEADS * TOPK, U32).rearrange("p (g q h k) -> p g q h k", g=2, q=NQ, h=HEADS)
        comb = a.take(HEADS * 64).rearrange("p (h a b) -> p h a b", h=HEADS, a=TOPK)
        best = a.take(NQ * PAIRS).rearrange("p (q h k) -> p q h k", q=NQ, h=HEADS)
        besti = a.take(NQ * PAIRS, U32)
        rank_of = [a.take(NQ * PAIRS, U32) for _ in range(2)]
        topf = a.take(2 * NQ * HEADS * TOPK).rearrange("p (g c r) -> p g c r", g=2, r=8)
        hit = [a.take(NQ * PAIRS * 8).rearrange("p (g k r) -> p g k r", k=8, r=8) for _ in range(2)]
        hit2 = a.take(NQ * PAIRS * 8).rearrange("p (g k r) -> p g k r", k=8, r=8)
        pick = [a.take(NQ * PAIRS) for _ in range(2)]
        past = a.take(NQ * PAIRS)
        esub = a.take(NQ * PAIRS)
        esum = a.take(NQ * HEADS)
        table = a.take(3 * NQ * PAIRS).rearrange("p (n c) -> p n c", n=3)
        tab16 = a.take(4 * P, F16).rearrange("p (h n t) -> p n h t", h=2, n=4)
        stats = a.take(NQ * 6).rearrange("p (q n) -> p q n", q=NQ)
        mv = a.take(NQ * 2).rearrange("p (q n) -> p q n", q=NQ)
        ve, nh, r0, r1, r2 = (a.take(NQ) for _ in range(5))

        c = Region(arena)
        p_sb = c.take(2 * NI * TH).rearrange("p (n i q t) -> p n i q t", n=2, i=NI, q=NQ)
        silu_z = c.take(2 * 2 * TH).rearrange("p (n t) -> p n t", n=2)
        g32 = c.take(2 * 2 * TH).rearrange("p (n t) -> p n t", n=2)
        g_s = c.take(2 * 2 * 2 * TH, F16).rearrange("p (n s i t) -> p n s i t", n=2, s=2, i=2)
        hit_i = c.take(16 * NI, F16).rearrange("p (t i) -> p t i", t=16)
        hit_p = c.take(2 * 16 * NI, F16).rearrange("p (s t i) -> p s t i", s=2, t=16)
        a_sb = c.take(2 * 2 * 16 * NQ * NI, F16).rearrange("p (n s t q i) -> p n s t q i", n=2, s=2, t=16, q=NQ)
        b_sb = c.take(2 * 16 * P, F16).rearrange("p (n t j) -> p n t j", n=2, t=16)
        x2_sb = c.take(2 * 2 * KC * TH, F16).rearrange("p (n s k t) -> p n s k t", n=2, s=2, k=KC)
        tab_sb = c.take(2 * 4 * TQ, F16).rearrange("p (n m t) -> p n m t", n=2, m=4)
        res = c.take(2 * 2 * D).rearrange("p (n u d) -> p n u d", n=2, u=2)
        fin = c.take(2 * 2 * D).rearrange("p (n u d) -> p n u d", n=2, u=2)

        def col(n, k=1):
            return scal[:, n:n + k]

        KF, WG, WU, WD_, DN, UP = range(6)
        mx, mxr, pw, rp, ws = (8 * n for n in range(5))
        SIM_OUT, GATE_IN, H_SCALE, MLP_OUT, Z_IN, PROB, EXP_OUT = range(40, 47)
        DEC, LA, NEG, POS, NAB, EXPN, LNN, LOGG, ALPHA = range(48, 57)

        def embs_part(m):
            down = down_s[:, m].rearrange("p k e -> p (k e)")
            upp = up_s[:, m].rearrange("p i d -> p (i d)")
            half = NPIECE // 2

            def piece(n):
                v = down if n < half else upp
                return v[:, (n % half) * PIECE:(n % half + 1) * PIECE]
            return piece

        def after(b, h, n):
            return b + (h + n) // 2, (h + n) % 2

        x_q = x.rearrange("b (q t) d -> b t q d", t=P)
        x1_q = x1_d.rearrange("b (q t) d -> b t q d", t=P)

        def at(v, b):
            return v[bass.ds(b, 1)]

        block = ctx.enter_context(nc.Block())

        @block.sync
        def _(sp):
            def load_x(b):
                sp.dma_start(xin, at(x_q, b).rearrange("o t q d -> (o t) q d")).then_inc(sem("x_in"), 16)

            load_x(0)
            for dst, src in ((ident[:, :], ident_d), (ww_sb, wwrite.rearrange("(k p) d -> p k d", p=P)),
                             (wr_sb, wreadT.rearrange("(k p) d -> p k d", p=P)), (diffs, diffs_d), (causal, causal_d),
                             (col(DEC), decay), (col(LA), log_alpha), (iota[:, :], iota_d), (rank[:, :], rank_d),
                             (qmask[:, :], qmask_d)):
                sp.dma_start(dst, src).then_inc(sem("const_in"), 16)
            sp.dma_start(wq_sb, wq.rearrange("(g n) d -> n g d", n=HALF)).then_inc(sem("wq_in"), 16)
            sp.dma_start(keys_sb, keys).then_inc(sem("wq_in"), 16)
            sp.dma_start(raw_gu[:, 0:KC * INTER], wg).then_inc(sem("mlp_in"), 16)
            sp.dma_start(raw_gu[:, KC * INTER:2 * KC * INTER], wu).then_inc(sem("mlp_in"), 16)
            sp.dma_start(raw_wd, wd).then_inc(sem("mlp_in"), 16)
            sp.dma_start(max_piece, emb[:, 0:PIECE]).then_inc(sem("piece_in"), 16)

            def prefetch(b):
                sp.wait_ge(sem("xin_used"), b + 1)
                load_x(b + 1)

            def store_x2(b):
                sp.wait_ge(sem("x2_lo"), 2 * b + 2)
                sp.dma_start(x2_d[bass.ds(b, 1)].rearrange("o p s k t -> (o p) s k t"), x2s).then_inc(sem("x2_out"), 16)

            def store_ffn(b):
                sp.wait_ge(sem("x1m"), NQ * b + NQ)
                sp.dma_start(at(x1_q, b).rearrange("o t q d -> (o t) q d"), x1m).then_inc(sem("x1_out"), 16)
                sp.wait_ge(sem("tab_ij"), b + 1)
                sp.wait_ge(sem("tab_lo"), b + 1)
                for h in range(2):
                    sp.dma_start(tab_d[bass.ds(b, 1), h].rearrange("o p n t -> (o p) n t"),
                                 tab16[:, :, h]).then_inc(sem("tab_out"), 16)

            prefetch(0)
            store_x2(0)
            def step(b, more):
                sp.wait_ge(sem("piece_max"), b + 1)
                sp.dma_start(max_piece, emb[:, bass.ds(b * PIECE + PIECE, PIECE)]).then_inc(sem("piece_in"), 16)
                if more:
                    prefetch(b + 1)
                store_x2(b + 1)
                store_ffn(b)

            with sp.Fori(0, NB - 2) as b:
                step(b, True)
            step(NB - 2, False)

            sp.wait_ge(sem("attn_room_free"), 1)
            for n in range(NPIECE):
                if n >= 2:
                    sp.wait_ge(sem("emb_lo"), n - 1)
                sp.dma_start(split_piece[:, n % 2], emb[:, n * PIECE:(n + 1) * PIECE]).then_inc(sem(f"split_in{n % 2}"), 16)
            store_ffn(NB - 1)
            sp.wait_ge(sem("x2_out"), 16 * NB)
            sp.wait_ge(sem("x1_out"), 16 * NB)
            sp.wait_ge(sem("tab_out"), 2 * 16 * NB)

            sp.wait_ge(sem("first_done"), 4)

            def load_tile(b, h):
                src = x2_d[bass.ds(b, 1)].rearrange("o p s k (q t) -> (o p) (s k q) t", q=NQ)[:, :, h * TQ:(h + 1) * TQ]
                sp.dma_start(x2_sb[:, h].rearrange("p s k (q t) -> p (s k q) t", q=NQ), src).then_inc(sem(f"x2_in{h}"), 16)

            def load_tab(b, h):
                sp.dma_start(tab_sb[:, h], tab_d[bass.ds(b, 1), h].rearrange("o p n t -> (o p) n t")).then_inc(sem(f"tab_in{h}"), 16)

            def rows(v, b, h, q):
                return v[bass.ds(b, 1), q * P + h * TQ:q * P + (h + 1) * TQ].rearrange("o t d -> (o t) d")

            def load_res(b, h):
                for q in range(NQ):
                    sp.dma_start(res[(q % 2) * TQ:(q % 2 + 1) * TQ, h, q // 2], rows(x1_d, b, h, q)).then_inc(sem(f"res_in{h}"), 16)

            def store(b, h):
                sp.wait_ge(sem("fin"), 4 * b + 2 * h + 2)
                for q in range(NQ):
                    sp.dma_start(rows(out, b, h, q), fin[(q % 2) * TQ:(q % 2 + 1) * TQ, h, q // 2]).then_inc(sem(f"stored{h}"), 16)

            for h in range(2):
                load_tile(0, h)
                load_tab(0, h)
                load_res(0, h)
            with sp.Fori(0, NB - 1) as b:
                sp.wait_ge(sem("a_built"), 8 * b + 4)
                sp.wait_ge(sem("b_built"), 8 * b + 4)
                load_tab(b + 1, 0)
                sp.wait_ge(sem("z"), 32 * b + 16)
                load_tile(b + 1, 0)
                sp.wait_ge(sem("a_built"), 8 * b + 8)
                sp.wait_ge(sem("b_built"), 8 * b + 8)
                load_tab(b + 1, 1)
                store(b, 0)
                load_res(b + 1, 0)
                sp.wait_ge(sem("z"), 32 * b + 32)
                load_tile(b + 1, 1)
                store(b, 1)
                load_res(b + 1, 1)
            store(NB - 1, 0)
            store(NB - 1, 1)
            for h in range(2):
                sp.wait_ge(sem(f"stored{h}"), 16 * NQ * NB)

        @block.tensor
        def _(pe):
            pe.wait_ge(sem("const_in"), 160)
            for ec in range(KC):
                for k in range(KC):
                    last = pe.matmul(bank[0][:, ec * D:(ec + 1) * D], ww_sb[:, k, ec * P:(ec + 1) * P], wr_sb[:, k, :],
                                     start=(k == 0), stop=(k == KC - 1))
            last.then_inc(sem("wc_full"), 1)
            pe.wait_ge(sem("wq_in"), 32)
            for dc in range(KC):
                for g in range(8):
                    last = pe.matmul(bank[4 + 2 * dc + g // 4][:, (g % 4) * NK:(g % 4 + 1) * NK],
                                     wq_sb[:, g, dc * P:(dc + 1) * P], keys_sb[:, g, :], start=True, stop=True)
            last.then_inc(sem("kf_full"), 1)

            def bank_free(n, b, k):
                pe.wait_ge(sem(f"att_free{n}"), 6 * b + k)

            def transpose_rows(src, b, k, ready, full):
                pe.wait_ge(sem(ready), b + 1)
                for kc in range(KC):
                    bank_free(kc, b, k)
                    for q in range(NQ):
                        last = pe.transpose(bank[kc][:, q * P:(q + 1) * P], src[:, q, kc * P:(kc + 1) * P], ident[:, :])
                    last.then_inc(sem(full), 1)

            def t1(b):
                transpose_rows(xhat, b, 0, "xhat", "t1_full")

            def values_scores(b):
                pe.wait_ge(sem("xT"), 2 * b + 2)
                pe.wait_ge(sem("wc"), 1)
                for n in range(2):
                    bank_free(n, b, 1)
                    for q in (2 * n, 2 * n + 1):
                        for k in range(KC):
                            last = pe.matmul(bank[n][:, (q % 2) * D:(q % 2 + 1) * D], xT[:, k, 1 + q * P:1 + (q + 1) * P],
                                             wc[:, k, :], start=(k == 0), stop=(k == KC - 1))
                    last.then_inc(sem("v_full"), 1)
                for s in range(NQ):
                    bank_free(s % 2, b, 2 + s // 2)
                    for k in range(KC):
                        last = pe.matmul(bank[s % 2][:, 0:T - P * s], xT[:, k, s * P:(s + 1) * P], xT[:, k, 1 + s * P:1 + T],
                                         start=(k == 0), stop=(k == KC - 1))
                    last.then_inc(sem("s_full"), 1)

            def reads(b):
                pe.wait_ge(sem("v"), 2 * b + 2)
                pe.wait_ge(sem("masked"), NQ * b + NQ)
                for n in range(2):
                    bank_free(n, b, 4)
                    for q in (2 * n, 2 * n + 1):
                        for s in range(q + 1):
                            last = pe.matmul(bank[n][:, (q % 2) * D:(q % 2 + 1) * D], att[s][:, (q - s) * P:(q - s + 1) * P],
                                             v_sb[:, s, :], start=(s == 0), stop=(s == q))
                    last.then_inc(sem("r_full"), 1)

            def t2(b):
                transpose_rows(x2n, b, 5, "x2n", "t2_full")

            def similarities(b):
                pe.wait_ge(sem("x2_lo"), 2 * b + 2)
                for q in range(NQ):
                    for n in range(2):
                        pe.wait_ge(sem(f"sim_free{n}"), (6 - n) * b + q)
                        last = three(bank[2 + n][:, :], lambda s, k: x2s[:, s, k, q * P:(q + 1) * P],
                                     lambda s, k: kf_s[:, s, k, n * 512:(n + 1) * 512])
                        last.then_inc(sem("sim_full"), 1)

            def three(dst, stat, mov, ks=KC):
                n = 0
                for k in range(ks):
                    for s, m in HALVES:
                        last = pe.matmul(dst, stat(s, k), mov(m, k), start=(n == 0), stop=(n == 3 * ks - 1))
                        n += 1
                return last

            def mlp_up(b, c):
                pe.wait_ge(sem(f"mlp_free{c % 2}"), 4 * b + c // 2)
                for g in range(2):
                    last = three(bank[4 + 2 * (c % 2) + g][:, :], lambda s, k: wgu_s[:, s, g, k, c * P:(c + 1) * P],
                                 lambda s, k: x2s[:, s, k])
                last.then_inc(sem("gu_full"), 1)

            def mlp_down(b):
                pe.wait_ge(sem("h_lo"), NIC * b + NIC)
                for n in range(2):
                    pe.wait_ge(sem(f"sim_free{n}"), (6 - n) * b + 4)
                    for q in (2 * n, 2 * n + 1):
                        last = three(bank[2 + n][:, (q % 2) * D:(q % 2 + 1) * D],
                                     lambda s, k: h_s[:, s, k, q * P:(q + 1) * P],
                                     lambda s, k: wd_s[:, s, k, :], ks=NIC)
                    last.then_inc(sem("down_full"), 1)

            def table_t(b):
                pe.wait_ge(sem("indices"), b + 1)
                pe.wait_ge(sem("probs"), b + 1)
                pe.wait_ge(sem("sim_free0"), 6 * b + 5)
                for n in range(3):
                    last = pe.transpose(bank[2][:, n * P:(n + 1) * P], table[:, n, :], ident[:, :])
                last.then_inc(sem("tab_full"), 1)

            pe.wait_ge(sem("wc"), 1)
            t1(0)
            values_scores(0)
            reads(0)
            t2(0)
            pe.wait_ge(sem("split_w"), 1)
            with pe.Fori(0, NB - 1) as b:
                similarities(b)
                t1(b + 1)
                mlp_up(b, 0)
                mlp_up(b, 1)
                values_scores(b + 1)
                mlp_up(b, 2)
                mlp_up(b, 3)
                reads(b + 1)
                for c in range(4, NIC):
                    mlp_up(b, c)
                t2(b + 1)
                mlp_down(b)
                table_t(b)
            b = NB - 1
            similarities(b)
            for c in range(NIC):
                mlp_up(b, c)
            mlp_down(b)
            table_t(b)
            pe.wait_ge(sem("tab_ij"), NB)
            pe.wait_ge(sem("tab_lo"), NB)
            pe.transpose(bank[3][:, 0:P], ident[:, :], ident[:, :]).then_inc(sem("first_done"), 1)
            pe.wait_ge(sem("first_done"), 4)

            def z(b, h, s):
                pe.wait_ge(sem(f"z_free{s % 2}"), 16 * b + 8 * h + s // 2)
                if s == 0:
                    pe.wait_ge(sem(f"x2_in{h}"), 16 * b + 16)
                for i in range(2):
                    e = (2 * s + i) * P
                    last = three(bank[s % 2][:, i * TH:(i + 1) * TH], lambda m, k: down_s[:, m, k, e:e + P],
                                 lambda m, k: x2_sb[:, h, m, k, :])
                last.then_inc(sem("z"), 1)

            def scatter(b, h, s):
                c = s // 4
                n = 2 + s % 2
                if s % 4 == 0:
                    pe.wait_ge(sem("a_built"), 8 * b + 4 * h + c + 1)
                    pe.wait_ge(sem("b_built"), 8 * b + 4 * h + c + 1)
                pe.wait_ge(sem(f"p_free{s % 2}"), 16 * b + 8 * h + s // 2)
                for t in range(4):
                    for m in range(2):
                        last = pe.matmul(bank[n][:, t * P:(t + 1) * P], b_sb[:, c % 2, 4 * (s % 4) + t, :],
                                         a_sb[:, c % 2, m, 4 * (s % 4) + t].rearrange("p q i -> p (q i)"),
                                         start=(m == 0), stop=(m == 1))
                last.then_inc(sem("p_full"), 1)

            def up(b, h, s):
                pe.wait_ge(sem("g_lo"), 32 * b + 16 * h + s + 1)
                if s == 0:
                    pe.wait_ge(sem(f"sum_free{h}"), 2 * b)
                for i in range(2):
                    for u in range(2):
                        for m, w in HALVES:
                            last = pe.matmul(bank[4 + 2 * h + u][:, 0:D], g_s[:, s % 2, m, i, u * P:(u + 1) * P],
                                             up_s[:, w, 2 * s + i, :], start=(s == 0 and i == 0 and (m, w) == (0, 0)),
                                             stop=(s == NI // 2 - 1 and i == 1 and (m, w) == HALVES[-1]))
                last.then_inc(sem("up"), 1)

            def tile(b, h, rest):
                for s in range(16):
                    n, m = divmod(s + 2, 16)
                    if n <= rest:
                        z(*after(b, h, n), m)
                    if n + 1 <= rest:
                        scatter(*after(b, h, n + 1), m)
                    up(b, h, s)

            for s in range(18):
                scatter(*after(0, 0, s // 16), s % 16)
            z(0, 0, 0)
            z(0, 0, 1)
            with pe.Fori(0, NB - 1) as b:
                tile(b, 0, 2)
                tile(b, 1, 2)
            tile(NB - 1, 0, 1)
            tile(NB - 1, 1, 0)

        @block.scalar
        def _(act):
            def copy(dst, src, scale=1.0):
                return act.activation(dst, src, ACT.Copy, scale=scale)

            act.wait_ge(sem("scal_chain"), 3)
            act.activation(col(EXPN), col(NAB), ACT.Exp).then_inc(sem("act_scal"), 1)
            act.wait_ge(sem("act_scal"), 1)
            act.activation(col(LNN), col(EXPN), ACT.Ln, bias=1.0).then_inc(sem("act_scal"), 1)
            act.activation(col(ALPHA), col(LA), ACT.Exp).then_inc(sem("act_scal"), 1)
            act.wait_ge(sem("act_scal"), 3)
            act.wait_ge(sem("wc_full"), 1)
            copy(wc.rearrange("p k d -> p (k d)"), bank[0][:, :], col(ALPHA)).then_inc(sem("wc"), 1)
            act.wait_ge(sem("scal_chain"), 4)
            act.activation(decay_tab, diffs, ACT.Exp, scale=col(LOGG)).then_inc(sem("act_scal"), 1)

            def xT_out(b):
                for k in range(KC):
                    act.wait_ge(sem("t1_full"), 2 * b + k + 1)
                    copy(xT[:, k, 1:1 + T], bank[k][:, :]).then_inc(sem("xT"), 1)
                    act.wait_ge(sem("xT"), 2 * b + k + 1)
                    act.sem_inc(sem(f"att_free{k}"), 1)

            def v_out(b):
                for n in range(2):
                    act.wait_ge(sem("v_full"), 2 * b + n + 1)
                    copy(v_sb[:, 2 * n:2 * n + 2].rearrange("p q d -> p (q d)"), bank[n][:, :]).then_inc(sem("v"), 1)
                    act.wait_ge(sem("v"), 2 * b + n + 1)
                    act.sem_inc(sem(f"att_free{n}"), 1)

            def x2_hi(b):
                act.wait_ge(sem("x2_out"), 16 * b)
                for k in range(KC):
                    act.wait_ge(sem("t2_full"), 2 * b + k + 1)
                    act.activation(x2s[:, 0, k], bank[k][:, :], ACT.Copy, scale=X_SCALE).then_inc(sem("x2_hi"), 1)

            def sim_out(b, q):
                for n in range(2):
                    act.wait_ge(sem("sim_full"), 8 * b + 2 * q + n + 1)
                    if n == 0 and q == 0:
                        act.wait_ge(sem("topped"), NQ * b)
                    copy(sim[:, q, 4 * n:4 * n + 4].rearrange("p g k -> p (g k)"), bank[2 + n][:, :],
                         col(SIM_OUT)).then_inc(sem("sim"), 1)
                    act.wait_ge(sem("sim"), 8 * b + 2 * q + n + 1)
                    act.sem_inc(sem(f"sim_free{n}"), 1)

            def silu_gate(b, c):
                act.wait_ge(sem("gu_full"), NIC * b + c + 1)
                act.wait_ge(sem(f"mlp_free{c % 2}"), 4 * b + c // 2)
                act.activation(gate[:, c % 2], bank[4 + 2 * (c % 2)][:, :], ACT.Silu, scale=col(GATE_IN)).then_inc(sem("gate"), 1)

            def h_hi(b, c):
                act.wait_ge(sem("h32"), NIC * b + c + 1)
                act.wait_ge(sem("down_full"), 2 * b)
                copy(h_s[:, 0, c], h32[:, c % 2]).then_inc(sem("h_hi"), 1)

            def exp_scores(b):
                act.wait_ge(sem("esub"), b + 1)
                act.activation(esub, esub, ACT.Exp).then_inc(sem("exped"), 1)

            def tab_hi(b):
                act.wait_ge(sem("tab_full"), b + 1)
                act.wait_ge(sem("tab_out"), 32 * b)
                act.activation(tab16[:, 0:2], bank[2][:, 0:2 * P].rearrange("p (n h t) -> p n h t", n=2, h=2),
                               ACT.Copy).then_inc(sem("tab_ij"), 1)
                act.activation(tab16[:, 2], bank[2][:, 2 * P:3 * P].rearrange("p (h t) -> p h t", h=2),
                               ACT.Copy, scale=P_SCALE).then_inc(sem("tab_hi"), 1)

            act.wait_ge(sem("kf_full"), 1)
            for k in range(4):
                copy(kf32[:, k * 512:(k + 1) * 512], bank[4 + k][:, :]).then_inc(sem("kf32"), 1)
            xT_out(0)
            v_out(0)
            act.wait_ge(sem("w_scales"), 1)
            act.wait_ge(sem("kf32"), 4)
            copy(wgu_s[:, 0, 0].rearrange("p k n -> p (k n)"), raw_gu[:, 0:KC * INTER], col(ws + WG)).then_inc(sem("w_hi"), 1)
            copy(wgu_s[:, 0, 1].rearrange("p k n -> p (k n)"), raw_gu[:, KC * INTER:], col(ws + WU)).then_inc(sem("w_hi"), 1)
            copy(wd_s[:, 0].rearrange("p c d -> p (c d)"), raw_wd, col(ws + WD_)).then_inc(sem("w_hi"), 1)
            copy(kf_s[:, 0].rearrange("p k n -> p (k n)"), kf32, col(ws + KF)).then_inc(sem("w_hi"), 1)
            x2_hi(0)
            with act.Fori(0, NB - 1) as b:
                for q in range(NQ):
                    sim_out(b, q)
                xT_out(b + 1)
                silu_gate(b, 0)
                silu_gate(b, 1)
                h_hi(b, 0)
                v_out(b + 1)
                for c in range(2, NIC):
                    silu_gate(b, c)
                    h_hi(b, c - 1)
                h_hi(b, NIC - 1)
                x2_hi(b + 1)
                exp_scores(b)
                tab_hi(b)
            b = NB - 1
            for q in range(NQ):
                sim_out(b, q)
            silu_gate(b, 0)
            for c in range(1, NIC):
                silu_gate(b, c)
                h_hi(b, c - 1)
            h_hi(b, NIC - 1)
            exp_scores(b)
            emb_hi = embs_part(0)
            act.wait_ge(sem("e_scales"), 1)
            for n in range(NPIECE):
                act.wait_ge(sem(f"split_in{n % 2}"), 16 * (n // 2 + 1))
                copy(emb_hi(n), split_piece[:, n % 2], col(ws + (DN if n < NPIECE // 2 else UP))).then_inc(sem("emb_hi"), 1)
            tab_hi(b)
            act.wait_ge(sem("emb_hi"), NPIECE)
            act.wait_ge(sem("tab_hi"), NB)
            act.activation(col(EXPN), col(NAB), ACT.Copy).then_inc(sem("first_done"), 1)
            act.wait_ge(sem("first_done"), 4)

            def silu_of(b, h, s):
                act.wait_ge(sem("z"), 32 * b + 16 * h + s + 1)
                act.wait_ge(sem(f"s_free{s % 2}"), 16 * b + 8 * h + s // 2)
                act.activation(silu_z[:, s % 2], bank[s % 2][:, :], ACT.Silu, scale=col(Z_IN)).then_inc(sem(f"z_free{s % 2}"), 1)

            def g_hi(b, h, s):
                act.wait_ge(sem(f"s_free{s % 2}"), 16 * b + 8 * h + s // 2 + 1)
                if not (isinstance(b, int) and b == h == s == 0):
                    act.wait_ge(sem("up"), 32 * b + 16 * h + s - 1)
                copy(g_s[:, s % 2, 0].rearrange("p i t -> p (i t)"), g32[:, s % 2]).then_inc(sem("g_hi"), 1)

            def p_out(b, h, s):
                act.wait_ge(sem("p_full"), 32 * b + 16 * h + s + 1)
                if s == 0 and not (isinstance(b, int) and b == h == 0):
                    act.wait_ge(sem("p_used"), 2 * b + h - 1)
                act.activation(p_sb[:, h, :, :, 4 * s:4 * s + 4], bank[2 + s % 2][:, :].rearrange("p (t q i) -> p i q t", t=4, q=NQ),
                               ACT.Copy, scale=col(PROB)).then_inc(sem(f"p_free{s % 2}"), 1)

            def tile(b, h, rest):
                for s in range(16):
                    n, m = divmod(s + 1, 16)
                    if n <= rest:
                        g_hi(*after(b, h, n), m)
                    n, m = divmod(s + 2, 16)
                    if n <= rest:
                        silu_of(*after(b, h, n), m)
                    if n + 1 <= rest:
                        p_out(*after(b, h, n + 1), m)

            for s in range(18):
                p_out(*after(0, 0, s // 16), s % 16)
            silu_of(0, 0, 0)
            silu_of(0, 0, 1)
            g_hi(0, 0, 0)
            with act.Fori(0, NB - 1) as b:
                tile(b, 0, 2)
                tile(b, 1, 2)
            tile(NB - 1, 0, 1)
            tile(NB - 1, 1, 0)

        @block.vector
        def _(dve):
            def chained(name, base=0):
                count = [0]

                def link(ins):
                    count[0] += 1
                    ins.then_inc(sem(name), 1)
                    dve.wait_ge(sem(name), base + count[0])
                return link

            def split(dst, src, scale, hi):
                return dve.scalar_tensor_tensor(dst, src, scale, hi, ALU.mult, ALU.subtract)

            def step_past():
                dve.sem_inc(sem("dve_steps"), 1)

            def rsqrt(link):
                link(dve.tensor_scalar(ve, mv[:, :, 1], EPS, None, ALU.add))
                link(dve.tensor_scalar(nh, ve, -0.5, None, ALU.mult))
                link(dve.tensor_scalar(r0.bitcast(I32), ve.bitcast(I32), 1, None, ALU.arith_shift_right))
                link(dve.tensor_scalar(r1.bitcast(I32), r0.bitcast(I32), -1.0, float(RSQRT_SEED), ALU.mult, ALU.add))
                r = r1
                for _ in range(3):
                    link(dve.tensor_tensor(r0, r, r, ALU.mult))
                    link(dve.tensor_tensor(r0, r0, nh, ALU.mult))
                    o = r2 if r is r1 else r1
                    link(dve.scalar_tensor_tensor(o, r0, 1.5, r, ALU.add, ALU.mult))
                    r = o
                return r

            def normalise(dst, src, link, done):
                for q in range(NQ):
                    last = dve.bn_stats(stats[:, q], src[:, q])
                link(last)
                step_past()
                for q in range(NQ):
                    last = dve.bn_aggr(mv[:, q], stats[:, q])
                link(last)
                r = rsqrt(link)
                for q in range(NQ):
                    last = dve.tensor_scalar(dst[:, q], src[:, q], mv[:, q, 0:1], r[:, q:q + 1], ALU.subtract, ALU.mult)
                last.then_inc(sem(done), 1)

            LN_LINKS = 2 + 4 + 9

            def ln1(b):
                link = chained("ln1_chain", LN_LINKS * b)
                dve.wait_ge(sem("x_in"), 16 * b + 16)
                dve.wait_ge(sem("t1_full"), 2 * b)
                dve.wait_ge(sem("x2n"), b)
                normalise(xhat, xin, link, "xhat")
                dve.wait_ge(sem("xhat"), b + 1)
                dve.tensor_tensor(xin, xin, xhat, ALU.add).then_inc(sem("xsum"), 1)

            def masks(b):
                dve.wait_ge(sem("r_full"), 2 * b)
                for s in range(NQ):
                    dve.wait_ge(sem("s_full"), NQ * b + s + 1)
                    dve.tensor_tensor(att[s], bank[s % 2][:, 0:T - P * s], decay_tab[:, 0:T - P * s], ALU.mult).then_inc(sem("masked"), 1)
                    dve.wait_ge(sem("masked"), NQ * b + s + 1)
                    dve.sem_inc(sem(f"att_free{s % 2}"), 1)

            def ln2(b):
                dve.wait_ge(sem("xsum"), b + 1)
                dve.wait_ge(sem("x2n"), b)
                dve.wait_ge(sem("x1_kept"), b)
                for n in range(2):
                    dve.wait_ge(sem("r_full"), 2 * b + n + 1)
                    dve.tensor_tensor(x1[:, 2 * n:2 * n + 2].rearrange("p q d -> p (q d)"), bank[n][:, :],
                                      xin[:, 2 * n:2 * n + 2].rearrange("p q d -> p (q d)"), ALU.add).then_inc(sem("x1"), 1)
                    dve.wait_ge(sem("x1"), 2 * b + n + 1)
                    dve.sem_inc(sem(f"att_free{n}"), 1)
                dve.sem_inc(sem("xin_used"), 1)
                link = chained("ln2_chain", LN_LINKS * b)
                dve.wait_ge(sem("t2_full"), 2 * b)
                normalise(x2n, x1, link, "x2n")

            def x2_lo(b):
                for k in range(KC):
                    dve.wait_ge(sem("x2_hi"), 2 * b + k + 1)
                    split(x2s[:, 1, k], bank[k][:, :], X_SCALE, x2s[:, 0, k]).then_inc(sem("x2_lo"), 1)
                    dve.wait_ge(sem("x2_lo"), 2 * b + k + 1)
                    dve.sem_inc(sem(f"att_free{k}"), 1)

            def top8(b, q):
                if q == 0:
                    dve.wait_ge(sem("picks"), b)
                    dve.wait_ge(sem("hit"), 3 * b)
                    dve.wait_ge(sem("esub"), b)
                dve.wait_ge(sem("sim"), 8 * b + 2 * q + 2)
                step_past()
                for g in range(8):
                    last = dve.max(top[:, g // 4, q, g % 4], sim[:, q, g])
                last.then_inc(sem("top_chain"), 1)
                dve.wait_ge(sem("top_chain"), 5 * (NQ * b + q) + 1)
                dve.tensor_tensor(comb, top[:, 0, q, :, :].unsqueeze(3).to_broadcast([P, HEADS, 8, 8]),
                                  top[:, 1, q, :, :].unsqueeze(2).to_broadcast([P, HEADS, 8, 8]), ALU.add).then_inc(sem("top_chain"), 1)
                step_past()
                for g in range(8):
                    last = dve.max_index(topi[:, g // 4, q, g % 4], top[:, g // 4, q, g % 4], sim[:, q, g])
                last.then_inc(sem("top_chain"), 1)
                dve.wait_ge(sem("top_chain"), 5 * (NQ * b + q) + 3)
                step_past()
                for h in range(HEADS):
                    last = dve.max(best[:, q, h], comb[:, h].rearrange("p a b -> p (a b)"))
                last.then_inc(sem("top_chain"), 1)
                dve.wait_ge(sem("top_chain"), 5 * (NQ * b + q) + 4)
                step_past()
                for h in range(HEADS):
                    last = dve.max_index(besti[:, (q * HEADS + h) * 8:(q * HEADS + h) * 8 + 8], best[:, q, h],
                                         comb[:, h].rearrange("p a b -> p (a b)"))
                last.then_inc(sem("top_chain"), 1)
                dve.wait_ge(sem("top_chain"), 5 * (NQ * b + q) + 5)
                dve.sem_inc(sem("topped"), 1)

            def ranks(b):
                dve.wait_ge(sem("probs"), b)
                dve.tensor_scalar(rank_of[0], besti, 3, None, ALU.logical_shift_right)
                dve.tensor_scalar(rank_of[1], besti, 7, None, ALU.bitwise_and).then_inc(sem("ranks"), 1)
                dve.wait_ge(sem("ranks"), b + 1)
                for g in range(2):
                    dve.tensor_tensor(hit[g], rank_of[g].rearrange("p (g k) -> p g k", k=8).unsqueeze(3).to_broadcast([P, NQ * HEADS, 8, 8]),
                                      rank[:, :].unsqueeze(1).unsqueeze(1).to_broadcast([P, NQ * HEADS, 8, 8]),
                                      ALU.is_equal).then_inc(sem("hit"), 1)
                dve.tensor_copy(topf, topi.rearrange("p g q h r -> p g (q h) r")).then_inc(sem("hit"), 1)
                bq = best.rearrange("p q h k -> p (q h) k")
                dve.tensor_tensor(esub.rearrange("p (g k) -> p g k", k=8), bq, bq[:, :, 0:1].to_broadcast([P, NQ * HEADS, 8]),
                                  ALU.subtract).then_inc(sem("esub"), 1)

            def indices(b):
                dve.wait_ge(sem("picks"), b + 1)
                dve.wait_ge(sem("tab_full"), b)
                dve.wait_ge(sem("indices"), b)
                dve.tensor_scalar(past, pick[0], float(NI), float(P - 1), ALU.is_ge, ALU.mult).then_inc(sem("past"), 1)
                dve.tensor_scalar(table[:, 0], pick[0], float(NI - 1), None, ALU.min)
                dve.wait_ge(sem("past"), b + 1)
                dve.tensor_tensor(table[:, 1], pick[1], past, ALU.max).then_inc(sem("indices"), 1)

            def softmax(b):
                link = chained("softmax_chain", 2 * b)
                dve.wait_ge(sem("exped"), b + 1)
                dve.wait_ge(sem("tab_full"), b)
                e3 = esub.rearrange("p (g k) -> p g k", k=8)
                link(dve.tensor_reduce(esum, e3, AX_X, ALU.add))
                link(dve.reciprocal(esum, esum))
                dve.tensor_tensor(table[:, 2, :].rearrange("p (g k) -> p g k", k=8), e3,
                                  esum.unsqueeze(2).to_broadcast([P, NQ * HEADS, 8]), ALU.mult).then_inc(sem("probs"), 1)

            def hidden(b, c):
                dve.wait_ge(sem("gate"), NIC * b + c + 1)
                dve.wait_ge(sem("h_lo"), NIC * b + max(c - 1, 0))
                dve.scalar_tensor_tensor(h32[:, c % 2], bank[5 + 2 * (c % 2)][:, :], col(H_SCALE), gate[:, c % 2],
                                         ALU.mult, ALU.mult).then_inc(sem("h32"), 1)
                dve.wait_ge(sem("h32"), NIC * b + c + 1)
                dve.sem_inc(sem(f"mlp_free{c % 2}"), 1)

            def h_lo(b, c):
                dve.wait_ge(sem("h_hi"), NIC * b + c + 1)
                dve.tensor_tensor(h_s[:, 1, c], h32[:, c % 2], h_s[:, 0, c], ALU.subtract).then_inc(sem("h_lo"), 1)

            def add_mlp(b):
                dve.wait_ge(sem("x1_out"), 16 * b)
                dve.wait_ge(sem("x1_kept"), b + 1)
                for q in range(NQ):
                    dve.wait_ge(sem("down_full"), 2 * b + q // 2 + 1)
                    dve.scalar_tensor_tensor(x1m[:, q], bank[2 + q // 2][:, (q % 2) * D:(q % 2 + 1) * D], col(MLP_OUT),
                                             x1k[:, q], ALU.mult, ALU.add).then_inc(sem("x1m"), 1)
                    if q % 2:
                        dve.wait_ge(sem("x1m"), NQ * b + q + 1)
                        dve.sem_inc(sem(f"sim_free{q // 2}"), 1)

            def tab_lo(b):
                dve.wait_ge(sem("tab_hi"), b + 1)
                dve.wait_ge(sem("tab_ij"), b + 1)
                split(tab16[:, 3], bank[2][:, 2 * P:3 * P].rearrange("p (h t) -> p h t", h=2), P_SCALE,
                      tab16[:, 2]).then_inc(sem("tab_lo"), 1)
                dve.wait_ge(sem("tab_lo"), b + 1)
                dve.sem_inc(sem("sim_free0"), 1)

            dve.wait_ge(sem("const_in"), 160)
            dve.tensor_scalar(col(NEG), col(DEC), -1.0, None, ALU.mult).then_inc(sem("scal_chain"), 1)
            dve.wait_ge(sem("scal_chain"), 1)
            dve.tensor_scalar(col(POS), col(NEG), 0.0, None, ALU.max).then_inc(sem("scal_chain"), 1)
            dve.tensor_tensor(col(NAB), col(NEG), col(DEC), ALU.min).then_inc(sem("scal_chain"), 1)
            dve.memset(xT[:, :, 0:1], 0.0).then_inc(sem("zero_col"), 1)
            ln1(0)
            dve.wait_ge(sem("act_scal"), 2)
            dve.wait_ge(sem("scal_chain"), 3)
            dve.scalar_tensor_tensor(col(LOGG), col(POS), -1.0, col(LNN), ALU.mult, ALU.subtract).then_inc(sem("scal_chain"), 1)
            dve.wait_ge(sem("act_scal"), 4)
            dve.tensor_tensor(decay_tab, decay_tab, causal, ALU.mult).then_inc(sem("decay_tab"), 1)
            dve.wait_ge(sem("decay_tab"), 1)
            dve.wait_ge(sem("zero_col"), 1)

            dve.wait_ge(sem("mlp_in"), 48)
            for n, v in ((WG, raw_gu[:, 0:KC * INTER]), (WU, raw_gu[:, KC * INTER:]), (WD_, raw_wd)):
                dve.tensor_reduce(col(mx + n), v, AX_X, ALU.max, apply_absolute_value=True).then_inc(sem("w_max"), 1)
            dve.wait_ge(sem("kf32"), 4)
            dve.tensor_reduce(col(mx + KF), kf32, AX_X, ALU.max, apply_absolute_value=True).then_inc(sem("w_max"), 1)

            def scales(first, n, link):
                link(dve.tensor_scalar(col(mxr + first, n), col(mxr + first, n), 1e-30, None, ALU.max))
                link(dve.tensor_scalar(col(pw + first, n).bitcast(I32), col(mxr + first, n).bitcast(I32), EXPONENT, None, ALU.bitwise_and))
                link(dve.reciprocal(col(rp + first, n), col(pw + first, n)))
                link(dve.tensor_scalar(col(ws + first, n), col(rp + first, n), W_SCALE, None, ALU.mult))

            masks(0)
            ln2(0)
            link = chained("scale_chain")
            dve.wait_ge(sem("w_maxed"), 1)
            scales(0, 4, link)
            link(dve.tensor_scalar(col(SIM_OUT), col(pw + KF), 1.0 / (X_SCALE * W_SCALE), None, ALU.mult))
            link(dve.tensor_scalar(col(GATE_IN), col(pw + WG), 1.0 / (X_SCALE * W_SCALE), None, ALU.mult))
            link(dve.tensor_scalar(col(H_SCALE), col(rp + WG), 1.0 / (8 * X_SCALE * W_SCALE), None, ALU.mult))
            link(dve.tensor_tensor(col(MLP_OUT), col(pw + WG), col(pw + WU), ALU.mult))
            link(dve.scalar_tensor_tensor(col(MLP_OUT), col(MLP_OUT), 8 / W_SCALE, col(pw + WD_), ALU.mult, ALU.mult))
            dve.sem_inc(sem("w_scales"), 1)
            dve.wait_ge(sem("w_hi"), 4)
            link(split(wgu_s[:, 1, 0].rearrange("p k n -> p (k n)"), raw_gu[:, 0:KC * INTER], col(ws + WG),
                       wgu_s[:, 0, 0].rearrange("p k n -> p (k n)")))
            link(split(wgu_s[:, 1, 1].rearrange("p k n -> p (k n)"), raw_gu[:, KC * INTER:], col(ws + WU),
                       wgu_s[:, 0, 1].rearrange("p k n -> p (k n)")))
            link(split(wd_s[:, 1].rearrange("p c d -> p (c d)"), raw_wd, col(ws + WD_), wd_s[:, 0].rearrange("p c d -> p (c d)")))
            link(split(kf_s[:, 1].rearrange("p k n -> p (k n)"), kf32, col(ws + KF), kf_s[:, 0].rearrange("p k n -> p (k n)")))
            dve.sem_inc(sem("split_w"), 1)
            dve.wait_ge(sem("piece_in"), 16)
            dve.tensor_reduce(col(mx + DN), max_piece, AX_X, ALU.max, apply_absolute_value=True).then_inc(sem("piece_max"), 1)
            dve.wait_ge(sem("piece_max"), 1)
            dve.memset(col(mx + UP), 0.0).then_inc(sem("up_zero"), 1)
            dve.wait_ge(sem("up_zero"), 1)
            x2_lo(0)
            with dve.Fori(0, NB - 1) as b:
                ln1(b + 1)
                top8(b, 0)
                hidden(b, 0)
                hidden(b, 1)
                h_lo(b, 0)
                masks(b + 1)
                top8(b, 1)
                hidden(b, 2)
                h_lo(b, 1)
                hidden(b, 3)
                h_lo(b, 2)
                ln2(b + 1)
                hidden(b, 4)
                h_lo(b, 3)
                top8(b, 2)
                hidden(b, 5)
                h_lo(b, 4)
                top8(b, 3)
                ranks(b)
                hidden(b, 6)
                h_lo(b, 5)
                hidden(b, 7)
                h_lo(b, 6)
                h_lo(b, 7)
                x2_lo(b + 1)
                dve.wait_ge(sem("piece_in"), 16 * b + 32)
                dve.tensor_reduce(col(58), max_piece, AX_X, ALU.max, apply_absolute_value=True).then_inc(sem("piece_max"), 1)
                dve.wait_ge(sem("piece_max"), b + 2)
                dve.wait_ge(sem("mx_chain"), b)
                dve.tensor_tensor(col(mx + DN), col(mx + DN), col(58), ALU.max).then_inc(sem("mx_chain"), 1)
                softmax(b)
                indices(b)
                add_mlp(b)
                tab_lo(b)
            b = NB - 1
            dve.wait_ge(sem("t2_full"), 2 * NB)
            dve.wait_ge(sem("mx_chain"), NB - 1)
            dve.sem_inc(sem("e_max"), 1)
            dve.sem_inc(sem("attn_room_free"), 1)
            for q in range(NQ):
                top8(b, q)
                hidden(b, q)
                if q:
                    h_lo(b, q - 1)
            ranks(b)
            for c in range(4, NIC):
                hidden(b, c)
                h_lo(b, c - 1)
            h_lo(b, NIC - 1)
            link = chained("scale2_chain")
            dve.wait_ge(sem("e_maxed"), 1)
            scales(DN, 2, link)
            link(dve.tensor_scalar(col(Z_IN), col(pw + DN), 1.0 / (X_SCALE * W_SCALE), None, ALU.mult))
            link(dve.tensor_scalar(col(PROB), col(rp + DN), 16 / P_SCALE, None, ALU.mult))
            link(dve.tensor_scalar(col(EXP_OUT), col(pw + DN), 1.0 / 16, None, ALU.mult))
            link(dve.scalar_tensor_tensor(col(EXP_OUT), col(EXP_OUT), 1.0 / W_SCALE, col(pw + UP), ALU.mult, ALU.mult))
            dve.sem_inc(sem("e_scales"), 1)
            softmax(b)
            indices(b)
            hi, lo = embs_part(0), embs_part(1)
            for n in range(NPIECE):
                dve.wait_ge(sem("emb_hi"), n + 1)
                split(lo(n), split_piece[:, n % 2], col(ws + (DN if n < NPIECE // 2 else UP)), hi(n)).then_inc(sem("emb_lo"), 1)
            add_mlp(b)
            tab_lo(b)
            dve.wait_ge(sem("emb_lo"), NPIECE)
            dve.memset(col(59), 0.0).then_inc(sem("first_done"), 1)
            dve.wait_ge(sem("first_done"), 4)

            def product(b, h, s):
                dve.wait_ge(sem(f"z_free{s % 2}"), 16 * b + 8 * h + s // 2 + 1)
                if not (isinstance(b, int) and b == h == s == 0):
                    dve.wait_ge(sem("g_lo"), 32 * b + 16 * h + s - 1)
                if s == 0:
                    for n in range(2):
                        dve.wait_ge(sem(f"p_free{n}"), 16 * b + 8 * h + 8)
                dve.tensor_tensor(g32[:, s % 2].rearrange("p (i q t) -> p i q t", i=2, q=NQ),
                                  silu_z[:, s % 2].rearrange("p (i q t) -> p i q t", i=2, q=NQ),
                                  p_sb[:, h, 2 * s:2 * s + 2], ALU.mult).then_inc(sem(f"s_free{s % 2}"), 1)
                if s == 15:
                    dve.wait_ge(sem("s_free1"), 16 * b + 8 * h + 8)
                    dve.wait_ge(sem("s_free0"), 16 * b + 8 * h + 8)
                    dve.sem_inc(sem("p_used"), 1)

            def g_lo(b, h, s):
                dve.wait_ge(sem("g_hi"), 32 * b + 16 * h + s + 1)
                dve.tensor_tensor(g_s[:, s % 2, 1].rearrange("p i t -> p (i t)"), g32[:, s % 2],
                                  g_s[:, s % 2, 0].rearrange("p i t -> p (i t)"), ALU.subtract).then_inc(sem("g_lo"), 1)

            def build_a(b, h, c, step):
                tab = tab_sb[:, h]
                t0 = 16 * c
                if step == 0:
                    dve.wait_ge(sem(f"tab_in{h}"), 16 * b + 16)
                    dve.wait_ge(sem("hit_p"), 2 * (8 * b + 4 * h + c))
                    dve.tensor_tensor(hit_i, iota[:, 0:NI].unsqueeze(1).to_broadcast([P, 16, NI]),
                                      tab[:, 0, t0:t0 + 16].unsqueeze(2).to_broadcast([P, 16, NI]), ALU.is_equal).then_inc(sem("hit_i"), 1)
                elif step == 1:
                    dve.wait_ge(sem("hit_i"), 8 * b + 4 * h + c + 1)
                    dve.wait_ge(sem("a_built"), 8 * b + 4 * h + c)
                    for m in range(2):
                        dve.tensor_tensor(hit_p[:, m], hit_i, tab[:, 2 + m, t0:t0 + 16].unsqueeze(2).to_broadcast([P, 16, NI]),
                                          ALU.mult).then_inc(sem("hit_p"), 1)
                else:
                    m = step - 2
                    dve.wait_ge(sem("hit_p"), 2 * (8 * b + 4 * h + c + 1))
                    if m == 0 and not (isinstance(b, int) and b == 0 and h == 0 and c < 2):
                        dve.wait_ge(sem("p_full"), 4 * (8 * b + 4 * h + c - 1))
                    for q in range(NQ):
                        last = dve.tensor_scalar(a_sb[:, c % 2, m, :, q, :], hit_p[:, m], qmask[:, q:q + 1], None, ALU.mult)
                    if m == 1:
                        last.then_inc(sem("a_built"), 1)
                        dve.wait_ge(sem("b_differ"), 8 * b + 4 * h + c + 1)
                        dve.tensor_scalar(b_sb[:, c % 2], b_sb[:, c % 2], 0.0, None, ALU.is_equal).then_inc(sem("b_built"), 1)

            def finish(b, h):
                dve.wait_ge(sem("up"), 32 * b + 16 * h + 16)
                dve.wait_ge(sem(f"res_in{h}"), 16 * NQ * b + 16 * NQ)
                dve.wait_ge(sem(f"stored{h}"), 16 * NQ * b)
                for u in range(2):
                    dve.scalar_tensor_tensor(fin[:, h, u], bank[4 + 2 * h + u][:, 0:D], col(EXP_OUT), res[:, h, u],
                                             ALU.mult, ALU.add).then_inc(sem("fin"), 1)
                dve.wait_ge(sem("fin"), 4 * b + 2 * h + 2)
                dve.sem_inc(sem(f"sum_free{h}"), 2)

            def tile(b, h, rest):
                for s in range(16):
                    n, m = divmod(s + 22, 16)
                    if n <= rest:
                        build_a(*after(b, h, n), m // 4, m % 4)
                    n, m = divmod(s + 1, 16)
                    if n <= rest:
                        g_lo(*after(b, h, n), m)
                    n, m = divmod(s + 2, 16)
                    if n <= rest:
                        product(*after(b, h, n), m)
                    if s == 1:
                        prev(b, h)

            def prev(b, h):
                if h == 1:
                    finish(b, 0)
                elif isinstance(b, int) and b == 0:
                    pass
                else:
                    finish(b - 1, 1)

            for m in range(22):
                build_a(0, m // 16, m % 16 // 4, m % 4)
            product(0, 0, 0)
            product(0, 0, 1)
            g_lo(0, 0, 0)
            tile(0, 0, 2)
            tile(0, 1, 2)
            with dve.Fori(1, NB - 1) as b:
                tile(b, 0, 2)
                tile(b, 1, 2)
            tile(NB - 1, 0, 1)
            tile(NB - 1, 1, 0)
            finish(NB - 1, 1)

        @block.gpsimd
        def _(pool):
            MAX = bass.bass_isa.ReduceOp.max
            pool.wait_ge(sem("w_max"), 4)
            pool.partition_all_reduce(col(mxr, 4), col(mx, 4), P, MAX).then_inc(sem("w_maxed"), 1)

            def keep(b):
                pool.wait_ge(sem("x1"), 2 * b + 2)
                pool.wait_ge(sem("x1m"), NQ * b)
                pool.sem_inc(sem("pool_steps"), 1)
                pool.tensor_copy(x1k, x1).then_inc(sem("x1_kept"), 1)

            def select(b):
                pool.wait_ge(sem("hit"), 3 * b + 3)
                pool.wait_ge(sem("indices"), b)
                G = NQ * HEADS
                n = [0]

                def link(ins):
                    n[0] += 1
                    ins.then_inc(sem("sel_chain"), 1)
                    pool.wait_ge(sem("sel_chain"), SEL * b + n[0])

                for g in range(2):
                    link(pool.tensor_tensor(hit2, hit[g], topf[:, g].unsqueeze(2).to_broadcast([P, G, 8, 8]), ALU.mult))
                    link(pool.tensor_tensor(hit[g][:, :, :, 0:4], hit2[:, :, :, 0:4], hit2[:, :, :, 4:8], ALU.add))
                    link(pool.tensor_tensor(hit2[:, :, :, 0:2], hit[g][:, :, :, 0:2], hit[g][:, :, :, 2:4], ALU.add))
                    link(pool.tensor_tensor(pick[g].rearrange("p (g k) -> p g k", k=8), hit2[:, :, :, 0], hit2[:, :, :, 1], ALU.add))
                pool.sem_inc(sem("picks"), 1)

            SEL = 8
            with pool.Fori(0, NB - 1) as b:
                keep(b)
                select(b)
            keep(NB - 1)
            pool.wait_ge(sem("e_max"), 1)
            pool.partition_all_reduce(col(mxr + DN, 2), col(mx + DN, 2), P, MAX).then_inc(sem("e_red"), 1)
            pool.wait_ge(sem("e_red"), 1)
            pool.tensor_copy(col(mxr + UP), col(mxr + DN)).then_inc(sem("e_maxed"), 1)
            select(NB - 1)
            pool.wait_ge(sem("picks"), NB)
            pool.wait_ge(sem("x1_kept"), NB)
            pool.memset(col(60), 0.0).then_inc(sem("first_done"), 1)
            pool.wait_ge(sem("first_done"), 4)

            def differ_b(b, h, c):
                if c == 0:
                    pool.wait_ge(sem(f"tab_in{h}"), 16 * b + 16)
                if not (isinstance(b, int) and b == 0 and h == 0 and c < 2):
                    pool.wait_ge(sem("p_full"), 4 * (8 * b + 4 * h + c - 1))
                pool.tensor_tensor(b_sb[:, c % 2], iota[:, :].unsqueeze(1).to_broadcast([P, 16, P]),
                                   tab_sb[:, h, 1, 16 * c:16 * c + 16].unsqueeze(2).to_broadcast([P, 16, P]),
                                   ALU.subtract).then_inc(sem("b_differ"), 1)

            for n in range(8):
                differ_b(0, n // 4, n % 4)
            with pool.Fori(1, NB) as b:
                for n in range(8):
                    differ_b(b, n // 4, n % 4)


def kernel(L0_attn_out, L0_attn_W_write, L0_attn_W_read, L0_attn_decay, L0_attn_log_alpha, L0_ffn_Wq,
           L0_ffn_keys, L0_ffn_down_embed, L0_ffn_up_embed, L0_ffn_Wg, L0_ffn_Wu, L0_ffn_Wd):
    import numpy as np
    import concourse.bacc as bacc
    from concourse import mybir as mb
    from concourse.bass_utils import run_bass_kernel_spmd

    def rows128(w):
        w = np.asarray(w)
        return np.ascontiguousarray(w.reshape(-1, 128, w.shape[1]).transpose(1, 0, 2).reshape(128, -1))

    def one(v):
        return np.ascontiguousarray(np.broadcast_to(np.asarray(v).reshape(1, 1), (128, 1)))

    lane, tok = np.arange(128)[:, None], np.arange(T)[None, :]
    ins = [
        ("x", np.ascontiguousarray(L0_attn_out)),
        ("wwrite", np.ascontiguousarray(L0_attn_W_write)),
        ("wreadT", np.ascontiguousarray(np.asarray(L0_attn_W_read).T)),
        ("decay", one(L0_attn_decay)),
        ("log_alpha", one(L0_attn_log_alpha)),
        ("wq", np.ascontiguousarray(L0_ffn_Wq)),
        ("keys", np.ascontiguousarray(np.asarray(L0_ffn_keys).transpose(3, 2, 0, 1).reshape(HALF, 8, NK))),
        ("emb", np.ascontiguousarray(np.concatenate([rows128(np.asarray(L0_ffn_down_embed).T), rows128(L0_ffn_up_embed)], axis=1))),
        ("wg", rows128(np.asarray(L0_ffn_Wg).T)),
        ("wu", rows128(np.asarray(L0_ffn_Wu).T)),
        ("wd", rows128(np.asarray(L0_ffn_Wd).T)),
        ("ident", np.eye(128, dtype=np.float32)),
        ("diffs", np.maximum(tok - 1 - lane, 0).astype(np.float32)),
        ("causal", (tok > lane).astype(np.float32)),
        ("iota", np.ascontiguousarray(np.broadcast_to(np.arange(128), (128, 128))).astype(np.float16)),
        ("rank", np.ascontiguousarray(np.broadcast_to(np.arange(8), (128, 8))).astype(np.float32)),
        ("qmask", (lane // PAIRS == np.arange(NQ)[None, :]).astype(np.float32)),
    ]
    nc = bacc.Bacc("TRN2", target_bir_lowering=False, num_devices=1)
    arrays, args = {}, []
    for name, arr in ins:
        arrays[f"in_{name}"] = arr
        args.append(nc.dram_tensor(f"in_{name}", arr.shape, mb.dt.from_np(arr.dtype), kind="ExternalInput").ap())
    args.append(nc.dram_tensor("x2_parts", [NB, P, 2, KC, T], F16, kind="Internal").ap())
    args.append(nc.dram_tensor("pick_tables", [NB, 2, P, 4, TQ], F16, kind="Internal").ap())
    args.append(nc.dram_tensor("x1_rows", [NB, T, D], F32, kind="Internal").ap())
    args.append(nc.dram_tensor("out_0", [NB, T, D], F32, kind="ExternalOutput").ap())
    dense_kernel(nc, *args)
    r = run_bass_kernel_spmd(nc, [arrays], core_ids=[0])
    return r.results[0]["out_0"]
```

```python
from contextlib import ExitStack

import concourse.bass as bass
from concourse import mybir

ALU = mybir.AluOpType
ACT = mybir.ActivationFunctionType
F32, F16, I32, U32 = mybir.dt.float32, mybir.dt.float16, mybir.dt.int32, mybir.dt.uint32
AX_X = mybir.AxisListType.X

P = 128
NB, T, D = 8, 512, 256
NQ = T // P
KC = D // P
INTER, NIC = 1024, 1024 // P
HEADS, NK, TOPK, HALF = 4, 128, 8, 64
PAIRS = HEADS * TOPK
NE = 4096
NI = NE // P
TH = T // 2
TQ = TH // NQ
EPS = 1e-5

X_SCALE = 2.0 ** 10
W_SCALE = 2.0 ** 14
P_SCALE = 2.0 ** 12
ROWS, SCORES, READS, ROWS2 = 1, 4, 5, 6
RSQRT_SEED = 0x5F3759DF
EXPONENT = 0x7F800000
PIECE = 1024
NPIECE = 2 * KC * NE // PIECE
TABLE_AT = 8
RANKS_BEFORE = 6
MAX_SEQ = (1, 5)
SPLITS = {5: range(0, NPIECE // 2), 6: range(NPIECE // 2, NPIECE)}
LOOK = 2 * KC * NE // (MAX_SEQ[1] - MAX_SEQ[0])
HALVES = ((0, 0), (0, 1), (1, 0))


def dense_kernel(nc, x, wwrite, wreadT, decay, log_alpha, wq, keys, emb, wg, wu, wd,
                 ident_d, diffs_d, causal_d, iota_d, rank_d, qmask_d, x2_d, tab_d, x1_d, out):
    ctx = ExitStack()
    with ctx:
        ARENA = 36520
        X1_AT = NQ * D + KC * (T + 2) + NQ * D + NQ * T - P * 6 + T + KC * D
        SECOND = X1_AT + NQ * D + 16 * P + 2 * NI * TH + 5 * 4 * D
        arena = ctx.enter_context(nc.sbuf_tensor("arena", [P, ARENA], F32))
        embs = ctx.enter_context(nc.sbuf_tensor("embs", [P, 2 * KC * NE], F32))
        ident = ctx.enter_context(nc.sbuf_tensor("ident", [P, P], F32))
        iota = ctx.enter_context(nc.sbuf_tensor("iota", [P, P], F16))
        rank = ctx.enter_context(nc.sbuf_tensor("rank", [P, TOPK], F32))
        qmask = ctx.enter_context(nc.sbuf_tensor("qmask", [P, NQ], F32))
        scal = ctx.enter_context(nc.sbuf_tensor("scal", [P, 64], F32))
        bank = [ctx.enter_context(nc.psum_tensor(f"bank{i}", [P, 512], F32)) for i in range(8)]

        sems = {}

        def sem(name):
            if name not in sems:
                sems[name] = ctx.enter_context(nc.semaphore(name))
            return sems[name]

        class Region:

            def __init__(self, whole, start=0):
                self.whole, self.at = whole, start

            def take(self, n, dt=F32):
                words = n if dt in (F32, I32, U32) else n // 2
                v = self.whole[:, self.at:self.at + words]
                self.at += words
                assert self.at <= self.whole.shape[1], self.at
                return v if dt == F32 else v.bitcast(dt)

        raw_emb = embs[:, :]
        parts = embs[:, :].bitcast(F16).rearrange("p (m s c) -> p m s c", m=NPIECE, s=2)

        def down_w(s, k, i):
            n = PIECE // P
            return parts[:, k * (NPIECE // 4) + i // n, s, (i % n) * P:(i % n + 1) * P]

        def up_w(s, i):
            n = PIECE // D
            return parts[:, NPIECE // 2 + i // n, s, (i % n) * D:(i % n + 1) * D]

        e = Region(embs)
        raw_gu = e.take(2 * KC * INTER)
        raw_wd = e.take(NIC * D)
        kf32 = e.take(KC * 2 * HEADS * NK)
        wq_sb = e.take(8 * D)[0:HALF].rearrange("p (g d) -> p g d", g=8)
        keys_sb = e.take(8 * NK)[0:HALF].rearrange("p (g k) -> p g k", g=8)
        ww_sb = e.take(KC * D).rearrange("p (k d) -> p k d", k=KC)
        wr_sb = e.take(KC * D).rearrange("p (k d) -> p k d", k=KC)
        diffs = e.take(T)
        causal = e.take(T)

        a = Region(arena)
        xin = a.take(NQ * D).rearrange("p (q d) -> p q d", q=NQ)
        xT = a.take(KC * (T + 2)).rearrange("p (k t) -> p k t", k=KC)
        v_sb = a.take(NQ * D).rearrange("p (q d) -> p q d", q=NQ)
        x2n = v_sb
        xhat = arena[:, a.at:a.at + NQ * D].rearrange("p (q d) -> p q d", q=NQ)
        att = [a.take(T - P * s) for s in range(NQ)]
        decay_tab = a.take(T)
        wc = a.take(KC * D).rearrange("p (k d) -> p k d", k=KC)
        x1 = a.take(NQ * D).rearrange("p (q d) -> p q d", q=NQ)
        kf_s = a.take(2 * KC * 2 * HEADS * NK, F16).rearrange("p (s k n) -> p s k n", s=2, k=KC)
        wgu_s = a.take(4 * KC * INTER, F16).rearrange("p (s g k n) -> p s g k n", s=2, g=2, k=KC)
        sim = a.take(NQ * 8 * NK).rearrange("p (q g k) -> p q g k", q=NQ, g=8)
        wd_s = a.take(2 * NIC * D, F16).rearrange("p (s c d) -> p s c d", s=2, c=NIC)
        x1k = a.take(NQ * D).rearrange("p (q d) -> p q d", q=NQ)
        x2s = a.take(2 * KC * T, F16).rearrange("p (s k t) -> p s k t", s=2, k=KC)
        h_s = a.take(2 * NIC * T, F16).rearrange("p (s c t) -> p s c t", s=2, c=NIC)
        gate = a.take(2 * T).rearrange("p (n t) -> p n t", n=2)
        h32 = a.take(2 * T).rearrange("p (n t) -> p n t", n=2)
        scaled = a.take(2 * PIECE).rearrange("p (n c) -> p n c", n=2)
        stats = a.take(NQ * 6).rearrange("p (q n) -> p q n", q=NQ)
        mv = a.take(NQ * 2).rearrange("p (q n) -> p q n", q=NQ)
        ve, nh, r0, r1, r2 = (a.take(NQ) for _ in range(5))
        a.at = max(a.at, SECOND)
        x1m = a.take(NQ * D).rearrange("p (q d) -> p q d", q=NQ)
        top = a.take(2 * NQ * HEADS * TOPK).rearrange("p (g q h k) -> p g q h k", g=2, q=NQ, h=HEADS)
        topi = a.take(2 * NQ * HEADS * TOPK, U32).rearrange("p (g q h k) -> p g q h k", g=2, q=NQ, h=HEADS)
        comb = a.take(HEADS * 64).rearrange("p (h a b) -> p h a b", h=HEADS, a=TOPK)
        best = a.take(NQ * PAIRS).rearrange("p (q h k) -> p q h k", q=NQ, h=HEADS)
        besti = a.take(NQ * PAIRS, U32)
        rank_of = [a.take(NQ * PAIRS, U32) for _ in range(2)]
        topf = a.take(2 * NQ * HEADS * TOPK).rearrange("p (g c r) -> p g c r", g=2, r=8)
        hit = [a.take(NQ * PAIRS * 8).rearrange("p (g k r) -> p g k r", k=8, r=8) for _ in range(2)]
        hit2 = a.take(NQ * PAIRS * 8).rearrange("p (g k r) -> p g k r", k=8, r=8)
        pick = [v.bitcast(F32) for v in rank_of]
        past = a.take(NQ * PAIRS)
        esub = a.take(NQ * PAIRS)
        esum = a.take(NQ * HEADS)
        table = a.take(3 * NQ * PAIRS).rearrange("p (n c) -> p n c", n=3)
        tab16 = a.take(4 * P, F16).rearrange("p (h n t) -> p n h t", h=2, n=4)

        c = Region(arena)
        a_sb = c.take(2 * 2 * 16 * NQ * NI, F16).rearrange("p (n s t q i) -> p n s t q i", n=2, s=2, t=16, q=NQ)
        x2_sb = c.take(2 * 2 * KC * TH, F16).rearrange("p (n s k t) -> p n s k t", n=2, s=2, k=KC)
        tab_sb = c.take(2 * 4 * TQ, F16).rearrange("p (n m t) -> p n m t", n=2, m=4)
        assert c.at <= X1_AT
        c.at = X1_AT
        hit_i = c.take(16 * NI, F16).rearrange("p (t i) -> p t i", t=16)
        hit_p = c.take(2 * 16 * NI, F16).rearrange("p (s t i) -> p s t i", s=2, t=16)
        c.at = X1_AT + NQ * D
        b_sb = c.take(2 * 16 * P, F16).rearrange("p (n t j) -> p n t j", n=2, t=16)
        p_sb = c.take(2 * NI * TH).rearrange("p (n i q t) -> p n i q t", n=2, i=NI, q=NQ)
        silu_z = c.take(2 * 2 * TH).rearrange("p (n t) -> p n t", n=2)
        g32 = c.take(2 * 2 * TH).rearrange("p (n t) -> p n t", n=2)
        g_s = c.take(2 * 2 * 2 * TH, F16).rearrange("p (n s i t) -> p n s i t", n=2, s=2, i=2)
        res = c.take(2 * 2 * D).rearrange("p (n u d) -> p n u d", n=2, u=2)
        fin = c.take(2 * 2 * D).rearrange("p (n u d) -> p n u d", n=2, u=2)
        assert c.at == SECOND

        def col(n, k=1):
            return scal[:, n:n + k]

        KF, WG, WU, WD_, DN, UP = range(6)
        mx, mxr, pw, rp, ws = (8 * n for n in range(5))
        SIM_OUT, GATE_IN, H_SCALE, MLP_OUT, Z_IN, PROB, EXP_OUT = range(40, 47)
        DEC, LA, NEG, POS, NAB, EXPN, LNN, LOGG, ALPHA = range(48, 57)

        def weight_parts(m):
            return (kf_s[:, m].rearrange("p k n -> p (k n)"), wgu_s[:, m, 0].rearrange("p k n -> p (k n)"),
                    wgu_s[:, m, 1].rearrange("p k n -> p (k n)"), wd_s[:, m].rearrange("p c d -> p (c d)"))

        def after(b, h, n):
            return b + (h + n) // 2, (h + n) % 2

        x_q = x.rearrange("b (q t) d -> b t q d", t=P)
        x1_q = x1_d.rearrange("b (q t) d -> b t q d", t=P)

        def at(v, b):
            return v[bass.ds(b, 1)]

        block = ctx.enter_context(nc.Block())

        @block.sync
        def _(sp):
            def load_x(b):
                sp.dma_start(xin, at(x_q, b).rearrange("o t q d -> (o t) q d")).then_inc(sem("x_in"), 16)

            load_x(0)
            for dst, src in ((ident[:, :], ident_d), (ww_sb, wwrite.rearrange("(k p) d -> p k d", p=P)),
                             (wr_sb, wreadT.rearrange("(k p) d -> p k d", p=P)), (diffs, diffs_d), (causal, causal_d),
                             (col(DEC), decay), (col(LA), log_alpha), (iota[:, :], iota_d), (rank[:, :], rank_d),
                             (qmask[:, :], qmask_d)):
                sp.dma_start(dst, src).then_inc(sem("const_in"), 16)
            sp.dma_start(wq_sb, wq.rearrange("(g n) d -> n g d", n=HALF)).then_inc(sem("wq_in"), 16)
            sp.dma_start(keys_sb, keys).then_inc(sem("wq_in"), 16)
            sp.dma_start(raw_gu[:, 0:KC * INTER], wg).then_inc(sem("mlp_in"), 16)
            sp.dma_start(raw_gu[:, KC * INTER:2 * KC * INTER], wu).then_inc(sem("mlp_in"), 16)
            sp.dma_start(raw_wd, wd).then_inc(sem("mlp_in"), 16)

            def prefetch(b):
                sp.wait_ge(sem("xin_used"), b + 1)
                load_x(b + 1)

            def store_x2(b):
                for n in range(2):
                    sp.wait_ge(sem(f"att_free{n}"), 6 * b + ROWS2)
                sp.dma_start(x2_d[bass.ds(b, 1)].rearrange("o p s k t -> (o p) s k t"), x2s).then_inc(sem("x2_out"), 16)

            def store_rows(b):
                sp.wait_ge(sem("sim_free0"), 6 * b + 6)
                sp.wait_ge(sem("sim_free1"), 5 * b + 5)
                sp.dma_start(at(x1_q, b).rearrange("o t q d -> (o t) q d"), x1m).then_inc(sem("x1_out"), 16)

            def store_table(b):
                sp.wait_ge(sem("tab_ij"), b + 1)
                sp.wait_ge(sem("tab_lo"), b + 1)
                for h in range(2):
                    sp.dma_start(tab_d[bass.ds(b, 1), h].rearrange("o p n t -> (o p) n t"),
                                 tab16[:, :, h]).then_inc(sem("tab_out"), 16)

            prefetch(0)
            store_x2(0)
            def sequence(b, first=False, last=False):
                if not first:
                    store_table(b - 1)
                if not last:
                    prefetch(b + 1)
                store_x2(b + 1)
                store_rows(b)

            sp.wait_ge(sem("mlp_lo"), 3)
            sp.wait_ge(sem("kf_lo"), 1)
            sp.wait_ge(sem("decay_tab"), 1)
            sp.wait_ge(sem("wc"), 1)
            for n in range(4):
                sp.dma_start(raw_emb[:, n * LOOK:(n + 1) * LOOK], emb[:, n * LOOK:(n + 1) * LOOK]).then_inc(sem("emb_in"), 16)
            sequence(0, first=True)
            with sp.Fori(1, NB - 2) as b:
                sequence(b)
            sequence(NB - 2, last=True)

            sp.wait_ge(sem("t2_full"), 2 * NB)
            for n in range(2):
                sp.wait_ge(sem(f"att_free{n}"), 6 * NB)
            sp.wait_ge(sem("x2_out"), 16 * NB)
            sp.wait_ge(sem("tab_out"), 2 * 16 * (NB - 2))

            def load_tile(b, h):
                src = x2_d[bass.ds(b, 1)].rearrange("o p s k (q t) -> (o p) (s k q) t", q=NQ)[:, :, h * TQ:(h + 1) * TQ]
                sp.dma_start(x2_sb[:, h].rearrange("p s k (q t) -> p (s k q) t", q=NQ), src).then_inc(sem(f"x2_in{h}"), 16)

            def load_tab(b, h):
                sp.dma_start(tab_sb[:, h], tab_d[bass.ds(b, 1), h].rearrange("o p n t -> (o p) n t")).then_inc(sem(f"tab_in{h}"), 16)

            def rows(v, b, h, q):
                return v[bass.ds(b, 1), q * P + h * TQ:q * P + (h + 1) * TQ].rearrange("o t d -> (o t) d")

            def load_res(b, h):
                for q in range(NQ):
                    sp.dma_start(res[(q % 2) * TQ:(q % 2 + 1) * TQ, h, q // 2], rows(x1_d, b, h, q)).then_inc(sem(f"res_in{h}"), 16)

            def store(b, h):
                sp.wait_ge(sem("fin"), 4 * b + 2 * h + 2)
                for q in range(NQ):
                    sp.dma_start(rows(out, b, h, q), fin[(q % 2) * TQ:(q % 2 + 1) * TQ, h, q // 2]).then_inc(sem(f"stored{h}"), 16)

            for h in range(2):
                load_tab(0, h)
                load_tile(0, h)
            store_table(NB - 2)
            store_rows(NB - 1)
            sp.wait_ge(sem("x1_out"), 16 * NB)
            sp.wait_ge(sem("down_full"), 2 * NB)
            sp.wait_ge(sem("emb_lo"), NPIECE)
            for h in range(2):
                load_res(0, h)
            store_table(NB - 1)
            sp.wait_ge(sem("tab_out"), 2 * 16 * NB)
            with sp.Fori(0, NB - 1) as b:
                sp.wait_ge(sem("a_built"), 8 * b + 4)
                sp.wait_ge(sem("b_built"), 8 * b + 4)
                load_tab(b + 1, 0)
                sp.wait_ge(sem("z"), 32 * b + 16)
                load_tile(b + 1, 0)
                sp.wait_ge(sem("a_built"), 8 * b + 8)
                sp.wait_ge(sem("b_built"), 8 * b + 8)
                load_tab(b + 1, 1)
                store(b, 0)
                load_res(b + 1, 0)
                sp.wait_ge(sem("z"), 32 * b + 32)
                load_tile(b + 1, 1)
                store(b, 1)
                load_res(b + 1, 1)
            store(NB - 1, 0)
            store(NB - 1, 1)
            for h in range(2):
                sp.wait_ge(sem(f"stored{h}"), 16 * NQ * NB)

        @block.tensor
        def _(pe):
            pe.wait_ge(sem("const_in"), 160)
            for ec in range(KC):
                for k in range(KC):
                    last = pe.matmul(bank[0][:, ec * D:(ec + 1) * D], ww_sb[:, k, ec * P:(ec + 1) * P], wr_sb[:, k, :],
                                     start=(k == 0), stop=(k == KC - 1))
            last.then_inc(sem("wc_full"), 1)
            pe.wait_ge(sem("wq_in"), 32)
            for dc in range(KC):
                for g in range(8):
                    last = pe.matmul(bank[4 + 2 * dc + g // 4][:, (g % 4) * NK:(g % 4 + 1) * NK],
                                     wq_sb[:, g, dc * P:(dc + 1) * P], keys_sb[:, g, :], start=True, stop=True)
            last.then_inc(sem("kf_full"), 1)

            def bank_free(n, b, k):
                pe.wait_ge(sem(f"att_free{n}"), 6 * b + k)

            def transpose_rows(src, b, k, ready, full):
                pe.wait_ge(sem(ready), b + 1)
                for kc in range(KC):
                    bank_free(kc, b, k)
                    for q in range(NQ):
                        last = pe.transpose(bank[kc][:, q * P:(q + 1) * P], src[:, q, kc * P:(kc + 1) * P], ident[:, :])
                    last.then_inc(sem(full), 1)

            def t1(b):
                transpose_rows(xhat, b, 0, "xhat", "t1_full")

            def values_scores(b):
                for n in range(2):
                    pe.wait_ge(sem(f"att_free{n}"), 6 * b + ROWS)
                pe.wait_ge(sem("wc"), 1)
                for n in range(2):
                    bank_free(n, b, 1)
                    for q in (2 * n, 2 * n + 1):
                        for k in range(KC):
                            last = pe.matmul(bank[n][:, (q % 2) * D:(q % 2 + 1) * D], xT[:, k, 1 + q * P:1 + (q + 1) * P],
                                             wc[:, k, :], start=(k == 0), stop=(k == KC - 1))
                    last.then_inc(sem("v_full"), 1)
                for s in range(NQ):
                    bank_free(s % 2, b, 2 + s // 2)
                    for k in range(KC):
                        last = pe.matmul(bank[s % 2][:, 0:T - P * s], xT[:, k, s * P:(s + 1) * P], xT[:, k, 1 + s * P:1 + T],
                                         start=(k == 0), stop=(k == KC - 1))
                    last.then_inc(sem("s_full"), 1)

            def reads(b):
                for n in range(2):
                    pe.wait_ge(sem(f"att_free{n}"), 6 * b + SCORES)
                for n in range(2):
                    bank_free(n, b, 4)
                    for q in (2 * n, 2 * n + 1):
                        for s in range(q + 1):
                            last = pe.matmul(bank[n][:, (q % 2) * D:(q % 2 + 1) * D], att[s][:, (q - s) * P:(q - s + 1) * P],
                                             v_sb[:, s, :], start=(s == 0), stop=(s == q))
                    last.then_inc(sem("r_full"), 1)

            def t2(b):
                transpose_rows(x2n, b, 5, "x2n", "t2_full")

            def similarities(b):
                for n in range(2):
                    pe.wait_ge(sem(f"att_free{n}"), 6 * b + ROWS2)
                for q in range(NQ):
                    for n in range(2):
                        pe.wait_ge(sem(f"sim_free{n}"), (6 - n) * b + q)
                        last = three(bank[2 + n][:, :], lambda s, k: x2s[:, s, k, q * P:(q + 1) * P],
                                     lambda s, k: kf_s[:, s, k, n * 512:(n + 1) * 512])
                        last.then_inc(sem("sim_full"), 1)

            def three(dst, stat, mov, ks=KC, each=None):
                n = 0
                for k in range(ks):
                    if each:
                        each(k)
                    for s, m in HALVES:
                        last = pe.matmul(dst, stat(s, k), mov(m, k), start=(n == 0), stop=(n == 3 * ks - 1))
                        n += 1
                return last

            def mlp_up(b, c):
                pe.wait_ge(sem(f"mlp_free{c % 2}"), 4 * b + c // 2)
                for g in range(2):
                    last = three(bank[4 + 2 * (c % 2) + g][:, :], lambda s, k: wgu_s[:, s, g, k, c * P:(c + 1) * P],
                                 lambda s, k: x2s[:, s, k])
                last.then_inc(sem("gu_full"), 1)

            def mlp_down(b):
                for n in range(2):
                    pe.wait_ge(sem(f"sim_free{n}"), (6 - n) * b + 5 - n)
                    for q in (2 * n, 2 * n + 1):
                        last = three(bank[2 + n][:, (q % 2) * D:(q % 2 + 1) * D],
                                     lambda s, k: h_s[:, s, k, q * P:(q + 1) * P],
                                     lambda s, k: wd_s[:, s, k, :], ks=NIC,
                                     each=(lambda k: pe.wait_ge(sem("h_lo"), NIC * b + k + 1)) if q == 0 else None)
                    last.then_inc(sem("down_full"), 1)

            def table_t(b, n, bank_sem, uses):
                pe.wait_ge(sem("indices"), b + 1)
                pe.wait_ge(sem("probs"), b + 1)
                pe.wait_ge(sem(bank_sem), uses)
                for m in range(3):
                    last = pe.transpose(bank[n][:, m * P:(m + 1) * P], table[:, m, :], ident[:, :])
                last.then_inc(sem("tab_full"), 1)

            def z(b, h, s):
                pe.wait_ge(sem(f"z_free{s % 2}"), 16 * b + 8 * h + s // 2)
                if s == 0:
                    pe.wait_ge(sem(f"x2_in{h}"), 16 * b + 16)
                for i in range(2):
                    last = three(bank[2 + s % 2][:, i * TH:(i + 1) * TH], lambda m, k: down_w(m, k, 2 * s + i),
                                 lambda m, k: x2_sb[:, h, m, k, :])
                last.then_inc(sem("z"), 1)

            def scatter(b, h, s):
                c = s // 4
                n = s % 2
                if s % 4 == 0:
                    pe.wait_ge(sem("a_built"), 8 * b + 4 * h + c + 1)
                    pe.wait_ge(sem("b_built"), 8 * b + 4 * h + c + 1)
                pe.wait_ge(sem(f"p_free{s % 2}"), 16 * b + 8 * h + s // 2)
                for t in range(4):
                    for m in range(2):
                        last = pe.matmul(bank[n][:, t * P:(t + 1) * P], b_sb[:, c % 2, 4 * (s % 4) + t, :],
                                         a_sb[:, c % 2, m, 4 * (s % 4) + t].rearrange("p q i -> p (q i)"),
                                         start=(m == 0), stop=(m == 1))
                last.then_inc(sem("p_full"), 1)

            def up(b, h, s):
                pe.wait_ge(sem("g_lo"), 32 * b + 16 * h + s + 1)
                if s == 0:
                    pe.wait_ge(sem(f"sum_free{h}"), 2 * b)
                for i in range(2):
                    for u in range(2):
                        for m, w in HALVES:
                            last = pe.matmul(bank[4 + 2 * h + u][:, 0:D], g_s[:, s % 2, m, i, u * P:(u + 1) * P],
                                             up_w(w, 2 * s + i), start=(s == 0 and i == 0 and (m, w) == (0, 0)),
                                             stop=(s == NI // 2 - 1 and i == 1 and (m, w) == HALVES[-1]))
                last.then_inc(sem("up"), 1)

            pe.wait_ge(sem("wc"), 1)
            t1(0)
            values_scores(0)
            reads(0)
            t2(0)
            pe.wait_ge(sem("kf_lo"), 1)

            def sequence(b, first=False, last=False):
                similarities(b)
                if first:
                    pe.wait_ge(sem("mlp_lo"), 3)
                mlp_up(b, 0)
                if not last:
                    t1(b + 1)
                mlp_up(b, 1)
                if not first:
                    table_t(b - 1, 2, "sim_free0", 6 * b + NQ)
                if not last:
                    values_scores(b + 1)
                mlp_up(b, 2)
                if not last:
                    reads(b + 1)
                for c in range(3, NIC):
                    mlp_up(b, c)
                if not last:
                    t2(b + 1)
                else:
                    for n in range(2):
                        pe.wait_ge(sem(f"att_free{n}"), 6 * NB)
                    for g in range(8):
                        scatter(0, 0, g)
                mlp_down(b)

            def tile(b, h, rest, table_at=None):
                for s in range(16):
                    n, m = divmod(s + 2, 16)
                    if n <= rest:
                        z(*after(b, h, n), m)
                    if n + 1 <= rest:
                        scatter(*after(b, h, n + 1), m)
                    up(b, h, s)
                    if table_at == s:
                        table_t(NB - 1, 6, "mlp_free1", 4 * NB)
                if table_at is not None:
                    pe.wait_ge(sem("tab_ij"), NB)
                    pe.wait_ge(sem("tab_lo"), NB)

            sequence(0, first=True)
            with pe.Fori(1, NB - 1) as b:
                sequence(b)
            sequence(NB - 1, last=True)
            for s in range(8, 16):
                scatter(0, 0, s)
            pe.wait_ge(sem("sim_free0"), 6 * NB)
            pe.wait_ge(sem("sim_free1"), 5 * NB)
            pe.wait_ge(sem("emb_lo"), NPIECE)
            z(0, 0, 0)
            z(0, 0, 1)
            scatter(0, 1, 0)
            scatter(0, 1, 1)
            for n in range(2):
                pe.wait_ge(sem(f"mlp_free{n}"), 4 * NB)
            tile(0, 0, 2, table_at=TABLE_AT)
            tile(0, 1, 2)
            with pe.Fori(1, NB - 1) as b:
                tile(b, 0, 2)
                tile(b, 1, 2)
            tile(NB - 1, 0, 1)
            tile(NB - 1, 1, 0)

        @block.scalar
        def _(act):
            def copy(dst, src, scale=1.0):
                return act.activation(dst, src, ACT.Copy, scale=scale)

            act.wait_ge(sem("scal_chain"), 3)
            act.activation(col(EXPN), col(NAB), ACT.Exp).then_inc(sem("act_scal"), 1)
            act.wait_ge(sem("act_scal"), 1)
            act.activation(col(LNN), col(EXPN), ACT.Ln, bias=1.0).then_inc(sem("act_scal"), 1)
            act.activation(col(ALPHA), col(LA), ACT.Exp).then_inc(sem("act_scal"), 1)
            act.wait_ge(sem("act_scal"), 3)
            act.wait_ge(sem("wc_full"), 1)
            copy(wc.rearrange("p k d -> p (k d)"), bank[0][:, :], col(ALPHA)).then_inc(sem("wc"), 1)
            act.wait_ge(sem("scal_chain"), 4)
            act.activation(decay_tab, diffs, ACT.Exp, scale=col(LOGG)).then_inc(sem("act_scal"), 1)

            def normalise(dst, src, b, ready, done):
                act.wait_ge(sem(ready), b + 1)
                act.wait_ge(sem("r_full"), 2 * b + (2 if done == "x2n" else 0))
                act.sem_inc(sem("act_steps"), 1)
                for q in range(NQ):
                    last = act.activation(dst[:, q], src[:, q], ACT.Identity, bias=r0[:, q:q + 1], scale=r2[:, q:q + 1])
                last.then_inc(sem(done), 1)

            def xT_out(b):
                for k in range(KC):
                    act.wait_ge(sem("t1_full"), 2 * b + k + 1)
                    copy(xT[:, k, 1:1 + T], bank[k][:, :]).then_inc(sem(f"att_free{k}"), 1)

            def v_out(b):
                for n in range(2):
                    act.wait_ge(sem("v_full"), 2 * b + n + 1)
                    copy(v_sb[:, 2 * n:2 * n + 2].rearrange("p q d -> p (q d)"), bank[n][:, :]).then_inc(sem(f"att_free{n}"), 1)

            def x2_hi(b):
                act.wait_ge(sem("x2_out"), 16 * b)
                for k in range(KC):
                    act.wait_ge(sem("t2_full"), 2 * b + k + 1)
                    act.activation(x2s[:, 0, k], bank[k][:, :], ACT.Copy, scale=X_SCALE).then_inc(sem("x2_hi"), 1)

            def sim_out(b, q):
                for n in range(2):
                    act.wait_ge(sem("sim_full"), 8 * b + 2 * q + n + 1)
                    if n == 0 and q == 0:
                        act.wait_ge(sem("topped"), NQ * b)
                    copy(sim[:, q, 4 * n:4 * n + 4].rearrange("p g k -> p (g k)"), bank[2 + n][:, :],
                         col(SIM_OUT)).then_inc(sem(f"sim_free{n}"), 1)

            def silu_gate(b, c):
                act.wait_ge(sem("gu_full"), NIC * b + c + 1)
                act.wait_ge(sem(f"mlp_free{c % 2}"), 4 * b + c // 2)
                act.activation(gate[:, c % 2], bank[4 + 2 * (c % 2)][:, :], ACT.Silu, scale=col(GATE_IN)).then_inc(sem("gate"), 1)

            def h_hi(b, c):
                act.wait_ge(sem(f"mlp_free{c % 2}"), 4 * b + c // 2 + 1)
                act.wait_ge(sem("down_full"), 2 * b)
                copy(h_s[:, 0, c], h32[:, c % 2]).then_inc(sem("h_hi"), 1)

            def exp_scores(b):
                act.wait_ge(sem("esub"), b + 1)
                act.activation(esub, esub, ACT.Exp).then_inc(sem("exped"), 1)

            def tab_hi(b, n):
                act.wait_ge(sem("tab_full"), b + 1)
                act.wait_ge(sem("tab_out"), 32 * b)
                act.activation(tab16[:, 0:2], bank[n][:, 0:2 * P].rearrange("p (n h t) -> p n h t", n=2, h=2),
                               ACT.Copy).then_inc(sem("tab_ij"), 1)
                act.activation(tab16[:, 2], bank[n][:, 2 * P:3 * P].rearrange("p (h t) -> p h t", h=2),
                               ACT.Copy, scale=P_SCALE).then_inc(sem("tab_hi"), 1)

            normalise(xhat, xin, 0, "ln1", "xhat")
            act.wait_ge(sem("kf_full"), 1)
            for k in range(4):
                copy(kf32[:, k * 512:(k + 1) * 512], bank[4 + k][:, :]).then_inc(sem("kf32"), 1)
            xT_out(0)
            v_out(0)
            act.wait_ge(sem("w_scales"), 1)
            act.wait_ge(sem("kf32"), 4)
            kp, gp, up_, dp = weight_parts(0)
            copy(kp, kf32, col(ws + KF)).then_inc(sem("w_hi"), 1)
            copy(gp, raw_gu[:, 0:KC * INTER], col(ws + WG)).then_inc(sem("w_hi"), 1)
            copy(up_, raw_gu[:, KC * INTER:], col(ws + WU)).then_inc(sem("u_hi"), 1)
            act.wait_ge(sem("u_hi"), 1)
            copy(raw_gu[:, KC * INTER:], raw_gu[:, KC * INTER:], col(ws + WU)).then_inc(sem("u_hi"), 1)
            normalise(x2n, x1, 0, "ln2", "x2n")
            x2_hi(0)
            copy(dp, raw_wd, col(ws + WD_)).then_inc(sem("d_hi"), 1)
            act.wait_ge(sem("d_hi"), 1)
            copy(raw_wd, raw_wd, col(ws + WD_)).then_inc(sem("d_hi"), 1)

            def sequence(b, first=False, last=False):
                pieces = list(SPLITS.get(b, ())) if isinstance(b, int) else []
                if not first:
                    exp_scores(b - 1)
                for q in range(NQ):
                    sim_out(b, q)
                if not last:
                    normalise(xhat, xin, b + 1, "ln1", "xhat")
                silu_gate(b, 0)
                if not last:
                    xT_out(b + 1)
                silu_gate(b, 1)
                h_hi(b, 0)
                if not first:
                    tab_hi(b - 1, 2)
                if not last:
                    v_out(b + 1)
                for _ in range(4):
                    if pieces:
                        emb_high(pieces.pop(0))
                silu_gate(b, 2)
                h_hi(b, 1)
                for c in range(3, NIC):
                    if pieces and c < 5:
                        emb_high(pieces.pop(0))
                    if c == 7 and not last:
                        normalise(x2n, x1, b + 1, "ln2", "x2n")
                    silu_gate(b, c)
                    h_hi(b, c - 1)
                h_hi(b, NIC - 1)
                if not last:
                    x2_hi(b + 1)
                for m in pieces:
                    emb_high(m)

            def emb_high(m):
                act.wait_ge(sem("e_scales"), 1)
                if m >= 2:
                    act.wait_ge(sem("emb_lo"), m - 1)
                copy(scaled[:, m % 2], raw_emb[:, m * PIECE:(m + 1) * PIECE], col(ws + (DN if m < NPIECE // 2 else UP))).then_inc(sem("scaled"), 1)
                act.wait_ge(sem("scaled"), m + 1)
                copy(parts[:, m, 0], scaled[:, m % 2]).then_inc(sem("emb_hi"), 1)

            def silu_of(b, h, s):
                act.wait_ge(sem("z"), 32 * b + 16 * h + s + 1)
                act.wait_ge(sem(f"s_free{s % 2}"), 16 * b + 8 * h + s // 2)
                act.activation(silu_z[:, s % 2], bank[2 + s % 2][:, :], ACT.Silu, scale=col(Z_IN)).then_inc(sem(f"z_free{s % 2}"), 1)

            def g_hi(b, h, s):
                act.wait_ge(sem(f"s_free{s % 2}"), 16 * b + 8 * h + s // 2 + 1)
                if not (isinstance(b, int) and b == h == s == 0):
                    act.wait_ge(sem("up"), 32 * b + 16 * h + s - 1)
                copy(g_s[:, s % 2, 0].rearrange("p i t -> p (i t)"), g32[:, s % 2]).then_inc(sem("g_hi"), 1)

            def p_out(b, h, s):
                act.wait_ge(sem("p_full"), 32 * b + 16 * h + s + 1)
                if s == 0 and not (isinstance(b, int) and b == h == 0):
                    act.wait_ge(sem("p_used"), 2 * b + h - 1)
                act.activation(p_sb[:, h, :, :, 4 * s:4 * s + 4], bank[s % 2][:, :].rearrange("p (t q i) -> p i q t", t=4, q=NQ),
                               ACT.Copy, scale=col(PROB)).then_inc(sem(f"p_free{s % 2}"), 1)

            def tile(b, h, rest, table_at=None):
                for s in range(16):
                    n, m = divmod(s + 1, 16)
                    if n <= rest:
                        g_hi(*after(b, h, n), m)
                    n, m = divmod(s + 2, 16)
                    if n <= rest:
                        silu_of(*after(b, h, n), m)
                    if n + 1 <= rest:
                        p_out(*after(b, h, n + 1), m)
                    if table_at == s + 1:
                        exp_scores(NB - 1)
                    if table_at == s:
                        tab_hi(NB - 1, 6)

            sequence(0, first=True)
            with act.Fori(1, MAX_SEQ[1]) as b:
                sequence(b)
            for b in range(MAX_SEQ[1], NB):
                sequence(b, last=(b == NB - 1))
            act.wait_ge(sem("gu_full"), NIC * NB)
            act.wait_ge(sem("topped"), NQ * NB)
            for s in range(16):
                p_out(0, 0, s)
            act.wait_ge(sem("down_full"), 2 * NB)
            act.wait_ge(sem("sim_free0"), 6 * NB)
            act.wait_ge(sem("sim_free1"), 5 * NB)
            act.wait_ge(sem("emb_lo"), NPIECE)
            silu_of(0, 0, 0)
            p_out(0, 1, 0)
            silu_of(0, 0, 1)
            p_out(0, 1, 1)
            g_hi(0, 0, 0)
            tile(0, 0, 2, table_at=TABLE_AT)
            tile(0, 1, 2)
            with act.Fori(1, NB - 1) as b:
                tile(b, 0, 2)
                tile(b, 1, 2)
            tile(NB - 1, 0, 1)
            tile(NB - 1, 1, 0)

        @block.vector
        def _(dve):
            def chained(name, base=0):
                count = [0]

                def link(ins):
                    count[0] += 1
                    ins.then_inc(sem(name), 1)
                    dve.wait_ge(sem(name), base + count[0])
                return link

            def split(dst, src, scale, hi):
                return dve.scalar_tensor_tensor(dst, src, scale, hi, ALU.mult, ALU.subtract)

            def step_past():
                dve.sem_inc(sem("dve_steps"), 1)

            def rsqrt(link, step_between=lambda: None):
                link(dve.tensor_scalar(ve, mv[:, :, 1], EPS, None, ALU.add))
                link(dve.tensor_scalar(nh, ve, -0.5, None, ALU.mult))
                link(dve.tensor_scalar(r0.bitcast(I32), ve.bitcast(I32), 1, None, ALU.arith_shift_right))
                link(dve.tensor_scalar(r1.bitcast(I32), r0.bitcast(I32), -1.0, float(RSQRT_SEED), ALU.mult, ALU.add))
                step_between()
                r = r1
                for _ in range(3):
                    link(dve.tensor_tensor(r0, r, r, ALU.mult))
                    link(dve.tensor_tensor(r0, r0, nh, ALU.mult))
                    o = r2 if r is r1 else r1
                    link(dve.scalar_tensor_tensor(o, r0, 1.5, r, ALU.add, ALU.mult))
                    r = o
                return r

            def moments(src, link):
                for q in range(NQ):
                    last = dve.bn_stats(stats[:, q], src[:, q])
                link(last)
                step_past()
                for q in range(NQ):
                    last = dve.bn_aggr(mv[:, q], stats[:, q])
                link(last)

            def shift(r, done):
                dve.scalar_tensor_tensor(r0, mv[:, :, 0], -1.0, r, ALU.mult, ALU.mult).then_inc(sem(done), 1)

            LN_LINKS = 2 + 4 + 9

            def ln1(b):
                link = chained("ln1_chain", LN_LINKS * b)
                dve.wait_ge(sem("x_in"), 16 * b + 16)
                dve.wait_ge(sem("x2n"), b)
                moments(xin, link)
                shift(rsqrt(link), "ln1")

            def masks(b):
                dve.wait_ge(sem("r_full"), 2 * b)
                dve.wait_ge(sem("xsum"), b + 1)
                dve.wait_ge(sem("t1_full"), 2 * b + 2)
                for s in range(NQ):
                    dve.wait_ge(sem("s_full"), NQ * b + s + 1)
                    dve.tensor_tensor(att[s], bank[s % 2][:, 0:T - P * s], decay_tab[:, 0:T - P * s], ALU.mult).then_inc(sem(f"att_free{s % 2}"), 1)

            def add_reads(b):
                dve.wait_ge(sem("xsum"), b + 1)
                dve.wait_ge(sem("x2n"), b)
                dve.wait_ge(sem("x1_kept"), b)
                for n in range(2):
                    dve.wait_ge(sem("r_full"), 2 * b + n + 1)
                    dve.tensor_tensor(x1[:, 2 * n:2 * n + 2].rearrange("p q d -> p (q d)"), bank[n][:, :],
                                      xin[:, 2 * n:2 * n + 2].rearrange("p q d -> p (q d)"), ALU.add).then_inc(sem(f"att_free{n}"), 1)
                for n in range(2):
                    dve.wait_ge(sem(f"att_free{n}"), 6 * b + READS)
                dve.sem_inc(sem("xin_used"), 1)

            def ln2(b, steps_between=(lambda: None, lambda: None)):
                link = chained("ln2_chain", LN_LINKS * b)
                dve.wait_ge(sem("xhat"), b + 1)
                moments(x1, link)
                steps_between[0]()
                shift(rsqrt(link, steps_between[1]), "ln2")

            def x2_lo(b):
                for k in range(KC):
                    dve.wait_ge(sem("x2_hi"), 2 * b + k + 1)
                    split(x2s[:, 1, k], bank[k][:, :], X_SCALE, x2s[:, 0, k]).then_inc(sem(f"att_free{k}"), 1)

            def top8_halves(b, q):
                if q == 0:
                    dve.wait_ge(sem("picks"), b)
                    dve.wait_ge(sem("hit"), 3 * b)
                    dve.wait_ge(sem("esub"), b)
                for n in range(2):
                    dve.wait_ge(sem(f"sim_free{n}"), (6 - n) * b + q + 1)
                step_past()
                for g in range(8):
                    last = dve.max(top[:, g // 4, q, g % 4], sim[:, q, g])
                last.then_inc(sem("top_chain"), 1)
                dve.wait_ge(sem("top_chain"), 4 * (NQ * b + q) + 1)
                dve.tensor_tensor(comb, top[:, 0, q, :, :].unsqueeze(3).to_broadcast([P, HEADS, 8, 8]),
                                  top[:, 1, q, :, :].unsqueeze(2).to_broadcast([P, HEADS, 8, 8]), ALU.add).then_inc(sem("top_chain"), 1)

            def top8_pairs(b, q):
                for n in range(2):
                    dve.wait_ge(sem(f"sim_free{n}"), (6 - n) * b + q + 1)
                step_past()
                for g in range(8):
                    last = dve.max_index(topi[:, g // 4, q, g % 4], top[:, g // 4, q, g % 4], sim[:, q, g])
                last.then_inc(sem("top_chain"), 1)
                dve.wait_ge(sem("top_chain"), 4 * (NQ * b + q) + 2)
                step_past()
                for h in range(HEADS):
                    last = dve.max(best[:, q, h], comb[:, h].rearrange("p a b -> p (a b)"))
                last.then_inc(sem("top_chain"), 1)
                dve.wait_ge(sem("top_chain"), 4 * (NQ * b + q) + 4)
                step_past()
                for h in range(HEADS):
                    last = dve.max_index(besti[:, (q * HEADS + h) * 8:(q * HEADS + h) * 8 + 8], best[:, q, h],
                                         comb[:, h].rearrange("p a b -> p (a b)"))
                last.then_inc(sem("topped"), 1)

            def top8(b, q):
                top8_halves(b, q)
                top8_pairs(b, q)

            def ranks(b):
                dve.wait_ge(sem("topped"), NQ * b + NQ)
                dve.wait_ge(sem("probs"), b)
                dve.wait_ge(sem("indices"), b)
                dve.tensor_scalar(rank_of[0], besti, 3, None, ALU.logical_shift_right)
                dve.tensor_scalar(rank_of[1], besti, 7, None, ALU.bitwise_and).then_inc(sem("ranks"), 1)
                dve.wait_ge(sem("ranks"), b + 1)
                for g in range(2):
                    dve.tensor_tensor(hit[g], rank_of[g].rearrange("p (g k) -> p g k", k=8).unsqueeze(3).to_broadcast([P, NQ * HEADS, 8, 8]),
                                      rank[:, :].unsqueeze(1).unsqueeze(1).to_broadcast([P, NQ * HEADS, 8, 8]),
                                      ALU.is_equal).then_inc(sem("hit"), 1)
                dve.tensor_copy(topf, topi.rearrange("p g q h r -> p g (q h) r")).then_inc(sem("hit"), 1)
                bq = best.rearrange("p q h k -> p (q h) k")
                dve.tensor_tensor(esub.rearrange("p (g k) -> p g k", k=8), bq, bq[:, :, 0:1].to_broadcast([P, NQ * HEADS, 8]),
                                  ALU.subtract).then_inc(sem("esub"), 1)

            def indices(b):
                dve.wait_ge(sem("picks"), b + 1)
                dve.wait_ge(sem("tab_full"), b)
                dve.wait_ge(sem("indices"), b)
                dve.tensor_scalar(past, pick[0], float(NI), float(P - 1), ALU.is_ge, ALU.mult).then_inc(sem("past"), 1)
                dve.tensor_scalar(table[:, 0], pick[0], float(NI - 1), None, ALU.min)
                dve.wait_ge(sem("past"), b + 1)
                dve.tensor_tensor(table[:, 1], pick[1], past, ALU.max).then_inc(sem("indices"), 1)

            def softmax(b):
                link = chained("softmax_chain", 2 * b)
                dve.wait_ge(sem("exped"), b + 1)
                dve.wait_ge(sem("tab_full"), b)
                e3 = esub.rearrange("p (g k) -> p g k", k=8)
                link(dve.tensor_reduce(esum, e3, AX_X, ALU.add))
                link(dve.reciprocal(esum, esum))
                dve.tensor_tensor(table[:, 2, :].rearrange("p (g k) -> p g k", k=8), e3,
                                  esum.unsqueeze(2).to_broadcast([P, NQ * HEADS, 8]), ALU.mult).then_inc(sem("probs"), 1)

            def hidden(b, c):
                dve.wait_ge(sem("gate"), NIC * b + c + 1)
                dve.wait_ge(sem("h_lo"), NIC * b + max(c - 1, 0))
                dve.scalar_tensor_tensor(h32[:, c % 2], bank[5 + 2 * (c % 2)][:, :], col(H_SCALE), gate[:, c % 2],
                                         ALU.mult, ALU.mult).then_inc(sem(f"mlp_free{c % 2}"), 1)

            def add_mlp(b, half):
                dve.wait_ge(sem("x1_out"), 16 * b)
                dve.wait_ge(sem("x1_kept"), b + 1)
                for q in (2 * half, 2 * half + 1):
                    dve.wait_ge(sem("down_full"), 2 * b + q // 2 + 1)
                    last = dve.scalar_tensor_tensor(x1m[:, q], bank[2 + q // 2][:, (q % 2) * D:(q % 2 + 1) * D], col(MLP_OUT),
                                                    x1k[:, q], ALU.mult, ALU.add)
                last.then_inc(sem(f"sim_free{half}"), 1)

            def tab_lo(b, n):
                dve.wait_ge(sem("tab_hi"), b + 1)
                dve.wait_ge(sem("tab_ij"), b + 1)
                split(tab16[:, 3], bank[n][:, 2 * P:3 * P].rearrange("p (h t) -> p h t", h=2), P_SCALE,
                      tab16[:, 2]).then_inc(sem("tab_lo"), 1)
                dve.wait_ge(sem("tab_lo"), b + 1)
                if n == 2:
                    dve.sem_inc(sem("sim_free0"), 1)

            dve.wait_ge(sem("const_in"), 160)
            dve.tensor_scalar(col(NEG), col(DEC), -1.0, None, ALU.mult).then_inc(sem("scal_chain"), 1)
            dve.wait_ge(sem("scal_chain"), 1)
            dve.tensor_scalar(col(POS), col(NEG), 0.0, None, ALU.max).then_inc(sem("scal_chain"), 1)
            dve.tensor_tensor(col(NAB), col(NEG), col(DEC), ALU.min).then_inc(sem("scal_chain"), 1)
            dve.memset(xT[:, :, 0:1], 0.0).then_inc(sem("zero_col"), 1)
            ln1(0)
            dve.wait_ge(sem("act_scal"), 2)
            dve.wait_ge(sem("scal_chain"), 3)
            dve.scalar_tensor_tensor(col(LOGG), col(POS), -1.0, col(LNN), ALU.mult, ALU.subtract).then_inc(sem("scal_chain"), 1)
            dve.wait_ge(sem("act_scal"), 4)
            dve.tensor_tensor(decay_tab, decay_tab, causal, ALU.mult).then_inc(sem("decay_tab"), 1)
            dve.wait_ge(sem("decay_tab"), 1)
            dve.wait_ge(sem("zero_col"), 1)

            dve.wait_ge(sem("mlp_in"), 48)
            for n, v in ((WG, raw_gu[:, 0:KC * INTER]), (WU, raw_gu[:, KC * INTER:]), (WD_, raw_wd)):
                dve.tensor_reduce(col(mx + n), v, AX_X, ALU.max, apply_absolute_value=True).then_inc(sem("w_max"), 1)
            dve.wait_ge(sem("kf32"), 4)
            dve.tensor_reduce(col(mx + KF), kf32, AX_X, ALU.max, apply_absolute_value=True).then_inc(sem("w_max"), 1)

            def scales(first, n, link):
                link(dve.tensor_scalar(col(mxr + first, n), col(mxr + first, n), 1e-30, None, ALU.max))
                link(dve.tensor_scalar(col(pw + first, n).bitcast(I32), col(mxr + first, n).bitcast(I32), EXPONENT, None, ALU.bitwise_and))
                link(dve.reciprocal(col(rp + first, n), col(pw + first, n)))
                link(dve.tensor_scalar(col(ws + first, n), col(rp + first, n), W_SCALE, None, ALU.mult))

            link = chained("scale_chain")
            dve.wait_ge(sem("w_maxed"), 1)
            scales(0, 4, link)
            link(dve.tensor_scalar(col(SIM_OUT), col(pw + KF), 1.0 / (X_SCALE * W_SCALE), None, ALU.mult))
            link(dve.tensor_scalar(col(GATE_IN), col(pw + WG), 1.0 / (X_SCALE * W_SCALE), None, ALU.mult))
            link(dve.tensor_scalar(col(H_SCALE), col(rp + WG), 1.0 / (8 * X_SCALE * W_SCALE), None, ALU.mult))
            link(dve.tensor_tensor(col(MLP_OUT), col(pw + WG), col(pw + WU), ALU.mult))
            link(dve.scalar_tensor_tensor(col(MLP_OUT), col(MLP_OUT), 8 / W_SCALE, col(pw + WD_), ALU.mult, ALU.mult))
            dve.sem_inc(sem("w_scales"), 1)
            masks(0)
            (kh, gh, _, _), (kl, gl, _, _) = weight_parts(0), weight_parts(1)
            dve.wait_ge(sem("w_hi"), 1)
            split(kl, kf32, col(ws + KF), kh).then_inc(sem("kf_lo"), 1)
            add_reads(0)
            ln2(0)
            x2_lo(0)
            dve.wait_ge(sem("w_hi"), 2)
            split(gl, raw_gu[:, 0:KC * INTER], col(ws + WG), gh).then_inc(sem("mlp_lo"), 1)
            dve.memset(col(mx + DN, 2), 0.0).then_inc(sem("mx_chain"), 1)

            def look(b, half):
                n = 2 * b - 1 + half
                dve.wait_ge(sem("emb_in"), 64)
                dve.wait_ge(sem("mx_chain"), n)
                step_past()
                dve.tensor_reduce(col(58), raw_emb[:, bass.ds((2 * (b - MAX_SEQ[0]) + half) * (LOOK // 2), LOOK // 2)], AX_X, ALU.max,
                                  apply_absolute_value=True).then_inc(sem("looked"), 1)
                dve.wait_ge(sem("looked"), n)
                dve.tensor_tensor(col(mx + DN), col(mx + DN), col(58), ALU.max).then_inc(sem("mx_chain"), 1)

            def emb_scales():
                link = chained("scale2_chain")
                dve.wait_ge(sem("e_maxed"), 1)
                scales(DN, 2, link)
                link(dve.tensor_scalar(col(Z_IN), col(pw + DN), 1.0 / (X_SCALE * W_SCALE), None, ALU.mult))
                link(dve.tensor_scalar(col(PROB), col(rp + DN), 16 / P_SCALE, None, ALU.mult))
                link(dve.tensor_scalar(col(EXP_OUT), col(pw + DN), 1.0 / 16, None, ALU.mult))
                link(dve.scalar_tensor_tensor(col(EXP_OUT), col(EXP_OUT), 1.0 / W_SCALE, col(pw + UP), ALU.mult, ALU.mult))
                dve.sem_inc(sem("e_scales"), 1)

            def sequence(b, first=False):
                if not first:
                    softmax(b - 1)
                ln1(b + 1)
                top8(b, 0)
                if isinstance(b, int) and b == MAX_SEQ[1]:
                    emb_scales()
                if not first:
                    indices(b - 1)
                top8_halves(b, 1)
                hidden(b, 0)
                hidden(b, 1)
                if first:
                    dve.wait_ge(sem("sim_free0"), NQ)
                    dve.sem_inc(sem("sim_free0"), 1)
                else:
                    tab_lo(b - 1, 2)
                top8_pairs(b, 1)
                masks(b + 1)
                top8(b, 2)
                hidden(b, 2)
                add_reads(b + 1)
                ln2(b + 1, (lambda: hidden(b, 3), lambda: hidden(b, 4)))
                hidden(b, 5)
                if not isinstance(b, int):
                    look(b, 0)
                top8_halves(b, 3)
                hidden(b, 6)
                hidden(b, 7)
                top8_pairs(b, 3)
                x2_lo(b + 1)
                ranks(b)
                add_mlp(b, 0)
                if not isinstance(b, int):
                    look(b, 1)
                add_mlp(b, 1)

            def last_sequence(b):
                softmax(b - 1)
                top8(b, 0)
                indices(b - 1)
                top8_halves(b, 1)
                hidden(b, 0)
                top8_pairs(b, 1)
                hidden(b, 1)
                tab_lo(b - 1, 2)
                for q in (2, 3):
                    top8_halves(b, q)
                    hidden(b, 2 * q - 2)
                    top8_pairs(b, q)
                    hidden(b, 2 * q - 1)
                build_a(0, 0, 0, 0)
                build_a(0, 0, 0, 1)
                hidden(b, 6)
                build_a(0, 0, 0, 2)
                build_a(0, 0, 0, 3)
                hidden(b, 7)
                for c in (1, 2):
                    for m in range(4):
                        build_a(0, 0, c, m)
                add_mlp(b, 0)
                add_mlp(b, 1)

            def product(b, h, s):
                dve.wait_ge(sem(f"z_free{s % 2}"), 16 * b + 8 * h + s // 2 + 1)
                if not (isinstance(b, int) and b == h == s == 0):
                    dve.wait_ge(sem("g_lo"), 32 * b + 16 * h + s - 1)
                if s == 0:
                    for n in range(2):
                        dve.wait_ge(sem(f"p_free{n}"), 16 * b + 8 * h + 8)
                dve.tensor_tensor(g32[:, s % 2].rearrange("p (i q t) -> p i q t", i=2, q=NQ),
                                  silu_z[:, s % 2].rearrange("p (i q t) -> p i q t", i=2, q=NQ),
                                  p_sb[:, h, 2 * s:2 * s + 2], ALU.mult).then_inc(sem(f"s_free{s % 2}"), 1)
                if s == 15:
                    dve.wait_ge(sem("s_free1"), 16 * b + 8 * h + 8)
                    dve.wait_ge(sem("s_free0"), 16 * b + 8 * h + 8)
                    dve.sem_inc(sem("p_used"), 1)

            def g_lo(b, h, s):
                dve.wait_ge(sem("g_hi"), 32 * b + 16 * h + s + 1)
                dve.tensor_tensor(g_s[:, s % 2, 1].rearrange("p i t -> p (i t)"), g32[:, s % 2],
                                  g_s[:, s % 2, 0].rearrange("p i t -> p (i t)"), ALU.subtract).then_inc(sem("g_lo"), 1)

            def build_a(b, h, c, step):
                tab = tab_sb[:, h]
                t0 = 16 * c
                if isinstance(b, int) and b == h == c == step == 0:
                    dve.wait_ge(sem("t2_full"), 2 * NB)
                    dve.wait_ge(sem("x1_kept"), NB)
                if step == 0:
                    dve.wait_ge(sem(f"tab_in{h}"), 16 * b + 16)
                    dve.wait_ge(sem("hit_p"), 2 * (8 * b + 4 * h + c))
                    dve.tensor_tensor(hit_i, iota[:, 0:NI].unsqueeze(1).to_broadcast([P, 16, NI]),
                                      tab[:, 0, t0:t0 + 16].unsqueeze(2).to_broadcast([P, 16, NI]), ALU.is_equal).then_inc(sem("hit_i"), 1)
                elif step == 1:
                    dve.wait_ge(sem("hit_i"), 8 * b + 4 * h + c + 1)
                    dve.wait_ge(sem("a_built"), 8 * b + 4 * h + c)
                    for m in range(2):
                        dve.tensor_tensor(hit_p[:, m], hit_i, tab[:, 2 + m, t0:t0 + 16].unsqueeze(2).to_broadcast([P, 16, NI]),
                                          ALU.mult).then_inc(sem("hit_p"), 1)
                else:
                    m = step - 2
                    dve.wait_ge(sem("hit_p"), 2 * (8 * b + 4 * h + c + 1))
                    if m == 0 and not (isinstance(b, int) and b == 0 and h == 0 and c < 2):
                        dve.wait_ge(sem("p_full"), 4 * (8 * b + 4 * h + c - 1))
                    for q in range(NQ):
                        last = dve.tensor_scalar(a_sb[:, c % 2, m, :, q, :], hit_p[:, m], qmask[:, q:q + 1], None, ALU.mult)
                    if m == 1:
                        last.then_inc(sem("a_built"), 1)
                        dve.wait_ge(sem("b_differ"), 8 * b + 4 * h + c + 1)
                        dve.tensor_scalar(b_sb[:, c % 2], b_sb[:, c % 2], 0.0, None, ALU.is_equal).then_inc(sem("b_built"), 1)

            def finish(b, h):
                dve.wait_ge(sem("up"), 32 * b + 16 * h + 16)
                dve.wait_ge(sem(f"res_in{h}"), 16 * NQ * b + 16 * NQ)
                dve.wait_ge(sem(f"stored{h}"), 16 * NQ * b)
                for u in range(2):
                    dve.scalar_tensor_tensor(fin[:, h, u], bank[4 + 2 * h + u][:, 0:D], col(EXP_OUT), res[:, h, u],
                                             ALU.mult, ALU.add).then_inc(sem("fin"), 1)
                dve.wait_ge(sem("fin"), 4 * b + 2 * h + 2)
                dve.sem_inc(sem(f"sum_free{h}"), 2)

            def tile(b, h, rest, table_at=None):
                for s in range(16):
                    n, m = divmod(s + 22, 16)
                    if n <= rest:
                        build_a(*after(b, h, n), m // 4, m % 4)
                    n, m = divmod(s + 1, 16)
                    if n <= rest:
                        g_lo(*after(b, h, n), m)
                    n, m = divmod(s + 2, 16)
                    if n <= rest:
                        product(*after(b, h, n), m)
                    if s == 1:
                        prev(b, h)
                    if table_at == s + RANKS_BEFORE:
                        ranks(NB - 1)
                    if table_at == s + 1:
                        softmax(NB - 1)
                        indices(NB - 1)
                    if table_at == s:
                        tab_lo(NB - 1, 6)

            def prev(b, h):
                if h == 1:
                    finish(b, 0)
                elif isinstance(b, int) and b == 0:
                    pass
                else:
                    finish(b - 1, 1)

            sequence(0, first=True)
            with dve.Fori(1, MAX_SEQ[1]) as b:
                sequence(b)
            dve.wait_ge(sem("mx_chain"), 2 * MAX_SEQ[1] - 1)
            dve.sem_inc(sem("e_max"), 1)
            for b in range(MAX_SEQ[1], NB - 1):
                sequence(b)
            last_sequence(NB - 1)
            for m in range(12, 22):
                build_a(0, m // 16, m % 16 // 4, m % 4)
            dve.wait_ge(sem("h_lo"), NIC * NB)
            dve.wait_ge(sem("down_full"), 2 * NB)
            dve.wait_ge(sem("emb_lo"), NPIECE)
            product(0, 0, 0)
            product(0, 0, 1)
            g_lo(0, 0, 0)
            tile(0, 0, 2, table_at=TABLE_AT)
            tile(0, 1, 2)
            with dve.Fori(1, NB - 1) as b:
                tile(b, 0, 2)
                tile(b, 1, 2)
            tile(NB - 1, 0, 1)
            tile(NB - 1, 1, 0)
            finish(NB - 1, 1)

        @block.gpsimd
        def _(pool):
            MAX = bass.bass_isa.ReduceOp.max
            pool.wait_ge(sem("xhat"), 1)
            pool.tensor_tensor(xin, xin, xhat, ALU.add).then_inc(sem("xsum"), 1)
            pool.wait_ge(sem("w_max"), 4)
            pool.partition_all_reduce(col(mxr, 4), col(mx, 4), P, MAX).then_inc(sem("w_maxed"), 1)

            _, _, uh, dh = weight_parts(0)
            _, _, ul, dl = weight_parts(1)
            pool.wait_ge(sem("u_hi"), 2)
            pool.tensor_tensor(ul, raw_gu[:, KC * INTER:], uh, ALU.subtract).then_inc(sem("mlp_lo"), 1)
            pool.wait_ge(sem("d_hi"), 2)
            pool.tensor_tensor(dl, raw_wd, dh, ALU.subtract).then_inc(sem("mlp_lo"), 1)

            def residual(b):
                pool.wait_ge(sem("xhat"), b + 1)
                pool.tensor_tensor(xin, xin, xhat, ALU.add).then_inc(sem("xsum"), 1)

            def keep(b):
                for n in range(2):
                    pool.wait_ge(sem(f"att_free{n}"), 6 * b + READS)
                pool.wait_ge(sem("sim_free0"), 6 * b)
                pool.wait_ge(sem("sim_free1"), 5 * b)
                pool.sem_inc(sem("pool_steps"), 1)
                pool.tensor_copy(x1k, x1).then_inc(sem("x1_kept"), 1)

            def h_lo(b, c):
                pool.wait_ge(sem("h_hi"), NIC * b + c + 1)
                pool.tensor_tensor(h_s[:, 1, c], h32[:, c % 2], h_s[:, 0, c], ALU.subtract).then_inc(sem("h_lo"), 1)

            def select(b, g):
                if g == 0:
                    pool.wait_ge(sem("hit"), 3 * b + 3)
                    pool.wait_ge(sem("indices"), b)
                n = [4 * g]

                def link(ins):
                    n[0] += 1
                    ins.then_inc(sem("sel_chain"), 1)
                    pool.wait_ge(sem("sel_chain"), SEL * b + n[0])

                link(pool.tensor_tensor(hit2, hit[g], topf[:, g].unsqueeze(2).to_broadcast([P, NQ * HEADS, 8, 8]), ALU.mult))
                link(pool.tensor_tensor(hit[g][:, :, :, 0:4], hit2[:, :, :, 0:4], hit2[:, :, :, 4:8], ALU.add))
                link(pool.tensor_tensor(hit2[:, :, :, 0:2], hit[g][:, :, :, 0:2], hit[g][:, :, :, 2:4], ALU.add))
                link(pool.tensor_tensor(pick[g].rearrange("p (g k) -> p g k", k=8), hit2[:, :, :, 0], hit2[:, :, :, 1], ALU.add))
                if g == 1:
                    pool.sem_inc(sem("picks"), 1)

            SEL = 8
            def emb_low(m):
                pool.wait_ge(sem("emb_hi"), m + 1)
                pool.tensor_tensor(parts[:, m, 1], scaled[:, m % 2], parts[:, m, 0], ALU.subtract).then_inc(sem("emb_lo"), 1)

            def sequence(b, last=False):
                pieces = list(SPLITS.get(b, ())) if isinstance(b, int) else []

                keep(b)
                if not last:
                    residual(b + 1)
                else:
                    differ_b(0, 0, 0)
                for c in range(NIC):
                    h_lo(b, c)
                    if last and c == 2:
                        differ_b(0, 0, 1)
                    for _ in range({0: 4, 2: 1, 3: 1, NIC - 1: 2}.get(c, 0)):
                        if pieces:
                            emb_low(pieces.pop(0))
                if not last:
                    select(b, 0)
                    select(b, 1)

            def differ_b(b, h, c):
                if c == 0:
                    pool.wait_ge(sem(f"tab_in{h}"), 16 * b + 16)
                if isinstance(b, int) and b == 0 and h == 0 and c < 2:
                    pool.wait_ge(sem("sim_full"), 8 * NB)
                else:
                    pool.wait_ge(sem("p_full"), 4 * (8 * b + 4 * h + c - 1))
                pool.tensor_tensor(b_sb[:, c % 2], iota[:, :].unsqueeze(1).to_broadcast([P, 16, P]),
                                   tab_sb[:, h, 1, 16 * c:16 * c + 16].unsqueeze(2).to_broadcast([P, 16, P]),
                                   ALU.subtract).then_inc(sem("b_differ"), 1)

            sequence(0)
            with pool.Fori(1, MAX_SEQ[1]) as b:
                sequence(b)
            pool.wait_ge(sem("e_max"), 1)
            pool.partition_all_reduce(col(mxr + DN, 2), col(mx + DN, 2), P, MAX).then_inc(sem("e_red"), 1)
            pool.wait_ge(sem("e_red"), 1)
            pool.tensor_copy(col(mxr + UP), col(mxr + DN)).then_inc(sem("e_maxed"), 1)
            for b in range(MAX_SEQ[1], NB):
                sequence(b, last=(b == NB - 1))
            for n in range(2, 6):
                differ_b(0, n // 4, n % 4)
            select(NB - 1, 0)
            differ_b(0, 1, 2)
            select(NB - 1, 1)
            differ_b(0, 1, 3)
            with pool.Fori(1, NB) as b:
                for n in range(8):
                    differ_b(b, n // 4, n % 4)


def kernel(L0_attn_out, L0_attn_W_write, L0_attn_W_read, L0_attn_decay, L0_attn_log_alpha, L0_ffn_Wq,
           L0_ffn_keys, L0_ffn_down_embed, L0_ffn_up_embed, L0_ffn_Wg, L0_ffn_Wu, L0_ffn_Wd):
    import numpy as np
    import concourse.bacc as bacc
    from concourse import mybir as mb
    from concourse.bass_utils import run_bass_kernel_spmd

    def rows128(w):
        w = np.asarray(w)
        return np.ascontiguousarray(w.reshape(-1, 128, w.shape[1]).transpose(1, 0, 2).reshape(128, -1))

    def one(v):
        return np.ascontiguousarray(np.broadcast_to(np.asarray(v).reshape(1, 1), (128, 1)))

    lane, tok = np.arange(128)[:, None], np.arange(T)[None, :]
    ins = [
        ("x", np.ascontiguousarray(L0_attn_out)),
        ("wwrite", np.ascontiguousarray(L0_attn_W_write)),
        ("wreadT", np.ascontiguousarray(np.asarray(L0_attn_W_read).T)),
        ("decay", one(L0_attn_decay)),
        ("log_alpha", one(L0_attn_log_alpha)),
        ("wq", np.ascontiguousarray(L0_ffn_Wq)),
        ("keys", np.ascontiguousarray(np.asarray(L0_ffn_keys).transpose(3, 2, 0, 1).reshape(HALF, 8, NK))),
        ("emb", np.ascontiguousarray(np.concatenate([rows128(np.asarray(L0_ffn_down_embed).T), rows128(L0_ffn_up_embed)], axis=1))),
        ("wg", rows128(np.asarray(L0_ffn_Wg).T)),
        ("wu", rows128(np.asarray(L0_ffn_Wu).T)),
        ("wd", rows128(np.asarray(L0_ffn_Wd).T)),
        ("ident", np.eye(128, dtype=np.float32)),
        ("diffs", np.maximum(tok - 1 - lane, 0).astype(np.float32)),
        ("causal", (tok > lane).astype(np.float32)),
        ("iota", np.ascontiguousarray(np.broadcast_to(np.arange(128), (128, 128))).astype(np.float16)),
        ("rank", np.ascontiguousarray(np.broadcast_to(np.arange(8), (128, 8))).astype(np.float32)),
        ("qmask", (lane // PAIRS == np.arange(NQ)[None, :]).astype(np.float32)),
    ]
    nc = bacc.Bacc("TRN2", target_bir_lowering=False, num_devices=1)
    arrays, args = {}, []
    for name, arr in ins:
        arrays[f"in_{name}"] = arr
        args.append(nc.dram_tensor(f"in_{name}", arr.shape, mb.dt.from_np(arr.dtype), kind="ExternalInput").ap())
    args.append(nc.dram_tensor("x2_parts", [NB, P, 2, KC, T], F16, kind="Internal").ap())
    args.append(nc.dram_tensor("pick_tables", [NB, 2, P, 4, TQ], F16, kind="Internal").ap())
    args.append(nc.dram_tensor("x1_rows", [NB, T, D], F32, kind="Internal").ap())
    args.append(nc.dram_tensor("out_0", [NB, T, D], F32, kind="ExternalOutput").ap())
    dense_kernel(nc, *args)
    r = run_bass_kernel_spmd(nc, [arrays], core_ids=[0])
    return r.results[0]["out_0"]
```

```python
from contextlib import ExitStack

import concourse.bass as bass
from concourse import mybir

ALU = mybir.AluOpType
ACT = mybir.ActivationFunctionType
F32, F16, I32, U32 = mybir.dt.float32, mybir.dt.float16, mybir.dt.int32, mybir.dt.uint32
AX_X = mybir.AxisListType.X

P = 128
NB, T, D = 8, 512, 256
NQ = T // P
KC = D // P
INTER, NIC = 1024, 1024 // P
HEADS, NK, TOPK, HALF = 4, 128, 8, 64
PAIRS = HEADS * TOPK
NE = 4096
NI = NE // P
TH = T // 2
TQ = TH // NQ
TC = TQ // 2
EPS = 1e-5

X_SCALE = 2.0 ** 10
W_SCALE = 2.0 ** 14
P_SCALE = 2.0 ** 12
ROWS, SCORES, READS, ROWS2 = 1, 4, 5, 6
RSQRT_SEED = 0x5F3759DF
EXPONENT = 0x7F800000
PIECE = 1024
NPIECE = 2 * KC * NE // PIECE
TABLE_AT = 6
MAX_SEQ = (1, 5)
SPLITS = {5: range(0, NPIECE // 2), 6: range(NPIECE // 2, NPIECE)}
LOOK = 2 * KC * NE // (MAX_SEQ[1] - MAX_SEQ[0])
HALVES = ((0, 0), (0, 1), (1, 0))


def dense_kernel(nc, x, wwrite, wreadT, decay, log_alpha, wq, keys, emb, wg, wu, wd,
                 ident_d, diffs_d, causal_d, iota_d, rank_d, umask_d, x2_d, tab_d, x1_d, out):
    ctx = ExitStack()
    with ctx:
        ARENA = 36520
        X1_AT = NQ * D + KC * (T + 2) + NQ * D + NQ * T - P * 6 + T + KC * D
        SECOND = X1_AT + NQ * D + 16 * P + 2 * NI * TH + 5 * 4 * D
        arena = ctx.enter_context(nc.sbuf_tensor("arena", [P, ARENA], F32))
        embs = ctx.enter_context(nc.sbuf_tensor("embs", [P, 2 * KC * NE], F32))
        ident = ctx.enter_context(nc.sbuf_tensor("ident", [P, P], F32))
        iota = ctx.enter_context(nc.sbuf_tensor("iota", [P, P], F16))
        rank = ctx.enter_context(nc.sbuf_tensor("rank", [P, TOPK], F32))
        umask = ctx.enter_context(nc.sbuf_tensor("umask", [P, 2], F32))
        scal = ctx.enter_context(nc.sbuf_tensor("scal", [P, 64], F32))
        bank = [ctx.enter_context(nc.psum_tensor(f"bank{i}", [P, 512], F32)) for i in range(8)]

        sems = {}

        def sem(name):
            if name not in sems:
                sems[name] = ctx.enter_context(nc.semaphore(name))
            return sems[name]

        class Region:

            def __init__(self, whole, start=0):
                self.whole, self.at = whole, start

            def take(self, n, dt=F32):
                words = n if dt in (F32, I32, U32) else n // 2
                v = self.whole[:, self.at:self.at + words]
                self.at += words
                assert self.at <= self.whole.shape[1], self.at
                return v if dt == F32 else v.bitcast(dt)

        raw_emb = embs[:, :]
        parts = embs[:, :].bitcast(F16).rearrange("p (m s c) -> p m s c", m=NPIECE, s=2)

        def down_w(s, k, i):
            n = PIECE // P
            return parts[:, k * (NPIECE // 4) + i // n, s, (i % n) * P:(i % n + 1) * P]

        def up_w(s, i):
            n = PIECE // D
            return parts[:, NPIECE // 2 + i // n, s, (i % n) * D:(i % n + 1) * D]

        e = Region(embs)
        raw_gu = e.take(2 * KC * INTER)
        raw_wd = e.take(NIC * D)
        kf32 = e.take(KC * 2 * HEADS * NK)
        wq_sb = e.take(8 * D)[0:HALF].rearrange("p (g d) -> p g d", g=8)
        keys_sb = e.take(8 * NK)[0:HALF].rearrange("p (g k) -> p g k", g=8)
        ww_sb = e.take(KC * D).rearrange("p (k d) -> p k d", k=KC)
        wr_sb = e.take(KC * D).rearrange("p (k d) -> p k d", k=KC)
        diffs = e.take(T)
        causal = e.take(T)

        a = Region(arena)
        xin = a.take(NQ * D).rearrange("p (q d) -> p q d", q=NQ)
        xT = a.take(KC * (T + 2)).rearrange("p (k t) -> p k t", k=KC)
        v_sb = a.take(NQ * D).rearrange("p (q d) -> p q d", q=NQ)
        x2n = v_sb
        xhat = arena[:, a.at:a.at + NQ * D].rearrange("p (q d) -> p q d", q=NQ)
        att = [a.take(T - P * s) for s in range(NQ)]
        decay_tab = a.take(T)
        wc = a.take(KC * D).rearrange("p (k d) -> p k d", k=KC)
        x1 = a.take(NQ * D).rearrange("p (q d) -> p q d", q=NQ)
        kf_s = a.take(2 * KC * 2 * HEADS * NK, F16).rearrange("p (s k n) -> p s k n", s=2, k=KC)
        wgu_s = a.take(4 * KC * INTER, F16).rearrange("p (s g k n) -> p s g k n", s=2, g=2, k=KC)
        sim = a.take(NQ * 8 * NK).rearrange("p (q g k) -> p q g k", q=NQ, g=8)
        wd_s = a.take(2 * NIC * D, F16).rearrange("p (s c d) -> p s c d", s=2, c=NIC)
        x1k = a.take(NQ * D).rearrange("p (q d) -> p q d", q=NQ)
        x2s = a.take(2 * KC * T, F16).rearrange("p (s k t) -> p s k t", s=2, k=KC)
        h_s = a.take(2 * NIC * T, F16).rearrange("p (s c t) -> p s c t", s=2, c=NIC)
        gate = a.take(2 * T).rearrange("p (n t) -> p n t", n=2)
        h32 = a.take(2 * T).rearrange("p (n t) -> p n t", n=2)
        scaled = a.take(2 * PIECE).rearrange("p (n c) -> p n c", n=2)
        stats = a.take(NQ * 6).rearrange("p (q n) -> p q n", q=NQ)
        mv = a.take(NQ * 2).rearrange("p (q n) -> p q n", q=NQ)
        ve, nh, r0, r1, r2 = (a.take(NQ) for _ in range(5))
        a.at = max(a.at, SECOND)
        x1m = a.take(NQ * D).rearrange("p (q d) -> p q d", q=NQ)
        top = a.take(2 * NQ * HEADS * TOPK).rearrange("p (g q h k) -> p g q h k", g=2, q=NQ, h=HEADS)
        topi = a.take(2 * NQ * HEADS * TOPK, U32).rearrange("p (g q h k) -> p g q h k", g=2, q=NQ, h=HEADS)
        comb = a.take(HEADS * 64).rearrange("p (h a b) -> p h a b", h=HEADS, a=TOPK)
        best = a.take(NQ * PAIRS).rearrange("p (q h k) -> p q h k", q=NQ, h=HEADS)
        besti = a.take(NQ * PAIRS, U32)
        rank_of = [a.take(NQ * PAIRS, U32) for _ in range(2)]
        topf = a.take(2 * NQ * HEADS * TOPK).rearrange("p (g c r) -> p g c r", g=2, r=8)
        hit = [a.take(NQ * PAIRS * 8).rearrange("p (g k r) -> p g k r", k=8, r=8) for _ in range(2)]
        hit2 = a.take(NQ * PAIRS * 8).rearrange("p (g k r) -> p g k r", k=8, r=8)
        pick = [v.bitcast(F32) for v in rank_of]
        past = a.take(NQ * PAIRS)
        esub = a.take(NQ * PAIRS)
        esum = a.take(NQ * HEADS)
        table = a.take(3 * NQ * PAIRS).rearrange("p (n c) -> p n c", n=3)
        tab16 = a.take(4 * P, F16).rearrange("p (h n t) -> p n h t", h=2, n=4)

        c = Region(arena)
        a_sb = c.take(2 * TC * 2 * NI, F16).rearrange("p (n t u i) -> p n t u i", n=2, t=TC, u=2)
        x2_sb = c.take(2 * 2 * KC * TH, F16).rearrange("p (n s k t) -> p n s k t", n=2, s=2, k=KC)
        tab_sb = c.take(2 * 3 * 2 * TQ, F16).rearrange("p (n m t) -> p n m t", n=2, m=3)
        hit_i = c.take(TC * NI, F16).rearrange("p (t i) -> p t i", t=TC)
        b_sb = c.take(2 * TC * P, F16).rearrange("p (n t j) -> p n t j", n=2, t=TC)
        assert c.at <= X1_AT + NQ * D + 16 * P
        c.at = X1_AT + NQ * D + 16 * P
        p_sb = c.take(2 * NI * TH).rearrange("p (n i q t) -> p n i q t", n=2, i=NI, q=NQ)
        silu_z = c.take(2 * 2 * TH).rearrange("p (n t) -> p n t", n=2)
        g32 = c.take(2 * 2 * TH).rearrange("p (n t) -> p n t", n=2)
        g_s = c.take(2 * 2 * 2 * TH, F16).rearrange("p (n s i t) -> p n s i t", n=2, s=2, i=2)
        res = c.take(2 * 2 * D).rearrange("p (n u d) -> p n u d", n=2, u=2)
        fin = c.take(2 * 2 * D).rearrange("p (n u d) -> p n u d", n=2, u=2)
        assert c.at == SECOND

        def col(n, k=1):
            return scal[:, n:n + k]

        KF, WG, WU, WD_, DN, UP = range(6)
        mx, mxr, pw, rp, ws = (8 * n for n in range(5))
        SIM_OUT, GATE_IN, H_SCALE, MLP_OUT, Z_IN, PROB, EXP_OUT = range(40, 47)
        DEC, LA, NEG, POS, NAB, EXPN, LNN, LOGG, ALPHA = range(48, 57)

        def weight_parts(m):
            return (kf_s[:, m].rearrange("p k n -> p (k n)"), wgu_s[:, m, 0].rearrange("p k n -> p (k n)"),
                    wgu_s[:, m, 1].rearrange("p k n -> p (k n)"), wd_s[:, m].rearrange("p c d -> p (c d)"))

        def after(b, h, n):
            return b + (h + n) // 2, (h + n) % 2

        x_q = x.rearrange("b (q t) d -> b t q d", t=P)
        x1_q = x1_d.rearrange("b (q t) d -> b t q d", t=P)

        def at(v, b):
            return v[bass.ds(b, 1)]

        block = ctx.enter_context(nc.Block())

        @block.sync
        def _(sp):
            def load_x(b):
                sp.dma_start(xin, at(x_q, b).rearrange("o t q d -> (o t) q d")).then_inc(sem("x_in"), 16)

            load_x(0)
            for dst, src in ((col(DEC), decay), (col(LA), log_alpha)):
                sp.dma_start(dst, src).then_inc(sem("scal_in"), 16)
            for dst, src in ((ww_sb, wwrite.rearrange("(k p) d -> p k d", p=P)), (wr_sb, wreadT.rearrange("(k p) d -> p k d", p=P)),
                             (ident[:, :], ident_d)):
                sp.dma_start(dst, src).then_inc(sem("mat_in"), 16)
            sp.dma_start(wq_sb, wq.rearrange("(g n) d -> n g d", n=HALF)).then_inc(sem("wq_in"), 16)
            sp.dma_start(keys_sb, keys).then_inc(sem("wq_in"), 16)
            for dst, src in ((diffs, diffs_d), (causal, causal_d), (iota[:, :], iota_d), (rank[:, :], rank_d),
                             (umask[:, :], umask_d)):
                sp.dma_start(dst, src).then_inc(sem("const_in"), 16)
            sp.dma_start(raw_gu[:, 0:KC * INTER], wg).then_inc(sem("mlp_in"), 16)
            sp.dma_start(raw_gu[:, KC * INTER:2 * KC * INTER], wu).then_inc(sem("mlp_in"), 16)
            sp.dma_start(raw_wd, wd).then_inc(sem("mlp_in"), 16)

            def prefetch(b):
                sp.wait_ge(sem("xin_used"), b + 1)
                load_x(b + 1)

            def store_x2(b):
                for n in range(2):
                    sp.wait_ge(sem(f"att_free{n}"), 6 * b + ROWS2)
                sp.dma_start(x2_d[bass.ds(b, 1)].rearrange("o p s k t -> (o p) s k t"), x2s).then_inc(sem("x2_out"), 16)

            def store_rows(b):
                sp.wait_ge(sem("sim_free0"), 6 * b + 6)
                sp.wait_ge(sem("sim_free1"), 5 * b + 5)
                sp.dma_start(at(x1_q, b).rearrange("o t q d -> (o t) q d"), x1m).then_inc(sem("x1_out"), 16)

            def store_table(b):
                sp.wait_ge(sem("tab_ij"), b + 1)
                sp.wait_ge(sem("tab_lo"), b + 1)
                for h in range(2):
                    for v in range(2):
                        sp.dma_start(tab_d[bass.ds(b, 1), h, :, :, v * TQ:(v + 1) * TQ].rearrange("o p n t -> (o p) n t"),
                                     tab16[v * 64:(v + 1) * 64, :, h]).then_inc(sem("tab_out"), 16)

            prefetch(0)
            store_x2(0)

            def sequence(b, first=False):
                if not first:
                    store_table(b - 1)
                prefetch(b + 1)
                store_x2(b + 1)
                store_rows(b)

            for name in ("kf_lo", "gate_lo", "up_lo", "down_lo"):
                sp.wait_ge(sem(name), 1)
            sp.wait_ge(sem("decay_tab"), 1)
            sp.wait_ge(sem("wc"), 1)
            for n in range(4):
                sp.dma_start(raw_emb[:, n * LOOK:(n + 1) * LOOK], emb[:, n * LOOK:(n + 1) * LOOK]).then_inc(sem("emb_in"), 16)
            sequence(0, first=True)
            with sp.Fori(1, NB - 2) as b:
                sequence(b)
            def load_tile(b, h):
                src = x2_d[bass.ds(b, 1)].rearrange("o p s k (q t) -> (o p) (s k q) t", q=NQ)[:, :, h * TQ:(h + 1) * TQ]
                sp.dma_start(x2_sb[:, h].rearrange("p s k (q t) -> p (s k q) t", q=NQ), src).then_inc(sem(f"x2_in{h}"), 16)

            def load_tab(b, h):
                for u in range(2):
                    rows_u = tab_d[bass.ds(b, 1), h, u * PAIRS:(u + 1) * PAIRS].rearrange("o p n t -> (o p) n t")
                    for part in range(2):
                        to = (2 * u + part) * PAIRS
                        sp.dma_start(tab_sb[to:to + PAIRS, h, 0:2], rows_u[:, 0:2]).then_inc(sem(f"tab_in{h}"), 16)
                        sp.dma_start(tab_sb[to:to + PAIRS, h, 2:3], rows_u[:, 2 + part:3 + part]).then_inc(sem(f"tab_in{h}"), 16)

            def rows(v, b, h, q):
                return v[bass.ds(b, 1), q * P + h * TQ:q * P + (h + 1) * TQ].rearrange("o t d -> (o t) d")

            def load_res(b, h):
                for q in range(NQ):
                    sp.dma_start(res[(q % 2) * TQ:(q % 2 + 1) * TQ, h, q // 2], rows(x1_d, b, h, q)).then_inc(sem(f"res_in{h}"), 16)

            def store(b, h):
                sp.wait_ge(sem("fin"), 4 * b + 2 * h + 2)
                for q in range(NQ):
                    sp.dma_start(rows(out, b, h, q), fin[(q % 2) * TQ:(q % 2 + 1) * TQ, h, q // 2]).then_inc(sem(f"stored{h}"), 16)

            store_table(NB - 3)
            store_x2(NB - 1)
            sp.wait_ge(sem("t2_full"), 2 * NB)
            for n in range(2):
                sp.wait_ge(sem(f"att_free{n}"), 6 * (NB - 1) + READS)
            sp.wait_ge(sem("tab_out"), 64 * (NB - 2))
            for h in range(2):
                load_tab(0, h)
            store_rows(NB - 2)
            sp.wait_ge(sem("x2_out"), 16 * NB)
            for h in range(2):
                load_tile(0, h)
            store_table(NB - 2)
            store_rows(NB - 1)
            sp.wait_ge(sem("x1_out"), 16 * NB)
            sp.wait_ge(sem("down_full"), 2 * NB)
            sp.wait_ge(sem("emb_lo"), NPIECE)
            for h in range(2):
                load_res(0, h)

            def loads_after(b, table=False):
                sp.wait_ge(sem("a_built"), 8 * b + 4)
                sp.wait_ge(sem("b_built"), 8 * b + 4)
                load_tab(b + 1, 0)
                sp.wait_ge(sem("z"), 32 * b + 16)
                load_tile(b + 1, 0)
                sp.wait_ge(sem("a_built"), 8 * b + 8)
                sp.wait_ge(sem("b_built"), 8 * b + 8)
                load_tab(b + 1, 1)
                store(b, 0)
                load_res(b + 1, 0)
                if table:
                    store_table(NB - 1)
                    sp.wait_ge(sem("tab_out"), 64 * NB)
                sp.wait_ge(sem("z"), 32 * b + 32)
                load_tile(b + 1, 1)
                store(b, 1)
                load_res(b + 1, 1)

            loads_after(0, table=True)
            with sp.Fori(1, NB - 1) as b:
                loads_after(b)
            store(NB - 1, 0)
            store(NB - 1, 1)
            for h in range(2):
                sp.wait_ge(sem(f"stored{h}"), 16 * NQ * NB)

        @block.tensor
        def _(pe):
            pe.wait_ge(sem("mat_in"), 48)
            for ec in range(KC):
                for k in range(KC):
                    last = pe.matmul(bank[0][:, ec * D:(ec + 1) * D], ww_sb[:, k, ec * P:(ec + 1) * P], wr_sb[:, k, :],
                                     start=(k == 0), stop=(k == KC - 1))
            last.then_inc(sem("wc_full"), 1)
            pe.wait_ge(sem("wq_in"), 32)
            for dc in range(KC):
                for g in range(8):
                    last = pe.matmul(bank[4 + 2 * dc + g // 4][:, (g % 4) * NK:(g % 4 + 1) * NK],
                                     wq_sb[:, g, dc * P:(dc + 1) * P], keys_sb[:, g, :], start=True, stop=True)
            last.then_inc(sem("kf_full"), 1)

            def bank_free(n, b, k):
                pe.wait_ge(sem(f"att_free{n}"), 6 * b + k)

            def transpose_rows(src, b, k, ready, full):
                pe.wait_ge(sem(ready), b + 1)
                for kc in range(KC):
                    bank_free(kc, b, k)
                    for q in range(NQ):
                        last = pe.transpose(bank[kc][:, q * P:(q + 1) * P], src[:, q, kc * P:(kc + 1) * P], ident[:, :])
                    last.then_inc(sem(full), 1)

            def t1(b):
                transpose_rows(xhat, b, 0, "xhat", "t1_full")

            def values_scores(b):
                for n in range(2):
                    pe.wait_ge(sem(f"att_free{n}"), 6 * b + ROWS)
                pe.wait_ge(sem("wc"), 1)
                for n in range(2):
                    bank_free(n, b, 1)
                    for q in (2 * n, 2 * n + 1):
                        for k in range(KC):
                            last = pe.matmul(bank[n][:, (q % 2) * D:(q % 2 + 1) * D], xT[:, k, 1 + q * P:1 + (q + 1) * P],
                                             wc[:, k, :], start=(k == 0), stop=(k == KC - 1))
                    last.then_inc(sem("v_full"), 1)
                for s in range(NQ):
                    bank_free(s % 2, b, 2 + s // 2)
                    for k in range(KC):
                        last = pe.matmul(bank[s % 2][:, 0:T - P * s], xT[:, k, s * P:(s + 1) * P], xT[:, k, 1 + s * P:1 + T],
                                         start=(k == 0), stop=(k == KC - 1))
                    last.then_inc(sem("s_full"), 1)

            def reads(b):
                for n in range(2):
                    pe.wait_ge(sem(f"att_free{n}"), 6 * b + SCORES)
                for n in range(2):
                    bank_free(n, b, 4)
                    for q in (2 * n, 2 * n + 1):
                        for s in range(q + 1):
                            last = pe.matmul(bank[n][:, (q % 2) * D:(q % 2 + 1) * D], att[s][:, (q - s) * P:(q - s + 1) * P],
                                             v_sb[:, s, :], start=(s == 0), stop=(s == q))
                    last.then_inc(sem("r_full"), 1)

            def t2(b):
                transpose_rows(x2n, b, 5, "x2n", "t2_full")

            def similarities(b):
                for n in range(2):
                    pe.wait_ge(sem(f"att_free{n}"), 6 * b + ROWS2)
                for q in range(NQ):
                    for n in range(2):
                        pe.wait_ge(sem(f"sim_free{n}"), (6 - n) * b + q)
                        last = three(bank[2 + n][:, :], lambda s, k: x2s[:, s, k, q * P:(q + 1) * P],
                                     lambda s, k: kf_s[:, s, k, n * 512:(n + 1) * 512])
                        last.then_inc(sem("sim_full"), 1)

            def three(dst, stat, mov, ks=KC):
                n = 0
                for k in range(ks):
                    for s, m in HALVES:
                        last = pe.matmul(dst, stat(s, k), mov(m, k), start=(n == 0), stop=(n == 3 * ks - 1))
                        n += 1
                return last

            def mlp_up(b, c):
                pe.wait_ge(sem(f"mlp_free{c % 2}"), 4 * b + c // 2)
                for g in range(2):
                    last = three(bank[4 + 2 * (c % 2) + g][:, :], lambda s, k: wgu_s[:, s, g, k, c * P:(c + 1) * P],
                                 lambda s, k: x2s[:, s, k])
                last.then_inc(sem("gu_full"), 1)

            def mlp_down(b, n):
                pe.wait_ge(sem(f"sim_free{n}"), (6 - n) * b + 5 - n)
                for q in (2 * n, 2 * n + 1):
                    last = down_chunks(b, q, range(NIC))
                last.then_inc(sem("down_full"), 1)

            def mlp_down_both(b):
                for n in range(2):
                    pe.wait_ge(sem(f"sim_free{n}"), (6 - n) * b + 5 - n)
                    down_chunks(b, 2 * n, range(NIC - 1))
                for n in range(2):
                    down_chunks(b, 2 * n, (NIC - 1,))
                    down_chunks(b, 2 * n + 1, range(NIC)).then_inc(sem("down_full"), 1)

            def down_chunks(b, q, chunks):
                for k in chunks:
                    if q == 0:
                        pe.wait_ge(sem("h_lo"), NIC * b + k + 1)
                    for n, (s, m) in enumerate(HALVES):
                        last = pe.matmul(bank[2 + q // 2][:, (q % 2) * D:(q % 2 + 1) * D], h_s[:, s, k, q * P:(q + 1) * P],
                                         wd_s[:, m, k, :], start=(k == 0 and n == 0), stop=(k == NIC - 1 and n == 2))
                return last

            def table_t(b, n, bank_sem, uses):
                pe.wait_ge(sem("indices"), b + 1)
                pe.wait_ge(sem("probs"), b + 1)
                pe.wait_ge(sem(bank_sem), uses)
                for m in range(3):
                    last = pe.transpose(bank[n][:, m * P:(m + 1) * P], table[:, m, :], ident[:, :])
                last.then_inc(sem("tab_full"), 1)

            def z(b, h, s):
                pe.wait_ge(sem(f"z_free{s % 2}"), 16 * b + 8 * h + s // 2)
                if s == 0:
                    pe.wait_ge(sem(f"x2_in{h}"), 16 * b + 16)
                for i in range(2):
                    last = three(bank[2 + s % 2][:, i * TH:(i + 1) * TH], lambda m, k: down_w(m, k, 2 * s + i),
                                 lambda m, k: x2_sb[:, h, m, k, :])
                last.then_inc(sem("z"), 1)

            def scatter(b, h, s):
                c = s // 4
                n = s % 2
                if s % 4 == 0:
                    pe.wait_ge(sem("a_built"), 8 * b + 4 * h + c + 1)
                    pe.wait_ge(sem("b_built"), 8 * b + 4 * h + c + 1)
                pe.wait_ge(sem(f"p_free{s % 2}"), 16 * b + 8 * h + s // 2)
                for t in range(8):
                    last = pe.matmul(bank[n][:, t * 2 * NI:(t + 1) * 2 * NI], b_sb[:, c % 2, 8 * (s % 4) + t, :],
                                     a_sb[:, c % 2, 8 * (s % 4) + t].rearrange("p u i -> p (u i)"), start=True, stop=True)
                last.then_inc(sem("p_full"), 1)

            def up(b, h, s):
                pe.wait_ge(sem("g_lo"), 32 * b + 16 * h + s + 1)
                if s == 0:
                    pe.wait_ge(sem(f"sum_free{h}"), 2 * b)
                for i in range(2):
                    for u in range(2):
                        for m, w in HALVES:
                            last = pe.matmul(bank[4 + 2 * h + u][:, 0:D], g_s[:, s % 2, m, i, u * P:(u + 1) * P],
                                             up_w(w, 2 * s + i), start=(s == 0 and i == 0 and (m, w) == (0, 0)),
                                             stop=(s == NI // 2 - 1 and i == 1 and (m, w) == HALVES[-1]))
                last.then_inc(sem("up"), 1)

            pe.wait_ge(sem("wc"), 1)
            t1(0)
            values_scores(0)
            reads(0)
            t2(0)
            pe.wait_ge(sem("kf_lo"), 1)

            def sequence(b, first=False, last=False):
                similarities(b)
                if first:
                    pe.wait_ge(sem("gate_lo"), 1)
                    pe.wait_ge(sem("up_lo"), 1)
                mlp_up(b, 0)
                if not last:
                    t1(b + 1)
                mlp_up(b, 1)
                if not first:
                    table_t(b - 1, 2, "sim_free0", 6 * b + NQ)
                if not last:
                    values_scores(b + 1)
                mlp_up(b, 2)
                if not last:
                    reads(b + 1)
                for c in range(3, NIC):
                    mlp_up(b, c)
                if first:
                    pe.wait_ge(sem("down_lo"), 1)
                if not last:
                    t2(b + 1)
                    mlp_down_both(b)

            def tile(b, h, rest, table_at=None):
                for s in range(16):
                    n, m = divmod(s + 2, 16)
                    if n <= rest:
                        z(*after(b, h, n), m)
                    if n + 1 <= rest:
                        scatter(*after(b, h, n + 1), m)
                    up(b, h, s)
                    if table_at == s:
                        table_t(NB - 1, 4, "sum_free0", 2)
                if table_at is not None:
                    pe.wait_ge(sem("tab_ij"), NB)
                    pe.wait_ge(sem("tab_lo"), NB)

            sequence(0, first=True)
            with pe.Fori(1, NB - 1) as b:
                sequence(b)
            sequence(NB - 1, last=True)
            for n in range(2):
                pe.wait_ge(sem(f"att_free{n}"), 6 * NB)
            for s in range(8):
                scatter(0, 0, s)
            mlp_down(NB - 1, 0)
            for s in range(8, 12):
                scatter(0, 0, s)
            mlp_down(NB - 1, 1)
            for s in range(12, 16):
                scatter(0, 0, s)
            pe.wait_ge(sem("sim_free0"), 6 * NB)
            pe.wait_ge(sem("sim_free1"), 5 * NB)
            pe.wait_ge(sem("emb_lo"), NPIECE)
            z(0, 0, 0)
            z(0, 0, 1)
            scatter(0, 1, 0)
            scatter(0, 1, 1)
            for n in range(2):
                pe.wait_ge(sem(f"mlp_free{n}"), 4 * NB)
            tile(0, 0, 2)
            tile(0, 1, 2, table_at=TABLE_AT)
            with pe.Fori(1, NB - 1) as b:
                tile(b, 0, 2)
                tile(b, 1, 2)
            tile(NB - 1, 0, 1)
            tile(NB - 1, 1, 0)

        @block.scalar
        def _(act):
            def copy(dst, src, scale=1.0):
                return act.activation(dst, src, ACT.Copy, scale=scale)

            act.wait_ge(sem("scal_chain"), 3)
            act.activation(col(EXPN), col(NAB), ACT.Exp).then_inc(sem("act_scal"), 1)
            act.wait_ge(sem("act_scal"), 1)
            act.activation(col(LNN), col(EXPN), ACT.Ln, bias=1.0).then_inc(sem("act_scal"), 1)
            act.activation(col(ALPHA), col(LA), ACT.Exp).then_inc(sem("act_scal"), 1)
            act.wait_ge(sem("act_scal"), 3)
            act.wait_ge(sem("wc_full"), 1)
            copy(wc.rearrange("p k d -> p (k d)"), bank[0][:, :], col(ALPHA)).then_inc(sem("wc"), 1)
            act.wait_ge(sem("scal_chain"), 4)
            act.wait_ge(sem("const_in"), 80)
            act.activation(decay_tab, diffs, ACT.Exp, scale=col(LOGG)).then_inc(sem("act_scal"), 1)

            def normalise(dst, src, b, ready, done, groups=range(NQ)):
                act.wait_ge(sem(ready), b + 1)
                act.wait_ge(sem("r_full"), 2 * b + (2 if done == "x2n" else 0))
                act.sem_inc(sem("act_steps"), 1)
                for q in groups:
                    last = act.activation(dst[:, q], src[:, q], ACT.Identity, bias=r0[:, q:q + 1], scale=r2[:, q:q + 1])
                if q == NQ - 1:
                    last.then_inc(sem(done), 1)

            def xT_out(b):
                for k in range(KC):
                    act.wait_ge(sem("t1_full"), 2 * b + k + 1)
                    copy(xT[:, k, 1:1 + T], bank[k][:, :]).then_inc(sem(f"att_free{k}"), 1)

            def v_out(b):
                for n in range(2):
                    act.wait_ge(sem("v_full"), 2 * b + n + 1)
                    copy(v_sb[:, 2 * n:2 * n + 2].rearrange("p q d -> p (q d)"), bank[n][:, :]).then_inc(sem(f"att_free{n}"), 1)

            def x2_hi(b):
                act.wait_ge(sem("x2_out"), 16 * b)
                for k in range(KC):
                    act.wait_ge(sem("t2_full"), 2 * b + k + 1)
                    act.activation(x2s[:, 0, k], bank[k][:, :], ACT.Copy, scale=X_SCALE).then_inc(sem("x2_hi"), 1)

            def sim_out(b, q):
                for n in range(2):
                    act.wait_ge(sem("sim_full"), 8 * b + 2 * q + n + 1)
                    if n == 0 and q == 0:
                        act.wait_ge(sem("topped"), NQ * b)
                    copy(sim[:, q, 4 * n:4 * n + 4].rearrange("p g k -> p (g k)"), bank[2 + n][:, :],
                         col(SIM_OUT)).then_inc(sem(f"sim_free{n}"), 1)

            def silu_gate(b, c):
                act.wait_ge(sem("gu_full"), NIC * b + c + 1)
                act.wait_ge(sem(f"mlp_free{c % 2}"), 4 * b + c // 2)
                act.activation(gate[:, c % 2], bank[4 + 2 * (c % 2)][:, :], ACT.Silu, scale=col(GATE_IN)).then_inc(sem("gate"), 1)

            def h_hi(b, c):
                act.wait_ge(sem(f"mlp_free{c % 2}"), 4 * b + c // 2 + 1)
                act.wait_ge(sem("down_full"), 2 * b)
                copy(h_s[:, 0, c], h32[:, c % 2]).then_inc(sem("h_hi"), 1)

            def exp_scores(b):
                act.wait_ge(sem("esub"), b + 1)
                act.activation(esub, esub, ACT.Exp).then_inc(sem("exped"), 1)

            def tab_hi(b, n):
                act.wait_ge(sem("tab_full"), b + 1)
                act.wait_ge(sem("tab_out"), 64 * b)
                act.activation(tab16[:, 0:2], bank[n][:, 0:2 * P].rearrange("p (n h t) -> p n h t", n=2, h=2),
                               ACT.Copy).then_inc(sem("tab_ij"), 1)
                act.activation(tab16[:, 2], bank[n][:, 2 * P:3 * P].rearrange("p (h t) -> p h t", h=2),
                               ACT.Copy, scale=P_SCALE).then_inc(sem("tab_hi"), 1)

            normalise(xhat, xin, 0, "ln1", "xhat")
            act.wait_ge(sem("kf_full"), 1)
            for k in range(4):
                copy(kf32[:, k * 512:(k + 1) * 512], bank[4 + k][:, :]).then_inc(sem("kf32"), 1)
            xT_out(0)
            v_out(0)
            act.wait_ge(sem("w_scales"), 1)
            act.wait_ge(sem("kf32"), 4)
            kp, gp, up_, dp = weight_parts(0)
            copy(kp, kf32, col(ws + KF)).then_inc(sem("w_hi"), 1)
            normalise(x2n, x1, 0, "ln2", "x2n")
            x2_hi(0)

            def weights_high(n):
                hi, raw, scale = ((gp, raw_gu[:, 0:KC * INTER], WG), (up_, raw_gu[:, KC * INTER:], WU), (dp, raw_wd, WD_))[n]
                copy(hi, raw, col(ws + scale)).then_inc(sem("w_hi"), 1)

            def sequence(b, first=False, last=False):
                pieces = list(SPLITS.get(b, ())) if isinstance(b, int) else []
                if not first:
                    exp_scores(b - 1)
                for q in range(NQ):
                    if first and q < 3:
                        weights_high(q)
                    sim_out(b, q)
                if not last:
                    normalise(xhat, xin, b + 1, "ln1", "xhat")
                silu_gate(b, 0)
                if not last:
                    xT_out(b + 1)
                silu_gate(b, 1)
                h_hi(b, 0)
                if not first:
                    tab_hi(b - 1, 2)
                if not last:
                    v_out(b + 1)
                for _ in range(4):
                    if pieces:
                        emb_high(pieces.pop(0))
                silu_gate(b, 2)
                h_hi(b, 1)
                for c in range(3, NIC):
                    if pieces and c < 5:
                        emb_high(pieces.pop(0))
                    if c >= 6 and not last:
                        normalise(x2n, x1, b + 1, "ln2", "x2n", range(2 * (c - 6), 2 * (c - 5)))
                    silu_gate(b, c)
                    h_hi(b, c - 1)
                if last:
                    act.wait_ge(sem("gu_full"), NIC * NB)
                    act.wait_ge(sem("topped"), NQ * NB)
                    for s in range(4):
                        p_out(0, 0, s)
                h_hi(b, NIC - 1)
                if not last:
                    x2_hi(b + 1)
                for m in pieces:
                    emb_high(m)

            def emb_high(m):
                act.wait_ge(sem("e_scales"), 1)
                if m >= 2:
                    act.wait_ge(sem("emb_lo"), m - 1)
                copy(scaled[:, m % 2], raw_emb[:, m * PIECE:(m + 1) * PIECE], col(ws + (DN if m < NPIECE // 2 else UP))).then_inc(sem("scaled"), 1)
                act.wait_ge(sem("scaled"), m + 1)
                copy(parts[:, m, 0], scaled[:, m % 2]).then_inc(sem("emb_hi"), 1)

            def silu_of(b, h, s):
                act.wait_ge(sem("z"), 32 * b + 16 * h + s + 1)
                act.wait_ge(sem(f"s_free{s % 2}"), 16 * b + 8 * h + s // 2)
                act.activation(silu_z[:, s % 2], bank[2 + s % 2][:, :], ACT.Silu, scale=col(Z_IN)).then_inc(sem(f"z_free{s % 2}"), 1)

            def g_hi(b, h, s):
                act.wait_ge(sem(f"s_free{s % 2}"), 16 * b + 8 * h + s // 2 + 1)
                if not (isinstance(b, int) and b == h == s == 0):
                    act.wait_ge(sem("up"), 32 * b + 16 * h + s - 1)
                copy(g_s[:, s % 2, 0].rearrange("p i t -> p (i t)"), g32[:, s % 2]).then_inc(sem("g_hi"), 1)

            def p_out(b, h, s):
                act.wait_ge(sem("p_full"), 32 * b + 16 * h + s + 1)
                if s == 0 and not (isinstance(b, int) and b == h == 0):
                    act.wait_ge(sem("p_used"), 2 * b + h - 1)
                v, t = s // 8, 8 * (s % 8)
                act.activation(p_sb[:, h, :, 2 * v:2 * v + 2, t:t + 8], bank[s % 2][:, :].rearrange("p (t u i) -> p i u t", t=8, u=2),
                               ACT.Copy, scale=col(PROB)).then_inc(sem(f"p_free{s % 2}"), 1)

            def tile(b, h, rest, table_at=None):
                for s in range(16):
                    n, m = divmod(s + 1, 16)
                    if n <= rest:
                        g_hi(*after(b, h, n), m)
                    n, m = divmod(s + 2, 16)
                    if n <= rest:
                        silu_of(*after(b, h, n), m)
                    if n + 1 <= rest:
                        p_out(*after(b, h, n + 1), m)
                    if table_at == s + 1:
                        exp_scores(NB - 1)
                    if table_at == s:
                        tab_hi(NB - 1, 4)

            sequence(0, first=True)
            with act.Fori(1, MAX_SEQ[1]) as b:
                sequence(b)
            for b in range(MAX_SEQ[1], NB):
                sequence(b, last=(b == NB - 1))
            for s in range(4, 16):
                p_out(0, 0, s)
            act.wait_ge(sem("down_full"), 2 * NB)
            act.wait_ge(sem("sim_free0"), 6 * NB)
            act.wait_ge(sem("sim_free1"), 5 * NB)
            act.wait_ge(sem("emb_lo"), NPIECE)
            silu_of(0, 0, 0)
            p_out(0, 1, 0)
            silu_of(0, 0, 1)
            p_out(0, 1, 1)
            g_hi(0, 0, 0)
            tile(0, 0, 2)
            tile(0, 1, 2, table_at=TABLE_AT)
            with act.Fori(1, NB - 1) as b:
                tile(b, 0, 2)
                tile(b, 1, 2)
            tile(NB - 1, 0, 1)
            tile(NB - 1, 1, 0)

        @block.vector
        def _(dve):
            def chained(name, base=0):
                count = [0]

                def link(ins):
                    count[0] += 1
                    ins.then_inc(sem(name), 1)
                    dve.wait_ge(sem(name), base + count[0])
                return link

            def split(dst, src, scale, hi):
                return dve.scalar_tensor_tensor(dst, src, scale, hi, ALU.mult, ALU.subtract)

            def step_past():
                dve.sem_inc(sem("dve_steps"), 1)

            def rsqrt(link, step_between=lambda: None):
                link(dve.tensor_scalar(ve, mv[:, :, 1], EPS, None, ALU.add))
                link(dve.tensor_scalar(nh, ve, -0.5, None, ALU.mult))
                link(dve.tensor_scalar(r0.bitcast(I32), ve.bitcast(I32), 1, None, ALU.arith_shift_right))
                link(dve.tensor_scalar(r1.bitcast(I32), r0.bitcast(I32), -1.0, float(RSQRT_SEED), ALU.mult, ALU.add))
                step_between()
                r = r1
                for _ in range(3):
                    link(dve.tensor_tensor(r0, r, r, ALU.mult))
                    link(dve.tensor_tensor(r0, r0, nh, ALU.mult))
                    o = r2 if r is r1 else r1
                    link(dve.scalar_tensor_tensor(o, r0, 1.5, r, ALU.add, ALU.mult))
                    r = o
                return r

            def moments(src, link):
                for q in range(NQ):
                    last = dve.bn_stats(stats[:, q], src[:, q])
                link(last)
                step_past()
                for q in range(NQ):
                    last = dve.bn_aggr(mv[:, q], stats[:, q])
                link(last)

            def shift(r, done):
                dve.scalar_tensor_tensor(r0, mv[:, :, 0], -1.0, r, ALU.mult, ALU.mult).then_inc(sem(done), 1)

            LN_LINKS = 2 + 4 + 9

            def ln1(b):
                link = chained("ln1_chain", LN_LINKS * b)
                dve.wait_ge(sem("x_in"), 16 * b + 16)
                dve.wait_ge(sem("x2n"), b)
                moments(xin, link)
                shift(rsqrt(link), "ln1")

            def masks(b):
                dve.wait_ge(sem("r_full"), 2 * b)
                dve.wait_ge(sem("xsum"), b + 1)
                dve.wait_ge(sem("t1_full"), 2 * b + 2)
                for s in range(NQ):
                    dve.wait_ge(sem("s_full"), NQ * b + s + 1)
                    dve.tensor_tensor(att[s], bank[s % 2][:, 0:T - P * s], decay_tab[:, 0:T - P * s], ALU.mult).then_inc(sem(f"att_free{s % 2}"), 1)

            def add_reads(b):
                dve.wait_ge(sem("xsum"), b + 1)
                dve.wait_ge(sem("x2n"), b)
                dve.wait_ge(sem("x1_kept"), b)
                for n in range(2):
                    dve.wait_ge(sem("r_full"), 2 * b + n + 1)
                    dve.tensor_tensor(x1[:, 2 * n:2 * n + 2].rearrange("p q d -> p (q d)"), bank[n][:, :],
                                      xin[:, 2 * n:2 * n + 2].rearrange("p q d -> p (q d)"), ALU.add).then_inc(sem(f"att_free{n}"), 1)
                for n in range(2):
                    dve.wait_ge(sem(f"att_free{n}"), 6 * b + READS)
                dve.sem_inc(sem("xin_used"), 1)

            def ln2(b, steps_between=(lambda: None, lambda: None)):
                link = chained("ln2_chain", LN_LINKS * b)
                dve.wait_ge(sem("xhat"), b + 1)
                moments(x1, link)
                steps_between[0]()
                shift(rsqrt(link, steps_between[1]), "ln2")

            def x2_lo(b):
                for k in range(KC):
                    dve.wait_ge(sem("x2_hi"), 2 * b + k + 1)
                    split(x2s[:, 1, k], bank[k][:, :], X_SCALE, x2s[:, 0, k]).then_inc(sem(f"att_free{k}"), 1)

            def top8_halves(b, q):
                if q == 0:
                    dve.wait_ge(sem("hit"), 3 * b)
                    dve.wait_ge(sem("esub"), b)
                for n in range(2):
                    dve.wait_ge(sem(f"sim_free{n}"), (6 - n) * b + q + 1)
                step_past()
                for g in range(8):
                    last = dve.max(top[:, g // 4, q, g % 4], sim[:, q, g])
                last.then_inc(sem("top_chain"), 1)
                dve.wait_ge(sem("top_chain"), 4 * (NQ * b + q) + 1)
                dve.tensor_tensor(comb, top[:, 0, q, :, :].unsqueeze(3).to_broadcast([P, HEADS, 8, 8]),
                                  top[:, 1, q, :, :].unsqueeze(2).to_broadcast([P, HEADS, 8, 8]), ALU.add).then_inc(sem("top_chain"), 1)

            def top8_pairs(b, q):
                for n in range(2):
                    dve.wait_ge(sem(f"sim_free{n}"), (6 - n) * b + q + 1)
                step_past()
                for g in range(8):
                    last = dve.max_index(topi[:, g // 4, q, g % 4], top[:, g // 4, q, g % 4], sim[:, q, g])
                last.then_inc(sem("top_chain"), 1)
                dve.wait_ge(sem("top_chain"), 4 * (NQ * b + q) + 2)
                step_past()
                for h in range(HEADS):
                    last = dve.max(best[:, q, h], comb[:, h].rearrange("p a b -> p (a b)"))
                last.then_inc(sem("top_chain"), 1)
                dve.wait_ge(sem("top_chain"), 4 * (NQ * b + q) + 4)
                step_past()
                for h in range(HEADS):
                    last = dve.max_index(besti[:, (q * HEADS + h) * 8:(q * HEADS + h) * 8 + 8], best[:, q, h],
                                         comb[:, h].rearrange("p a b -> p (a b)"))
                last.then_inc(sem("topped"), 1)

            def top8(b, q):
                top8_halves(b, q)
                top8_pairs(b, q)

            def ranks(b):
                dve.wait_ge(sem("topped"), NQ * b + NQ)
                dve.wait_ge(sem("probs"), b)
                dve.wait_ge(sem("indices"), b)
                dve.tensor_scalar(rank_of[0], besti, 3, None, ALU.logical_shift_right)
                dve.tensor_scalar(rank_of[1], besti, 7, None, ALU.bitwise_and).then_inc(sem("ranks"), 1)
                dve.wait_ge(sem("ranks"), b + 1)
                for g in range(2):
                    dve.tensor_tensor(hit[g], rank_of[g].rearrange("p (g k) -> p g k", k=8).unsqueeze(3).to_broadcast([P, NQ * HEADS, 8, 8]),
                                      rank[:, :].unsqueeze(1).unsqueeze(1).to_broadcast([P, NQ * HEADS, 8, 8]),
                                      ALU.is_equal).then_inc(sem("hit"), 1)
                dve.tensor_copy(topf, topi.rearrange("p g q h r -> p g (q h) r")).then_inc(sem("hit"), 1)
                bq = best.rearrange("p q h k -> p (q h) k")
                dve.tensor_tensor(esub.rearrange("p (g k) -> p g k", k=8), bq, bq[:, :, 0:1].to_broadcast([P, NQ * HEADS, 8]),
                                  ALU.subtract).then_inc(sem("esub"), 1)

            def indices(b):
                dve.wait_ge(sem("picks"), b + 1)
                dve.wait_ge(sem("tab_full"), b)
                dve.wait_ge(sem("indices"), b)
                dve.tensor_scalar(past, pick[0], float(NI), float(P - 1), ALU.is_ge, ALU.mult).then_inc(sem("past"), 1)
                dve.tensor_scalar(table[:, 0], pick[0], float(NI - 1), None, ALU.min)
                dve.wait_ge(sem("past"), b + 1)
                dve.tensor_tensor(table[:, 1], pick[1], past, ALU.max).then_inc(sem("indices"), 1)

            def softmax(b):
                link = chained("softmax_chain", 2 * b)
                dve.wait_ge(sem("exped"), b + 1)
                dve.wait_ge(sem("tab_full"), b)
                e3 = esub.rearrange("p (g k) -> p g k", k=8)
                link(dve.tensor_reduce(esum, e3, AX_X, ALU.add))
                link(dve.reciprocal(esum, esum))
                dve.tensor_tensor(table[:, 2, :].rearrange("p (g k) -> p g k", k=8), e3,
                                  esum.unsqueeze(2).to_broadcast([P, NQ * HEADS, 8]), ALU.mult).then_inc(sem("probs"), 1)

            def hidden(b, c):
                dve.wait_ge(sem("gate"), NIC * b + c + 1)
                dve.wait_ge(sem("h_lo"), NIC * b + max(c - 1, 0))
                dve.scalar_tensor_tensor(h32[:, c % 2], bank[5 + 2 * (c % 2)][:, :], col(H_SCALE), gate[:, c % 2],
                                         ALU.mult, ALU.mult).then_inc(sem(f"mlp_free{c % 2}"), 1)

            def add_mlp(b, half):
                dve.wait_ge(sem("x1_out"), 16 * b)
                dve.wait_ge(sem("x1_kept"), b + 1)
                for q in (2 * half, 2 * half + 1):
                    dve.wait_ge(sem("down_full"), 2 * b + q // 2 + 1)
                    last = dve.scalar_tensor_tensor(x1m[:, q], bank[2 + q // 2][:, (q % 2) * D:(q % 2 + 1) * D], col(MLP_OUT),
                                                    x1k[:, q], ALU.mult, ALU.add)
                last.then_inc(sem(f"sim_free{half}"), 1)

            def tab_lo(b, n):
                dve.wait_ge(sem("tab_hi"), b + 1)
                dve.wait_ge(sem("tab_ij"), b + 1)
                split(tab16[:, 3], bank[n][:, 2 * P:3 * P].rearrange("p (h t) -> p h t", h=2), P_SCALE,
                      tab16[:, 2]).then_inc(sem("tab_lo"), 1)
                dve.wait_ge(sem("tab_lo"), b + 1)
                if n == 2:
                    dve.sem_inc(sem("sim_free0"), 1)

            dve.wait_ge(sem("scal_in"), 32)
            dve.tensor_scalar(col(NEG), col(DEC), -1.0, None, ALU.mult).then_inc(sem("scal_chain"), 1)
            dve.wait_ge(sem("scal_chain"), 1)
            dve.tensor_scalar(col(POS), col(NEG), 0.0, None, ALU.max).then_inc(sem("scal_chain"), 1)
            dve.tensor_tensor(col(NAB), col(NEG), col(DEC), ALU.min).then_inc(sem("scal_chain"), 1)
            dve.memset(xT[:, :, 0:1], 0.0).then_inc(sem("zero_col"), 1)
            ln1(0)
            dve.wait_ge(sem("act_scal"), 2)
            dve.wait_ge(sem("scal_chain"), 3)
            dve.scalar_tensor_tensor(col(LOGG), col(POS), -1.0, col(LNN), ALU.mult, ALU.subtract).then_inc(sem("scal_chain"), 1)
            dve.wait_ge(sem("act_scal"), 4)
            dve.tensor_tensor(decay_tab, decay_tab, causal, ALU.mult).then_inc(sem("decay_tab"), 1)
            dve.wait_ge(sem("decay_tab"), 1)
            dve.wait_ge(sem("zero_col"), 1)

            def largest(n, v):
                dve.tensor_reduce(col(mx + n), v, AX_X, ALU.max, apply_absolute_value=True).then_inc(sem("w_max"), 1)

            dve.wait_ge(sem("kf32"), 4)
            largest(KF, kf32)
            dve.wait_ge(sem("mlp_in"), 48)
            largest(WG, raw_gu[:, 0:KC * INTER])
            largest(WU, raw_gu[:, KC * INTER:])

            def scales(first, n, link):
                link(dve.tensor_scalar(col(mxr + first, n), col(mxr + first, n), 1e-30, None, ALU.max))
                link(dve.tensor_scalar(col(pw + first, n).bitcast(I32), col(mxr + first, n).bitcast(I32), EXPONENT, None, ALU.bitwise_and))
                link(dve.reciprocal(col(rp + first, n), col(pw + first, n)))
                link(dve.tensor_scalar(col(ws + first, n), col(rp + first, n), W_SCALE, None, ALU.mult))

            masks(0)
            largest(WD_, raw_wd)
            link = chained("scale_chain")
            dve.wait_ge(sem("w_maxed"), 1)
            scales(0, 4, link)
            link(dve.tensor_scalar(col(SIM_OUT), col(pw + KF), 1.0 / (X_SCALE * W_SCALE), None, ALU.mult))
            link(dve.tensor_scalar(col(GATE_IN), col(pw + WG), 1.0 / (X_SCALE * W_SCALE), None, ALU.mult))
            link(dve.tensor_scalar(col(H_SCALE), col(rp + WG), 1.0 / (8 * X_SCALE * W_SCALE), None, ALU.mult))
            link(dve.tensor_tensor(col(MLP_OUT), col(pw + WG), col(pw + WU), ALU.mult))
            link(dve.scalar_tensor_tensor(col(MLP_OUT), col(MLP_OUT), 8 / W_SCALE, col(pw + WD_), ALU.mult, ALU.mult))
            dve.sem_inc(sem("w_scales"), 1)
            add_reads(0)
            ln2(0)
            (kh, gh, uh, dh), (kl, gl, ul, dl) = weight_parts(0), weight_parts(1)
            dve.wait_ge(sem("w_hi"), 1)
            split(kl, kf32, col(ws + KF), kh).then_inc(sem("kf_lo"), 1)
            x2_lo(0)
            dve.wait_ge(sem("w_hi"), 2)
            split(gl, raw_gu[:, 0:KC * INTER], col(ws + WG), gh).then_inc(sem("gate_lo"), 1)
            dve.wait_ge(sem("w_hi"), 3)
            split(ul, raw_gu[:, KC * INTER:], col(ws + WU), uh).then_inc(sem("up_lo"), 1)
            dve.memset(col(mx + DN, 2), 0.0).then_inc(sem("mx_chain"), 1)

            def look(b, half):
                n = 2 * b - 1 + half
                dve.wait_ge(sem("emb_in"), 64)
                dve.wait_ge(sem("mx_chain"), n)
                step_past()
                dve.tensor_reduce(col(58), raw_emb[:, bass.ds((2 * (b - MAX_SEQ[0]) + half) * (LOOK // 2), LOOK // 2)], AX_X, ALU.max,
                                  apply_absolute_value=True).then_inc(sem("looked"), 1)
                dve.wait_ge(sem("looked"), n)
                dve.tensor_tensor(col(mx + DN), col(mx + DN), col(58), ALU.max).then_inc(sem("mx_chain"), 1)

            def emb_scales():
                link = chained("scale2_chain")
                dve.wait_ge(sem("e_maxed"), 1)
                scales(DN, 2, link)
                link(dve.tensor_scalar(col(Z_IN), col(pw + DN), 1.0 / (X_SCALE * W_SCALE), None, ALU.mult))
                link(dve.tensor_scalar(col(PROB), col(rp + DN), 16 / P_SCALE, None, ALU.mult))
                link(dve.tensor_scalar(col(EXP_OUT), col(pw + DN), 1.0 / 16, None, ALU.mult))
                link(dve.scalar_tensor_tensor(col(EXP_OUT), col(EXP_OUT), 1.0 / W_SCALE, col(pw + UP), ALU.mult, ALU.mult))
                dve.sem_inc(sem("e_scales"), 1)

            def sequence(b, first=False):
                if not first:
                    softmax(b - 1)
                ln1(b + 1)
                top8(b, 0)
                if isinstance(b, int) and b == MAX_SEQ[1]:
                    emb_scales()
                if not first:
                    indices(b - 1)
                top8_halves(b, 1)
                hidden(b, 0)
                if not isinstance(b, int):
                    look(b, 0)
                hidden(b, 1)
                if first:
                    dve.wait_ge(sem("sim_free0"), NQ)
                    dve.sem_inc(sem("sim_free0"), 1)
                    dve.wait_ge(sem("w_hi"), 4)
                    split(dl, raw_wd, col(ws + WD_), dh).then_inc(sem("down_lo"), 1)
                else:
                    tab_lo(b - 1, 2)
                top8_pairs(b, 1)
                masks(b + 1)
                top8(b, 2)
                hidden(b, 2)
                add_reads(b + 1)
                ln2(b + 1, (lambda: hidden(b, 3), lambda: hidden(b, 4)))
                hidden(b, 5)
                if not isinstance(b, int):
                    look(b, 1)
                hidden(b, 6)
                top8_halves(b, 3)
                hidden(b, 7)
                top8_pairs(b, 3)
                x2_lo(b + 1)
                ranks(b)
                add_mlp(b, 0)
                add_mlp(b, 1)

            def last_sequence(b):
                softmax(b - 1)
                for n in range(3):
                    build_a(0, 0, 0, n)
                top8(b, 0)
                indices(b - 1)
                top8_halves(b, 1)
                hidden(b, 0)
                top8_pairs(b, 1)
                hidden(b, 1)
                tab_lo(b - 1, 2)
                for q in (2, 3):
                    top8_halves(b, q)
                    hidden(b, 2 * q - 2)
                    top8_pairs(b, q)
                    hidden(b, 2 * q - 1)
                build_a(0, 0, 0, 3)
                hidden(b, 6)
                build_a(0, 0, 1, 0)
                build_a(0, 0, 1, 1)
                hidden(b, 7)
                for n in range(6, 15):
                    build_a(0, 0, n // 4, n % 4)
                add_mlp(b, 0)
                build_a(0, 0, 3, 3)
                add_mlp(b, 1)

            def product(b, h, s):
                dve.wait_ge(sem(f"z_free{s % 2}"), 16 * b + 8 * h + s // 2 + 1)
                if not (isinstance(b, int) and b == h == s == 0):
                    dve.wait_ge(sem("g_lo"), 32 * b + 16 * h + s - 1)
                if s == 0:
                    for n in range(2):
                        dve.wait_ge(sem(f"p_free{n}"), 16 * b + 8 * h + 8)
                dve.tensor_tensor(g32[:, s % 2].rearrange("p (i q t) -> p i q t", i=2, q=NQ),
                                  silu_z[:, s % 2].rearrange("p (i q t) -> p i q t", i=2, q=NQ),
                                  p_sb[:, h, 2 * s:2 * s + 2], ALU.mult).then_inc(sem(f"s_free{s % 2}"), 1)
                if s == 15:
                    dve.wait_ge(sem("s_free1"), 16 * b + 8 * h + 8)
                    dve.wait_ge(sem("s_free0"), 16 * b + 8 * h + 8)
                    dve.sem_inc(sem("p_used"), 1)

            def g_lo(b, h, s):
                dve.wait_ge(sem("g_hi"), 32 * b + 16 * h + s + 1)
                dve.tensor_tensor(g_s[:, s % 2, 1].rearrange("p i t -> p (i t)"), g32[:, s % 2],
                                  g_s[:, s % 2, 0].rearrange("p i t -> p (i t)"), ALU.subtract).then_inc(sem("g_lo"), 1)

            def build_a(b, h, c, step):
                tab = tab_sb[:, h]
                t0 = TC * c
                n = 8 * b + 4 * h + c
                if isinstance(b, int) and b == h == c == step == 0:
                    dve.wait_ge(sem("t2_full"), 2 * NB)
                if step == 0:
                    dve.wait_ge(sem(f"tab_in{h}"), 128 * b + 128)
                    dve.wait_ge(sem("a_built"), n)
                    dve.tensor_tensor(hit_i, iota[:, 0:NI].unsqueeze(1).to_broadcast([P, TC, NI]),
                                      tab[:, 0, t0:t0 + TC].unsqueeze(2).to_broadcast([P, TC, NI]), ALU.is_equal).then_inc(sem("hit_i"), 1)
                elif step == 1:
                    dve.wait_ge(sem("hit_i"), n + 1)
                    dve.tensor_tensor(hit_i, hit_i, tab[:, 2, t0:t0 + TC].unsqueeze(2).to_broadcast([P, TC, NI]),
                                      ALU.mult).then_inc(sem("hit_p"), 1)
                elif step == 2:
                    dve.wait_ge(sem("hit_p"), n + 1)
                    if not (isinstance(b, int) and b == 0 and h == 0 and c < 2):
                        dve.wait_ge(sem("p_full"), 4 * (n - 1))
                    for u in range(2):
                        last = dve.tensor_scalar(a_sb[:, c % 2, :, u, :], hit_i, umask[:, u:u + 1], None, ALU.mult)
                    last.then_inc(sem("a_built"), 1)
                else:
                    dve.wait_ge(sem("b_differ"), n + 1)
                    dve.tensor_scalar(b_sb[:, c % 2], b_sb[:, c % 2], 0.0, None, ALU.is_equal).then_inc(sem("b_built"), 1)

            def finish(b, h):
                dve.wait_ge(sem("up"), 32 * b + 16 * h + 16)
                dve.wait_ge(sem(f"res_in{h}"), 16 * NQ * b + 16 * NQ)
                dve.wait_ge(sem(f"stored{h}"), 16 * NQ * b)
                for u in range(2):
                    dve.scalar_tensor_tensor(fin[:, h, u], bank[4 + 2 * h + u][:, 0:D], col(EXP_OUT), res[:, h, u],
                                             ALU.mult, ALU.add).then_inc(sem("fin"), 1)
                dve.wait_ge(sem("fin"), 4 * b + 2 * h + 2)
                dve.sem_inc(sem(f"sum_free{h}"), 2)

            def tile(b, h, rest, table_at=None, ranks_at=None):
                for s in range(16):
                    n, m = divmod(s + 22, 16)
                    if n <= rest:
                        build_a(*after(b, h, n), m // 4, m % 4)
                    n, m = divmod(s + 1, 16)
                    if n <= rest:
                        g_lo(*after(b, h, n), m)
                    n, m = divmod(s + 2, 16)
                    if n <= rest:
                        product(*after(b, h, n), m)
                    if s == 1:
                        prev(b, h)
                    if ranks_at == s:
                        ranks(NB - 1)
                    if table_at == s + 1:
                        softmax(NB - 1)
                        indices(NB - 1)
                    if table_at == s:
                        tab_lo(NB - 1, 4)

            def prev(b, h):
                if h == 1:
                    finish(b, 0)
                elif not isinstance(b, int) or b > 0:
                    finish(b - 1, 1)

            sequence(0, first=True)
            with dve.Fori(1, MAX_SEQ[1]) as b:
                sequence(b)
            dve.wait_ge(sem("mx_chain"), 2 * MAX_SEQ[1] - 1)
            dve.sem_inc(sem("e_max"), 1)
            for b in range(MAX_SEQ[1], NB - 1):
                sequence(b)
            last_sequence(NB - 1)
            for m in range(16, 20):
                build_a(0, m // 16, m % 16 // 4, m % 4)
            dve.wait_ge(sem("h_lo"), NIC * NB)
            dve.wait_ge(sem("down_full"), 2 * NB)
            dve.wait_ge(sem("emb_lo"), NPIECE)
            product(0, 0, 0)
            product(0, 0, 1)
            build_a(0, 1, 1, 0)
            g_lo(0, 0, 0)
            build_a(0, 1, 1, 1)
            tile(0, 0, 2, ranks_at=3)
            tile(0, 1, 2, table_at=TABLE_AT)
            with dve.Fori(1, NB - 1) as b:
                tile(b, 0, 2)
                tile(b, 1, 2)
            tile(NB - 1, 0, 1)
            tile(NB - 1, 1, 0)
            finish(NB - 1, 1)

        @block.gpsimd
        def _(pool):
            MAX = bass.bass_isa.ReduceOp.max
            SEL = 8

            def residual(b):
                pool.wait_ge(sem("xhat"), b + 1)
                pool.tensor_tensor(xin, xin, xhat, ALU.add).then_inc(sem("xsum"), 1)

            def keep(b):
                for n in range(2):
                    pool.wait_ge(sem(f"att_free{n}"), 6 * b + READS)
                pool.wait_ge(sem("sim_free0"), 6 * b)
                pool.wait_ge(sem("sim_free1"), 5 * b)
                pool.sem_inc(sem("pool_steps"), 1)
                pool.tensor_copy(x1k, x1).then_inc(sem("x1_kept"), 1)

            def h_lo(b, c):
                pool.wait_ge(sem("h_hi"), NIC * b + c + 1)
                pool.tensor_tensor(h_s[:, 1, c], h32[:, c % 2], h_s[:, 0, c], ALU.subtract).then_inc(sem("h_lo"), 1)

            def select(b, g, steps=(0, 1)):
                if g == 0 and 0 in steps:
                    pool.wait_ge(sem("hit"), 3 * b + 3)
                    pool.wait_ge(sem("indices"), b)
                n = [4 * g + steps[0]]

                def link(ins):
                    n[0] += 1
                    ins.then_inc(sem("sel_chain"), 1)
                    pool.wait_ge(sem("sel_chain"), SEL * b + n[0])

                if 0 in steps:
                    link(pool.tensor_tensor(hit2, hit[g], topf[:, g].unsqueeze(2).to_broadcast([P, NQ * HEADS, 8, 8]), ALU.mult))
                if 1 not in steps:
                    return
                link(pool.tensor_tensor(hit[g][:, :, :, 0:4], hit2[:, :, :, 0:4], hit2[:, :, :, 4:8], ALU.add))
                link(pool.tensor_tensor(hit2[:, :, :, 0:2], hit[g][:, :, :, 0:2], hit[g][:, :, :, 2:4], ALU.add))
                link(pool.tensor_tensor(pick[g].rearrange("p (g k) -> p g k", k=8), hit2[:, :, :, 0], hit2[:, :, :, 1], ALU.add))
                if g == 1:
                    pool.sem_inc(sem("picks"), 1)

            def emb_low(m):
                pool.wait_ge(sem("emb_hi"), m + 1)
                pool.tensor_tensor(parts[:, m, 1], scaled[:, m % 2], parts[:, m, 0], ALU.subtract).then_inc(sem("emb_lo"), 1)

            def sequence(b, last=False):
                pieces = list(SPLITS.get(b, ())) if isinstance(b, int) else []

                keep(b)
                if not last:
                    residual(b + 1)
                else:
                    differ_b(0, 0, 0)
                for c in range(NIC):
                    h_lo(b, c)
                    if last and c in (1, 3):
                        differ_b(0, 0, 1, (c // 2,))
                    for _ in range({0: 4, 2: 1, 3: 1, NIC - 1: 2}.get(c, 0)):
                        if pieces:
                            emb_low(pieces.pop(0))
                if not last:
                    select(b, 0)
                    select(b, 1)

            def differ_b(b, h, c, halves=(0, 1)):
                if c == 0:
                    pool.wait_ge(sem(f"tab_in{h}"), 128 * b + 128)
                if isinstance(b, int) and b == 0 and h == 0 and c < 2:
                    pool.wait_ge(sem("t2_full"), 2 * NB)
                    pool.wait_ge(sem("x1_kept"), NB)
                    pool.wait_ge(sem("sim_full"), 8 * NB)
                else:
                    pool.wait_ge(sem("p_full"), 4 * (8 * b + 4 * h + c - 1))
                n = TC // 2 * len(halves)
                t0 = TC // 2 * halves[0]
                done = pool.tensor_tensor(b_sb[:, c % 2, t0:t0 + n], iota[:, :].unsqueeze(1).to_broadcast([P, n, P]),
                                          tab_sb[:, h, 1, TC * c + t0:TC * c + t0 + n].unsqueeze(2).to_broadcast([P, n, P]),
                                          ALU.subtract)
                if 1 in halves:
                    done.then_inc(sem("b_differ"), 1)

            residual(0)
            pool.wait_ge(sem("w_max"), 4)
            pool.partition_all_reduce(col(mxr, 4), col(mx, 4), P, MAX).then_inc(sem("w_maxed"), 1)
            sequence(0)
            with pool.Fori(1, MAX_SEQ[1]) as b:
                sequence(b)
            pool.wait_ge(sem("e_max"), 1)
            pool.partition_all_reduce(col(mxr + DN, 2), col(mx + DN, 2), P, MAX).then_inc(sem("e_red"), 1)
            pool.wait_ge(sem("e_red"), 1)
            pool.tensor_copy(col(mxr + UP), col(mxr + DN)).then_inc(sem("e_maxed"), 1)
            for b in range(MAX_SEQ[1], NB):
                sequence(b, last=(b == NB - 1))
            for n in range(2, 6):
                differ_b(0, n // 4, n % 4)
            for n, (half, step) in enumerate(((0, 0), (0, 1), (1, 0), (1, 1))):
                differ_b((6 + n) // 8, (6 + n) % 8 // 4, (6 + n) % 4)
                select(NB - 1, half, (step,))
            for n in range(2, 8):
                differ_b(1, n // 4, n % 4)
            with pool.Fori(2, NB) as b:
                for n in range(8):
                    differ_b(b, n // 4, n % 4)


def kernel(L0_attn_out, L0_attn_W_write, L0_attn_W_read, L0_attn_decay, L0_attn_log_alpha, L0_ffn_Wq,
           L0_ffn_keys, L0_ffn_down_embed, L0_ffn_up_embed, L0_ffn_Wg, L0_ffn_Wu, L0_ffn_Wd):
    import numpy as np
    import concourse.bacc as bacc
    from concourse import mybir as mb
    from concourse.bass_utils import run_bass_kernel_spmd

    def rows128(w):
        w = np.asarray(w)
        return np.ascontiguousarray(w.reshape(-1, 128, w.shape[1]).transpose(1, 0, 2).reshape(128, -1))

    def one(v):
        return np.ascontiguousarray(np.broadcast_to(np.asarray(v).reshape(1, 1), (128, 1)))

    lane, tok = np.arange(128)[:, None], np.arange(T)[None, :]
    ins = [
        ("x", np.ascontiguousarray(L0_attn_out)),
        ("wwrite", np.ascontiguousarray(L0_attn_W_write)),
        ("wreadT", np.ascontiguousarray(np.asarray(L0_attn_W_read).T)),
        ("decay", one(L0_attn_decay)),
        ("log_alpha", one(L0_attn_log_alpha)),
        ("wq", np.ascontiguousarray(L0_ffn_Wq)),
        ("keys", np.ascontiguousarray(np.asarray(L0_ffn_keys).transpose(3, 2, 0, 1).reshape(HALF, 8, NK))),
        ("emb", np.ascontiguousarray(np.concatenate([rows128(np.asarray(L0_ffn_down_embed).T), rows128(L0_ffn_up_embed)], axis=1))),
        ("wg", rows128(np.asarray(L0_ffn_Wg).T)),
        ("wu", rows128(np.asarray(L0_ffn_Wu).T)),
        ("wd", rows128(np.asarray(L0_ffn_Wd).T)),
        ("ident", np.eye(128, dtype=np.float32)),
        ("diffs", np.maximum(tok - 1 - lane, 0).astype(np.float32)),
        ("causal", (tok > lane).astype(np.float32)),
        ("iota", np.ascontiguousarray(np.broadcast_to(np.arange(128), (128, 128))).astype(np.float16)),
        ("rank", np.ascontiguousarray(np.broadcast_to(np.arange(8), (128, 8))).astype(np.float32)),
        ("umask", (lane // (2 * PAIRS) == np.arange(2)[None, :]).astype(np.float32)),
    ]
    nc = bacc.Bacc("TRN2", target_bir_lowering=False, num_devices=1)
    arrays, args = {}, []
    for name, arr in ins:
        arrays[f"in_{name}"] = arr
        args.append(nc.dram_tensor(f"in_{name}", arr.shape, mb.dt.from_np(arr.dtype), kind="ExternalInput").ap())
    args.append(nc.dram_tensor("x2_parts", [NB, P, 2, KC, T], F16, kind="Internal").ap())
    args.append(nc.dram_tensor("pick_tables", [NB, 2, 2 * PAIRS, 4, 2 * TQ], F16, kind="Internal").ap())
    args.append(nc.dram_tensor("x1_rows", [NB, T, D], F32, kind="Internal").ap())
    args.append(nc.dram_tensor("out_0", [NB, T, D], F32, kind="ExternalOutput").ap())
    dense_kernel(nc, *args)
    r = run_bass_kernel_spmd(nc, [arrays], core_ids=[0])
    return r.results[0]["out_0"]
```
